# Optimizing a Trainium2 kernel written in Bass

```python
import numpy as np
import jax
import jax.numpy as jnp

def _softmax(x, axis=-1):
    return jax.nn.softmax(x, axis=axis)

def _gelu(x):
    return jax.nn.gelu(x, approximate=True)

def _silu(x):
    return jax.nn.silu(x)

def _sigmoid(x):
    return jax.nn.sigmoid(x)

def _layernorm(x, axis=-1, eps=1e-05):
    m = jnp.mean(x, axis=axis, keepdims=True)
    v = jnp.var(x, axis=axis, keepdims=True)
    return (x - m) / jnp.sqrt(v + eps)

def _scatter_add(tgt, idx, src, axis=0):
    return tgt.at[idx].add(src)

def _segment_sum(src, seg, n):
    return jax.ops.segment_sum(src, seg, n)
kernel_name = 'mk_hybrid_d1_jaxref_r8_8b4b0c'

def setup_inputs(seed: int=0):
    np.random.seed(seed)
    _w = jnp.asarray

    def _L0_attn_a_setup():
        import jax, jax.numpy as jnp
        import numpy as np
        B, SQ, H = (2, 256, 256)
        NH = 16
        HN = H // NH
        key = jax.random.key(seed)
        ks = jax.random.split(key, 6)
        query = jax.random.normal(ks[0], (B, SQ, H), dtype=jnp.float32)
        k_in = jax.random.normal(ks[1], (B, SQ, H), dtype=jnp.float32)
        v_in = jax.random.normal(ks[2], (B, SQ, H), dtype=jnp.float32)
        Wqkv = jax.random.normal(ks[3], (3 * H, H), dtype=jnp.float32) * (1.0 / np.sqrt(H))
        Wproj = jax.random.normal(ks[4], (H, H), dtype=jnp.float32) * (1.0 / np.sqrt(H))
        bproj = jnp.zeros((H,), dtype=jnp.float32)
        return {'query': query, 'key': k_in, 'value': v_in, 'Wqkv': Wqkv, 'Wproj': Wproj, 'bproj': bproj}
    _L0_attn_a_in = _L0_attn_a_setup()

    def _L0_attn_b_setup():
        import jax, jax.numpy as jnp
        import numpy as np
        from jax import lax
        B, L, D = (2, 256, 256)
        H, DK, DV, K = (16, 128, 128, 4)
        Q_DIM = H * DK
        V_DIM = H * DV

        def silu(x):
            return x * jax.nn.sigmoid(x)

        def causal_dwconv(x, w, b):
            Kk = w.shape[1]
            xp = jnp.pad(x, ((0, 0), (Kk - 1, 0), (0, 0)))
            kern = w.T[:, None, :]
            y = lax.conv_general_dilated(xp, kern, window_strides=(1,), padding='VALID', dimension_numbers=('NWC', 'WIO', 'NWC'), feature_group_count=w.shape[0])
            return y + b

        def layernorm(x, w, b, eps=1e-05):
            m = jnp.mean(x, axis=-1, keepdims=True)
            var = jnp.mean((x - m) ** 2, axis=-1, keepdims=True)
            return (x - m) * lax.rsqrt(var + eps) * w + b
        key = jax.random.key(seed)
        ks = jax.random.split(key, 16)
        s = 0.02
        f32 = jnp.float32
        return {'hidden_states': jax.random.normal(ks[0], (B, L, D), f32), 'Wq': jax.random.normal(ks[1], (D, Q_DIM), f32) * s, 'Wk': jax.random.normal(ks[2], (D, Q_DIM), f32) * s, 'Wv': jax.random.normal(ks[3], (D, V_DIM), f32) * s, 'Wb': jax.random.normal(ks[4], (D, H), f32) * s, 'bb': jnp.full((H,), -2.0, f32), 'Wg': jax.random.normal(ks[5], (D, V_DIM), f32) * s, 'Wo': jax.random.normal(ks[6], (V_DIM, D), f32) * s, 'qconv_w': jax.random.normal(ks[7], (Q_DIM, K), f32) * 0.5, 'qconv_b': jnp.zeros((Q_DIM,), f32), 'kconv_w': jax.random.normal(ks[8], (Q_DIM, K), f32) * 0.5, 'kconv_b': jnp.zeros((Q_DIM,), f32), 'qn_w': jnp.ones((DK,), f32), 'qn_b': jnp.zeros((DK,), f32), 'kn_w': jnp.ones((DK,), f32), 'kn_b': jnp.zeros((DK,), f32)}
    _L0_attn_b_in = _L0_attn_b_setup()

    def _L0_ffn_setup():
        import jax, jax.numpy as jnp
        import numpy as np
        TOP_K = 2
        key = jax.random.key(seed)
        ks = jax.random.split(key, 5)
        B, S, D, INTER, E = (4, 256, 256, 256, 8)
        x = jax.random.normal(ks[0], (B, S, D), dtype=jnp.float32)
        w1 = jax.random.normal(ks[1], (INTER, D), dtype=jnp.float32) * (1.0 / np.sqrt(D))
        w3 = jax.random.normal(ks[2], (INTER, INTER), dtype=jnp.float32) * (1.0 / np.sqrt(INTER))
        w2 = jax.random.normal(ks[3], (D, INTER), dtype=jnp.float32) * (1.0 / np.sqrt(INTER))
        wr = jax.random.normal(ks[4], (E, D), dtype=jnp.float32) * (1.0 / np.sqrt(D))
        return {'x': x, 'w1': w1, 'w3': w3, 'w2': w2, 'wr': wr}
    _L0_ffn_in = _L0_ffn_setup()
    _d = {'L0_attn_a_query': _L0_attn_a_in['query'], 'L0_attn_a_key': _L0_attn_a_in['key'], 'L0_attn_a_value': _L0_attn_a_in['value'], 'L0_attn_a_Wqkv': _L0_attn_a_in['Wqkv'], 'L0_attn_a_Wproj': _L0_attn_a_in['Wproj'], 'L0_attn_a_bproj': _L0_attn_a_in['bproj'], 'L0_attn_b_Wq': _L0_attn_b_in['Wq'], 'L0_attn_b_Wk': _L0_attn_b_in['Wk'], 'L0_attn_b_Wv': _L0_attn_b_in['Wv'], 'L0_attn_b_Wb': _L0_attn_b_in['Wb'], 'L0_attn_b_bb': _L0_attn_b_in['bb'], 'L0_attn_b_Wg': _L0_attn_b_in['Wg'], 'L0_attn_b_Wo': _L0_attn_b_in['Wo'], 'L0_attn_b_qconv_w': _L0_attn_b_in['qconv_w'], 'L0_attn_b_qconv_b': _L0_attn_b_in['qconv_b'], 'L0_attn_b_kconv_w': _L0_attn_b_in['kconv_w'], 'L0_attn_b_kconv_b': _L0_attn_b_in['kconv_b'], 'L0_attn_b_qn_w': _L0_attn_b_in['qn_w'], 'L0_attn_b_qn_b': _L0_attn_b_in['qn_b'], 'L0_attn_b_kn_w': _L0_attn_b_in['kn_w'], 'L0_attn_b_kn_b': _L0_attn_b_in['kn_b'], 'L0_ffn_w1': _L0_ffn_in['w1'], 'L0_ffn_w3': _L0_ffn_in['w3'], 'L0_ffn_w2': _L0_ffn_in['w2'], 'L0_ffn_wr': _L0_ffn_in['wr']}
    _x0 = _d['L0_attn_a_query']
    _d['L0_attn_a_query'] = jax.random.normal(jax.random.fold_in(jax.random.key(seed), 1), (4, 512, 256), dtype=_x0.dtype)
    del _x0
    return _d

def reference(L0_attn_a_query, L0_attn_a_key, L0_attn_a_value, L0_attn_a_Wqkv, L0_attn_a_Wproj, L0_attn_a_bproj, L0_attn_b_Wq, L0_attn_b_Wk, L0_attn_b_Wv, L0_attn_b_Wb, L0_attn_b_bb, L0_attn_b_Wg, L0_attn_b_Wo, L0_attn_b_qconv_w, L0_attn_b_qconv_b, L0_attn_b_kconv_w, L0_attn_b_kconv_b, L0_attn_b_qn_w, L0_attn_b_qn_b, L0_attn_b_kn_w, L0_attn_b_kn_b, L0_ffn_w1, L0_ffn_w3, L0_ffn_w2, L0_ffn_wr):

    def _L0_attn_a_ref(query, key, value, Wqkv, Wproj, bproj):
        import jax, jax.numpy as jnp
        import numpy as np
        B, SQ, H = (2, 256, 256)
        NH = 16
        HN = H // NH
        b, sq, h = query.shape
        nh, hn = (NH, HN)
        norm = 1.0 / jnp.sqrt(jnp.asarray(hn, query.dtype))
        x = jnp.transpose(query, (1, 0, 2)).reshape(sq * b, h)
        mixed = x @ Wqkv.T
        mixed = mixed.reshape(sq, b, nh, 3, hn)
        q = mixed[..., 0, :]
        k = mixed[..., 1, :]
        v = mixed[..., 2, :]
        q = q.reshape(sq, b * nh, hn).transpose(1, 0, 2)
        k = k.reshape(sq, b * nh, hn).transpose(1, 0, 2)
        v = v.reshape(sq, b * nh, hn).transpose(1, 0, 2)
        attn = jnp.einsum('gqd,gkd->gqk', q, k) * norm
        attn = jax.nn.softmax(attn, axis=-1)
        ctx = jnp.einsum('gqk,gkd->gqd', attn, v)
        ctx = ctx.reshape(nh, b, sq, hn)
        ctx = jnp.transpose(ctx, (2, 1, 0, 3)).reshape(sq * b, h)
        out = ctx @ Wproj.T + bproj
        out = out.reshape(sq, b, h)
        return jnp.transpose(out, (1, 0, 2))

    def _L0_attn_b_ref(hidden_states, Wq, Wk, Wv, Wb, bb, Wg, Wo, qconv_w, qconv_b, kconv_w, kconv_b, qn_w, qn_b, kn_w, kn_b):
        import jax, jax.numpy as jnp
        import numpy as np
        from jax import lax
        B, L, D = (2, 256, 256)
        H, DK, DV, K = (16, 128, 128, 4)
        Q_DIM = H * DK
        V_DIM = H * DV

        def silu(x):
            return x * jax.nn.sigmoid(x)

        def causal_dwconv(x, w, b):
            Kk = w.shape[1]
            xp = jnp.pad(x, ((0, 0), (Kk - 1, 0), (0, 0)))
            kern = w.T[:, None, :]
            y = lax.conv_general_dilated(xp, kern, window_strides=(1,), padding='VALID', dimension_numbers=('NWC', 'WIO', 'NWC'), feature_group_count=w.shape[0])
            return y + b

        def layernorm(x, w, b, eps=1e-05):
            m = jnp.mean(x, axis=-1, keepdims=True)
            var = jnp.mean((x - m) ** 2, axis=-1, keepdims=True)
            return (x - m) * lax.rsqrt(var + eps) * w + b
        Bs, Ls, Ds = hidden_states.shape
        q = hidden_states @ Wq
        k = hidden_states @ Wk
        v = hidden_states @ Wv
        beta = jax.nn.sigmoid(hidden_states @ Wb + bb)
        gate = silu(hidden_states @ Wg)
        q = silu(causal_dwconv(q, qconv_w, qconv_b))
        k = silu(causal_dwconv(k, kconv_w, kconv_b))
        q = layernorm(q.reshape(Bs, Ls, H, DK), qn_w, qn_b)
        k = layernorm(k.reshape(Bs, Ls, H, DK), kn_w, kn_b)
        v = v.reshape(Bs, Ls, H, DV)
        qs = q.transpose(1, 0, 2, 3)
        ks_ = k.transpose(1, 0, 2, 3)
        vs = v.transpose(1, 0, 2, 3)
        bs = beta.transpose(1, 0, 2)
        S0 = jnp.zeros((Bs, H, DV, DK), hidden_states.dtype)

        def step(S, inp):
            q_t, k_t, v_t, b_t = inp
            b = b_t[..., None, None]
            S = (1.0 - b) * S + b * (v_t[..., :, None] * k_t[..., None, :])
            o_t = jnp.einsum('bhvk,bhk->bhv', S, q_t)
            return (S, o_t)
        _, os = lax.scan(step, S0, (qs, ks_, vs, bs))
        o = os.transpose(1, 0, 2, 3).reshape(Bs, Ls, H * DV)
        o = o * gate
        return o @ Wo

    def _L0_ffn_ref(x, w1, w3, w2, wr):
        import jax, jax.numpy as jnp
        import numpy as np
        TOP_K = 2
        B, S, D = x.shape
        xr = x.reshape(-1, D)
        route_probs = jax.nn.softmax(xr @ wr.T, axis=-1)
        routes_k, indices_k = jax.lax.top_k(route_probs, TOP_K)
        gates = routes_k / jnp.sum(routes_k, axis=-1, keepdims=True)
        h = jax.nn.silu(xr @ w1.T)
        h = jax.nn.silu(h @ w3.T)
        h = h @ w2.T
        out = jnp.zeros_like(xr)
        for k in range(TOP_K):
            out = out.at[indices_k[:, k]].add(gates[:, k:k + 1] * h)
        return out.reshape(B, S, D)
    x = L0_attn_a_query
    x = x + _L0_attn_a_ref(_layernorm(x, axis=-1), L0_attn_a_key, L0_attn_a_value, L0_attn_a_Wqkv, L0_attn_a_Wproj, L0_attn_a_bproj)
    x = x + _L0_ffn_ref(_layernorm(x, axis=-1), L0_ffn_w1, L0_ffn_w3, L0_ffn_w2, L0_ffn_wr)
    x = x + _L0_attn_b_ref(_layernorm(x, axis=-1), L0_attn_b_Wq, L0_attn_b_Wk, L0_attn_b_Wv, L0_attn_b_Wb, L0_attn_b_bb, L0_attn_b_Wg, L0_attn_b_Wo, L0_attn_b_qconv_w, L0_attn_b_qconv_b, L0_attn_b_kconv_w, L0_attn_b_kconv_b, L0_attn_b_qn_w, L0_attn_b_qn_b, L0_attn_b_kn_w, L0_attn_b_kn_b)
    x = x + _L0_ffn_ref(_layernorm(x, axis=-1), L0_ffn_w1, L0_ffn_w3, L0_ffn_w2, L0_ffn_wr)
    return x

_drawn_inputs = setup_inputs


def setup_inputs(seed=0):
    import zlib

    import numpy as np

    out = dict(_drawn_inputs(seed))
    spreads = {'L0_attn_a_bproj': (0.0, 0.1),
     'L0_attn_b_bb': (-2.0, 0.6),
     'L0_attn_b_qconv_b': (0.0, 0.534),
     'L0_attn_b_kconv_b': (0.0, 0.518),
     'L0_attn_b_qn_w': (1.0, 0.6),
     'L0_attn_b_qn_b': (0.0, 0.8),
     'L0_attn_b_kn_w': (1.0, 0.6),
     'L0_attn_b_kn_b': (0.0, 0.8)}
    factors = {'L0_attn_b_Wb': 4.579}
    for name, (base, spread) in spreads.items():
        noise = np.random.default_rng([zlib.crc32(name.encode()), seed]).standard_normal(out[name].shape)
        drawn = base * np.exp(spread * noise) if base else spread * noise
        out[name] = jnp.asarray(drawn.astype(out[name].dtype))
    for name, factor in factors.items():
        out[name] = (out[name] * factor).astype(out[name].dtype)
    return out
```

```python
from contextlib import ExitStack

import concourse.bass as bass
from concourse import mybir

F32 = mybir.dt.float32
F32R = mybir.dt.float32r
ALU = mybir.AluOpType
ACT = mybir.ActivationFunctionType
AX = mybir.AxisListType

P = 128
EPS = 1e-5
NB, SEQ, D = 4, 512, 256
KD = D // P
NT = NB * SEQ // P
TPB = SEQ // P

NH, HN = 16, 16
SLOT = 32
HPG = P // HN
STACK = 3 * HN
SOFT_SCALE = float(HN) ** -0.5

NE = 8

LH, DK, TAPS = 16, 128, 4


def f32(ap):
    return ap.bitcast(F32)


def split_passes(hi_a, lo_a, hi_b, lo_b):
    return ((hi_a, hi_b), (hi_a, lo_b), (lo_a, hi_b))


def setup(nc, semaphore, x, ident, x_tok):
    with ExitStack() as ctx:
        x_loaded = semaphore("x_loaded")
        ident_zero = semaphore("ident_zero")
        ident_ready = semaphore("ident_ready")
        block = ctx.enter_context(nc.Block())

        @block.sync
        def _(sp):
            sp.dma_start(x_tok[:], x.rearrange("b (t p) d -> p (b t) d", p=P)).then_inc(x_loaded, 16)
            sp.wait_ge(x_loaded, 16)

        @block.gpsimd
        def _(pool):
            pool.memset(ident[:], 0.0).then_inc(ident_zero, 1)
            pool.wait_ge(ident_zero, 1)
            pool.affine_select(out=ident[:], in_=ident[:], compare_op=ALU.not_equal, fill=1.0, base=0,
                               pattern=[[-1, P]], channel_multiplier=1).then_inc(ident_ready, 1)
            pool.wait_ge(ident_ready, 1)


def norm_transpose(nc, semaphore, tag, x_tok, ident, xn_hi, xn_lo, tiles, group):
    groups = tiles // group
    cols = group * P
    with ExitStack() as ctx:
        def sb(name, shape, dt=F32):
            return ctx.enter_context(nc.sbuf_tensor(f"{name}_{tag}", shape, dt))

        def sem(name):
            return semaphore(f"{name}_{tag}")

        stats = sb("ln_stats", [P, tiles, 6])
        mean_var = sb("ln_mean_var", [P, tiles, 2])
        var_eps = sb("ln_var_eps", [P, tiles])
        rstd = sb("ln_rstd", [P, tiles])
        minus_half = sb("ln_minus_half", [P, group])
        xn = sb("ln_xn", [P, 2, group, D])
        xt = [[ctx.enter_context(nc.psum_tensor(f"ln_xt{i}{k}_{tag}", [P, cols], F32)) for k in range(KD)]
              for i in range(2)]
        stats_done, aggregated, half_set, eps_added, rstd_ready, normed, transposed, hi_done, lo_done = (
            sem(s) for s in ("stats_done", "aggregated", "half_set", "eps_added", "rstd_ready", "normed",
                             "transposed", "hi_done", "lo_done"))
        block = ctx.enter_context(nc.Block())

        @block.vector
        def _(dve):
            def statistics(g):
                for n in range(g * group, (g + 1) * group):
                    dve.bn_stats(stats[:, n, :], x_tok[:, n, :]).then_inc(stats_done, 1)
                for n in range(g * group, (g + 1) * group):
                    dve.wait_ge(stats_done, n + 1)
                    dve.bn_aggr(mean_var[:, n, :], stats[:, n, :]).then_inc(aggregated, 1)

            def normalise(g):
                dve.wait_ge(rstd_ready, g + 1)
                if g >= 2:
                    dve.wait_ge(transposed, g - 1)
                for t in range(group):
                    n = g * group + t
                    dve.tensor_scalar(xn[:, g % 2, t, :], x_tok[:, n, :], mean_var[:, n, 0:1], rstd[:, n:n + 1],
                                      ALU.subtract, ALU.mult).then_inc(normed, 1)

            def low_parts(g):
                for k in range(KD):
                    dve.wait_ge(hi_done, g * KD + k + 1)
                    c = slice(g * cols, (g + 1) * cols)
                    dve.tensor_tensor(xn_lo[:, k, c], xt[g % 2][k][:], f32(xn_hi[:, k, c]),
                                      ALU.subtract).then_inc(lo_done, 1)

            statistics(0)
            for g in range(groups):
                if g + 1 < groups:
                    statistics(g + 1)
                normalise(g)
                if g >= 1:
                    low_parts(g - 1)
            low_parts(groups - 1)

        @block.gpsimd
        def _(pool):
            pool.memset(minus_half[:], -0.5).then_inc(half_set, 1)
            pool.wait_ge(half_set, 1)
            for g in range(groups):
                c = slice(g * group, (g + 1) * group)
                pool.wait_ge(aggregated, (g + 1) * group)
                pool.tensor_scalar(var_eps[:, c], mean_var[:, c, 1], EPS, None, ALU.add).then_inc(eps_added, 1)
                pool.wait_ge(eps_added, g + 1)
                pool.tensor_tensor(rstd[:, c], var_eps[:, c], minus_half[:], ALU.pow).then_inc(rstd_ready, 1)

        @block.tensor
        def _(pe):
            for g in range(groups):
                pe.wait_ge(normed, (g + 1) * group)
                if g >= 2:
                    pe.wait_ge(lo_done, KD * (g - 1))
                for k in range(KD):
                    for t in range(group):
                        last = pe.transpose(xt[g % 2][k][:, t * P:(t + 1) * P],
                                            xn[:, g % 2, t, k * P:(k + 1) * P], ident[:])
                last.then_inc(transposed, 1)

        @block.scalar
        def _(act):
            for g in range(groups):
                act.wait_ge(transposed, g + 1)
                for k in range(KD):
                    act.activation(xn_hi[:, k, g * cols:(g + 1) * cols], xt[g % 2][k][:],
                                   ACT.Copy).then_inc(hi_done, 1)


def softmax_attention(nc, semaphore, w_qkv, xn_hi, xn_lo, ident, ctx_tok):
    groups = NB * KD
    tiles_per_group = HPG * TPB
    quads = HPG // 4
    chunks = quads * TPB
    max_per_chunk = 5
    qkv = 3 * D
    with ExitStack() as ctx:
        def sb(name, shape, dt=F32):
            return ctx.enter_context(nc.sbuf_tensor(name, shape, dt))

        def psum(name, shape):
            return ctx.enter_context(nc.psum_tensor(name, shape, F32))

        def sem(name):
            return semaphore(name)

        w_raw = sb("a_w_raw", [P, KD, qkv])
        w_hi = sb("a_w_hi", [P, KD, qkv], F32R)
        w_lo = sb("a_w_lo", [P, KD, qkv], F32R)
        dense_hi = sb("a_dense_hi", [P, 2, 2, SEQ], F32R)
        dense_lo = sb("a_dense_lo", [P, 2, 2, SEQ], F32R)
        q_stack = [sb(f"a_q_stack{i}", [STACK + 2, HPG, SEQ], F32R) for i in range(2)]
        k_stack = [sb(f"a_k_stack{i}", [STACK + 2, HPG, SEQ], F32R) for i in range(2)]
        v_tok = [sb(f"a_v_tok{i}", [P, TPB, HPG, SLOT]) for i in range(3)]
        neg_max = sb("a_neg_max", [P, 2, tiles_per_group])
        max_hi = sb("a_max_hi", [tiles_per_group, 2, P], F32R)
        max_lo = sb("a_max_lo", [tiles_per_group, 2, P], F32R)
        probs = sb("a_probs", [P, 2, 4, SEQ])
        ctx_t = sb("a_ctx_t", [P, 2, SEQ])
        rden = sb("a_rden", [P, 2, 4, TPB])

        scores_t = [psum(f"a_scores_t{i}", [P, 2, SEQ]) for i in range(2)]
        scores = [psum(f"a_scores{i}", [P, SEQ]) for i in range(2)]
        ctx_acc = psum("a_ctx_acc", [P, SEQ])
        misc = psum("a_misc", [P, SEQ])

        w_loaded = sem("a_w_loaded")
        w_hi_ready = sem("a_w_hi_ready")
        w_lo_ready = sem("a_w_lo_ready")
        constants = sem("a_constants")
        proj_done = sem("a_proj_done")
        dense_hi_done = sem("a_dense_hi_done")
        dense_lo_done = sem("a_dense_lo_done")
        stacked = [[sem(f"a_stacked{i}{q}") for q in range(quads)] for i in range(2)]
        v_done = sem("a_v_done")
        v_copied = sem("a_v_copied")
        scores_done = sem("a_scores_done")
        max_done = sem("a_max_done")
        max_t_done = sem("a_max_t_done")
        max_hi_done = sem("a_max_hi_done")
        max_lo_done = sem("a_max_lo_done")
        max_rows = [sem(f"a_max_rows{i}") for i in range(2)]
        scores_t_done = sem("a_scores_t_done")
        probs_done = sem("a_probs_done")
        pv_done = sem("a_pv_done")
        ctx_copied = sem("a_ctx_copied")
        ctx_t_done = sem("a_ctx_t_done")
        rden_done = sem("a_rden_done")
        ctx_done = sem("a_ctx_done")
        block = ctx.enter_context(nc.Block())

        @block.sync
        def _(sp):
            sp.dma_start(w_raw[:], w_qkv).then_inc(w_loaded, 16)

            def stack(g, quad):
                i, hs = g % 2, slice(quad * 4, quad * 4 + 4)
                rows = slice(quad * 4 * HN, (quad + 1) * 4 * HN)
                if g == 0:
                    sp.wait_ge(constants, 11)
                sp.wait_ge(dense_hi_done, 2 * g + 2)
                sp.wait_ge(dense_lo_done, 2 * g + 2)
                if g >= 2:
                    sp.wait_ge(pv_done, (g - 2) * chunks + (quad + 1) * TPB)
                for dst, w, parts in ((q_stack[i], 0, (dense_hi, dense_lo, dense_hi)),
                                      (k_stack[i], 1, (dense_hi, dense_hi, dense_lo))):
                    for r, src in enumerate(parts):
                        sp.dma_start(f32(dst[r * HN:(r + 1) * HN, hs, :]),
                                     f32(src[rows, i, w, :])).then_inc(stacked[i][quad], 16)

            def rows(g):
                i = g % 2
                sp.wait_ge(max_hi_done, g + 1)
                sp.dma_start(f32(q_stack[i][STACK:STACK + 1, :, :]), f32(max_hi[:, i, :])).then_inc(max_rows[i], 16)
                sp.wait_ge(max_lo_done, g + 1)
                sp.dma_start(f32(q_stack[i][STACK + 1:STACK + 2, :, :]), f32(max_lo[:, i, :])).then_inc(max_rows[i], 16)

            for quad in range(quads):
                stack(0, quad)
            for s in range(groups):
                if s + 1 < groups:
                    stack(s + 1, 0)
                rows(s)
                if s + 1 < groups:
                    stack(s + 1, 1)

        @block.gpsimd
        def _(pool):
            for i in range(2):
                pool.memset(f32(k_stack[i][:]), 1.0).then_inc(constants, 1)
            for i in range(3):
                pool.memset(v_tok[i][:, :, :, 0:HN], 0.0).then_inc(constants, 1)
                pool.memset(v_tok[i][:, :, :, HN:HN + 1], 1.0).then_inc(constants, 1)
                pool.memset(v_tok[i][:, :, :, HN + 1:SLOT], 0.0).then_inc(constants, 1)

        @block.tensor
        def _(pe):
            def project(g):
                b, m, i = g // KD, g % KD, g % 2
                tok = slice(b * SEQ, (b + 1) * SEQ)
                for w in range(2):
                    if g == 0:
                        pe.wait_ge(w_lo_ready, 1)
                        pe.wait_ge(w_hi_ready, 1)
                    elif g == 1:
                        pe.wait_ge(dense_lo_done, w + 1)
                        pe.wait_ge(v_copied, 1)
                    else:
                        pe.wait_ge(max_done, (g - 1) * tiles_per_group)
                    ch = slice(w * D + m * P, w * D + (m + 1) * P)
                    n = 0
                    for k in range(KD):
                        for lhs, rhs in split_passes(w_hi[:, k, ch], w_lo[:, k, ch], xn_hi[:, k, tok], xn_lo[:, k, tok]):
                            last = pe.matmul(scores[w][:], lhs, rhs, start=(n == 0), stop=(n == 3 * KD - 1))
                            n += 1
                    last.then_inc(proj_done, 1)
                ch = slice(2 * D + m * P, 2 * D + (m + 1) * P)
                for t in range(TPB):
                    tok = slice(b * SEQ + t * P, b * SEQ + (t + 1) * P)
                    n = 0
                    for k in range(KD):
                        for lhs, rhs in split_passes(xn_hi[:, k, tok], xn_lo[:, k, tok], w_hi[:, k, ch], w_lo[:, k, ch]):
                            last = pe.matmul(misc[:, t * P:(t + 1) * P], lhs, rhs, start=(n == 0), stop=(n == 3 * KD - 1))
                            n += 1
                last.then_inc(v_done, 1)

            def max_scores(g, j):
                h, t, i = j // TPB, j % TPB, g % 2
                n = g * tiles_per_group + j
                if j % (4 * TPB) == 0:
                    pe.wait_ge(stacked[i][j // (4 * TPB)], 6 * 16 * (g // 2 + 1))
                if j == 0:
                    pe.wait_ge(dense_lo_done, 2 * g + 2)
                    if g + 1 < groups:
                        pe.wait_ge(dense_lo_done, 2 * g + 4)
                if j >= 2:
                    pe.wait_ge(max_done, n - 1)
                pe.matmul(scores[n % 2][:], q_stack[i][0:STACK, h, t * P:(t + 1) * P], k_stack[i][0:STACK, h, :],
                          start=True, stop=True).then_inc(scores_done, 1)

            def transpose_max(g):
                pe.wait_ge(max_done, (g + 1) * tiles_per_group)
                pe.wait_ge(v_copied, min(g + 2, groups))
                pe.transpose(misc[0:tiles_per_group, 0:P], neg_max[:, g % 2, :], ident[:]).then_inc(max_t_done, 1)

            def probs_chunk(g, c):
                quad, t, i = c // TPB, c % TPB, g % 2
                n = g * chunks + c
                if c == 0:
                    pe.wait_ge(max_rows[i], 32 * (g // 2 + 1))
                for half in range(2):
                    if n >= 1:
                        pe.wait_ge(probs_done, 2 * (n - 1) + half + 1)
                    for e in range(2):
                        h = quad * 4 + half * 2 + e
                        last = pe.matmul(scores_t[half][:, e, :], k_stack[i][:, h, t * P:(t + 1) * P],
                                         q_stack[i][:, h, :], start=True, stop=True)
                    last.then_inc(scores_t_done, 1)

            def context(g, c):
                quad, t = c // TPB, c % TPB
                n = g * chunks + c
                pe.wait_ge(probs_done, 2 * n + 2)
                if t == 0:
                    if n >= TPB:
                        pe.wait_ge(ctx_copied, n // TPB)
                    pe.wait_ge(v_copied, g + 1)
                for e in range(4):
                    last = pe.matmul(ctx_acc[e * SLOT:(e + 1) * SLOT, :], v_tok[g % 3][:, t, quad * 4 + e, :],
                                     probs[:, n % 2, e, :], start=(t == 0), stop=(t == TPB - 1))
                last.then_inc(pv_done, 1)

            def transpose_context(q):
                pe.wait_ge(ctx_copied, q + 1)
                if q >= 1:
                    pe.wait_ge(ctx_done, q)
                for t in range(TPB):
                    last = pe.transpose(misc[:, t * P:(t + 1) * P], ctx_t[:, q % 2, t * P:(t + 1) * P], ident[:])
                last.then_inc(ctx_t_done, 1)

            project(0)
            for s in range(groups + 1):
                if s >= 1:
                    pe.wait_ge(max_hi_done, s)
                    pe.wait_ge(max_lo_done, s)
                if s >= 2:
                    transpose_context((s - 1) * quads - 1)
                if s + 1 < groups:
                    if s >= 2:
                        pe.wait_ge(ctx_done, (s - 1) * quads)
                    project(s + 1)
                done = 0
                for c in range(chunks):
                    if s >= 1:
                        probs_chunk(s - 1, c)
                    if s < groups:
                        for j in range(done, min(done + max_per_chunk, tiles_per_group)):
                            max_scores(s, j)
                        done = min(done + max_per_chunk, tiles_per_group)
                    if s >= 1:
                        if c >= 1:
                            context(s - 1, c - 1)
                        if c == TPB + 1:
                            pe.wait_ge(v_copied, min(s + 2, groups))
                            if s >= 1:
                                pe.wait_ge(max_lo_done, s)
                            transpose_context((s - 1) * quads)
                if s < groups:
                    if s >= 1:
                        pe.wait_ge(ctx_done, (s - 1) * quads + 1)
                    transpose_max(s)
                if s >= 1:
                    context(s - 1, chunks - 1)
            pe.wait_ge(max_lo_done, groups)
            transpose_context(groups * quads - 1)

        @block.scalar
        def _(act):
            act.wait_ge(w_loaded, 16)
            act.activation(w_hi[:], w_raw[:], ACT.Copy).then_inc(w_hi_ready, 1)

            def split_projection(g):
                i = g % 2
                for w in range(2):
                    act.wait_ge(proj_done, 2 * g + w + 1)
                    if g >= 2:
                        for quad in range(quads):
                            act.wait_ge(stacked[i][quad], 6 * 16 * (g // 2))
                    act.activation(dense_hi[:, i, w, :], scores[w][:], ACT.Copy).then_inc(dense_hi_done, 1)
                act.wait_ge(v_done, g + 1)
                if g == 0:
                    act.wait_ge(constants, 11)
                if g >= 3:
                    act.wait_ge(pv_done, (g - 2) * chunks)
                act.activation(v_tok[g % 3][:, :, :, 0:HN], misc[:].rearrange("p (t h e) -> p t h e", t=TPB, h=HPG),
                               ACT.Copy).then_inc(v_copied, 1)

            def exponentials(g, c):
                n = g * chunks + c
                for half in range(2):
                    act.wait_ge(scores_t_done, 2 * n + half + 1)
                    if n >= 2:
                        act.wait_ge(pv_done, n - 1)
                    act.activation(probs[:, n % 2, 2 * half:2 * half + 2, :], scores_t[half][:], ACT.Exp,
                                   scale=SOFT_SCALE).then_inc(probs_done, 1)

            def copy_context(q):
                act.wait_ge(pv_done, (q + 1) * TPB)
                if q >= 2:
                    act.wait_ge(ctx_t_done, q - 1)
                act.activation(ctx_t[:, q % 2, :], ctx_acc[:], ACT.Copy).then_inc(ctx_copied, 1)

            split_projection(0)
            for s in range(groups + 1):
                if s >= 2:
                    copy_context((s - 1) * quads - 1)
                if s + 1 < groups:
                    split_projection(s + 1)
                for c in range(chunks):
                    if s >= 1:
                        exponentials(s - 1, c)
                        if c == TPB:
                            copy_context((s - 1) * quads)
                if s < groups:
                    act.wait_ge(max_t_done, s + 1)
                    if s >= 2:
                        act.wait_ge(max_rows[s % 2], 32 * (s // 2))
                    act.activation(max_hi[:, s % 2, :], misc[0:tiles_per_group, 0:P], ACT.Copy).then_inc(max_hi_done, 1)
            copy_context(groups * quads - 1)

        @block.vector
        def _(dve):
            dve.wait_ge(w_hi_ready, 1)
            dve.tensor_tensor(w_lo[:], w_raw[:], f32(w_hi[:]), ALU.subtract).then_inc(w_lo_ready, 1)

            def split_projection(g):
                i = g % 2
                for w in range(2):
                    dve.wait_ge(dense_hi_done, 2 * g + w + 1)
                    dve.tensor_tensor(dense_lo[:, i, w, :], scores[w][:], f32(dense_hi[:, i, w, :]),
                                      ALU.subtract).then_inc(dense_lo_done, 1)

            def negated_max(g, j):
                n = g * tiles_per_group + j
                dve.wait_ge(scores_done, n + 1)
                if j == 0 and g >= 2:
                    dve.wait_ge(max_t_done, g - 1)
                dve.tensor_reduce(neg_max[:, g % 2, j:j + 1], scores[n % 2][:], AX.X, ALU.max,
                                  negate=True).then_inc(max_done, 1)

            def normalise(q):
                dve.wait_ge(ctx_t_done, q + 1)
                view = misc[:].rearrange("p (t h e) -> p h t e", t=TPB, h=4)
                dve.reciprocal(rden[:, q % 2, :, :], view[:, :, :, HN]).then_inc(rden_done, 1)
                dve.wait_ge(rden_done, q + 1)
                dve.tensor_tensor(ctx_tok[:, :, :, q * HN:(q + 1) * HN], view[:, :, :, 0:HN],
                                  rden[:, q % 2, :, :].unsqueeze(3).to_broadcast([P, 4, TPB, HN]),
                                  ALU.mult).then_inc(ctx_done, 1)

            split_projection(0)
            for s in range(groups + 1):
                if s >= 2:
                    normalise((s - 1) * quads - 1)
                if s + 1 < groups:
                    split_projection(s + 1)
                done = 0
                for c in range(chunks):
                    if s < groups:
                        for j in range(done, min(done + max_per_chunk, tiles_per_group)):
                            negated_max(s, j)
                        done = min(done + max_per_chunk, tiles_per_group)
                    if s >= 1 and c == TPB + 1:
                        normalise((s - 1) * quads)
                if s < groups:
                    dve.wait_ge(max_hi_done, s + 1)
                    dve.tensor_tensor(max_lo[:, s % 2, :], misc[0:tiles_per_group, 0:P], f32(max_hi[:, s % 2, :]),
                                      ALU.subtract).then_inc(max_lo_done, 1)
            normalise(groups * quads - 1)


def project_context(nc, semaphore, w_proj, b_proj, ctx_tok, ident, x_tok):
    with ExitStack() as ctx:
        def sem(name):
            return semaphore(name)

        w = ctx.enter_context(nc.sbuf_tensor("p_w", [P, KD, D], F32))
        bias = ctx.enter_context(nc.sbuf_tensor("p_bias", [1, D], F32))
        ones = ctx.enter_context(nc.sbuf_tensor("p_ones", [1, P], F32))
        ctx_t = ctx.enter_context(nc.sbuf_tensor("p_ctx_t", [P, 2, KD, SEQ], F32))
        turned = [[ctx.enter_context(nc.psum_tensor(f"p_turned{i}{k}", [P, SEQ], F32)) for k in range(KD)]
                  for i in range(2)]
        acc = [ctx.enter_context(nc.psum_tensor(f"p_acc{i}", [P, 2, D], F32)) for i in range(2)]
        w_loaded, ones_set, turned_done, copied_act, copied_dve, acc_done, added = (
            sem(s) for s in ("p_w_loaded", "p_ones_set", "p_turned_done", "p_copied_act", "p_copied_dve",
                             "p_acc_done", "p_added"))
        block = ctx.enter_context(nc.Block())

        @block.sync
        def _(sp):
            sp.dma_start(w[:], w_proj).then_inc(w_loaded, 16)
            sp.dma_start(bias[:], b_proj).then_inc(w_loaded, 16)

        @block.gpsimd
        def _(pool):
            pool.memset(ones[:], 1.0).then_inc(ones_set, 1)

        @block.tensor
        def _(pe):
            def turn(b):
                if b >= 2:
                    pe.wait_ge(copied_act, b - 1)
                    pe.wait_ge(copied_dve, b - 1)
                for k in range(KD):
                    for t in range(TPB):
                        last = pe.transpose(turned[b % 2][k][:, t * P:(t + 1) * P],
                                            ctx_tok[:, b, t, k * P:(k + 1) * P], ident[:])
                last.then_inc(turned_done, 1)

            turn(0)
            for b in range(NB):
                if b + 1 < NB:
                    turn(b + 1)
                if b == 0:
                    pe.wait_ge(w_loaded, 32)
                    pe.wait_ge(ones_set, 1)
                pe.wait_ge(copied_act, b + 1)
                pe.wait_ge(copied_dve, b + 1)
                for half in range(2):
                    n = 2 * b + half
                    if n >= 2:
                        pe.wait_ge(added, n - 1)
                    for e in range(2):
                        t = half * 2 + e
                        for k in range(KD):
                            pe.matmul(acc[half][:, e, :], ctx_t[:, b % 2, k, t * P:(t + 1) * P], w[:, k, :],
                                      start=(k == 0), stop=False)
                        last = pe.matmul(acc[half][:, e, :], ones[:], bias[:], start=False, stop=True)
                    last.then_inc(acc_done, 1)

        @block.scalar
        def _(act):
            for b in range(NB):
                act.wait_ge(turned_done, b + 1)
                if b >= 2:
                    act.wait_ge(acc_done, 2 * (b - 1))
                act.activation(ctx_t[:, b % 2, 0, :], turned[b % 2][0][:], ACT.Copy).then_inc(copied_act, 1)

        @block.vector
        def _(dve):
            def copy(b):
                dve.wait_ge(turned_done, b + 1)
                if b >= 2:
                    dve.wait_ge(acc_done, 2 * (b - 1))
                dve.tensor_copy(ctx_t[:, b % 2, 1, :], turned[b % 2][1][:]).then_inc(copied_dve, 1)

            copy(0)
            for b in range(NB):
                if b + 1 < NB:
                    copy(b + 1)
                for half in range(2):
                    dve.wait_ge(acc_done, 2 * b + half + 1)
                    t = b * TPB + half * 2
                    dve.tensor_tensor(x_tok[:, t:t + 2, :], acc[half][:], x_tok[:, t:t + 2, :],
                                      ALU.add).then_inc(added, 1)


def routed_ffn(nc, semaphore, tag, w_in, w_mid, w_out, xn_hi, xn_lo, ident, x_tok):
    with ExitStack() as ctx:
        def sb(name, shape, dt=F32):
            return ctx.enter_context(nc.sbuf_tensor(f"f_{name}_{tag}", shape, dt))

        def psum(name, shape):
            return ctx.enter_context(nc.psum_tensor(f"f_{name}_{tag}", shape, F32))

        def sem(name):
            return semaphore(f"f_{name}_{tag}")

        w_in_raw = sb("w_in_raw", [P, KD, D + NE])
        w_in_hi = sb("w_in_hi", [P, KD, D + NE], F32R)
        w_in_lo = sb("w_in_lo", [P, KD, D + NE], F32R)
        w3 = sb("w3", [P, KD, D])
        w2 = sb("w2", [P, KD, D])
        hidden_t = sb("hidden_t", [P, KD, NB * SEQ])
        hidden = sb("hidden", [P, 2, 2, D])
        rank = sb("rank", [P, NE])
        logits = sb("logits", [P, NT, NE])
        masked = sb("masked", [P, NT, NE])
        same = sb("same", [P, NT, NE])
        ranked = sb("ranked", [P, NT, NE])
        top = sb("top", [P, 2, NT])
        first = sb("first", [P, 2, NT])
        chosen = sb("chosen", [P, 2, NT, NE])
        gap = sb("gap", [P, NT])
        ratio = sb("ratio", [P, NT])
        total = sb("total", [P, NT])
        weight = sb("weight", [P, 2, NT])
        gates = sb("gates", [P, 3, NT, NE])
        summed = sb("summed", [NE, D])
        summed_t = sb("summed_t", [P, KD, NE])
        logits_ps = psum("logits_ps", [P, NT, NE])
        up = [psum(f"up{i}", [P, SEQ]) for i in range(2)]
        mid = [psum(f"mid{i}", [P, 2, D]) for i in range(2)]
        acc = psum("acc", [NE, D])
        tail = psum("tail", [P, KD, NE])
        rows = psum("rows", [NE, D])

        names = ("w_in_loaded", "w3_loaded", "w2_loaded", "rank_set", "w_hi_ready", "w_lo_ready", "logits_done", "route", "gap_ready",
                 "ratio_ready", "gates_ready", "up_done", "up_read", "mid_done", "mid_read", "acc_done",
                 "hidden_used", "summed_ready", "tail_done", "tail_read", "rows_done", "rows_added")
        (w_in_loaded, w3_loaded, w2_loaded, rank_set, w_hi_ready, w_lo_ready, logits_done, route, gap_ready,
         ratio_ready, gates_ready, up_done, up_read, mid_done, mid_read, acc_done,
         hidden_used, summed_ready, tail_done, tail_read, rows_done, rows_added) = (sem(n) for n in names)
        block = ctx.enter_context(nc.Block())

        @block.sync
        def _(sp):
            sp.dma_start(w_in_raw[:], w_in).then_inc(w_in_loaded, 16)
            sp.dma_start(w3[:], w_mid).then_inc(w3_loaded, 16)
            sp.dma_start(w2[:], w_out).then_inc(w2_loaded, 16)

        @block.gpsimd
        def _(pool):
            for e in range(NE):
                pool.memset(rank[:, e:e + 1], float(NE - e)).then_inc(rank_set, 1)

        @block.tensor
        def _(pe):
            pe.wait_ge(w_hi_ready, 1)
            pe.wait_ge(w_lo_ready, 1)
            for n in range(NT):
                tok, j = slice(n * P, (n + 1) * P), 0
                for k in range(KD):
                    for lhs, rhs in split_passes(xn_hi[:, k, tok], xn_lo[:, k, tok],
                                                 w_in_hi[:, k, D:], w_in_lo[:, k, D:]):
                        last = pe.matmul(logits_ps[:, n, :], lhs, rhs, start=(j == 0), stop=(j == 3 * KD - 1))
                        j += 1
            last.then_inc(logits_done, 1)

            for n in range(KD * NB):
                b, m, j = n // KD, n % KD, 0
                tok, ch = slice(b * SEQ, (b + 1) * SEQ), slice(m * P, (m + 1) * P)
                if n >= 2:
                    pe.wait_ge(up_read, n - 1)
                for k in range(KD):
                    for lhs, rhs in split_passes(w_in_hi[:, k, ch], w_in_lo[:, k, ch],
                                                 xn_hi[:, k, tok], xn_lo[:, k, tok]):
                        last = pe.matmul(up[n % 2][:], lhs, rhs, start=(j == 0), stop=(j == 3 * KD - 1))
                        j += 1
                last.then_inc(up_done, 1)

            pe.wait_ge(w3_loaded, 16)

            def middle(n):
                pe.wait_ge(up_read, KD * (n * 2 // TPB + 1))
                if n >= 2:
                    pe.wait_ge(mid_read, n - 1)
                for e in range(2):
                    t = 2 * n + e
                    for k in range(KD):
                        last = pe.matmul(mid[n % 2][:, e, :], hidden_t[:, k, t * P:(t + 1) * P], w3[:, k, :],
                                         start=(k == 0), stop=(k == KD - 1))
                last.then_inc(mid_done, 1)

            def gather(n):
                pe.wait_ge(mid_read, n + 1)
                if n == 0:
                    pe.wait_ge(gates_ready, 1)
                for e in range(2):
                    t = 2 * n + e
                    last = pe.matmul(acc[:], gates[:, 2, t, :], hidden[:, n % 2, e, :], start=(t == 0), stop=(t == NT - 1))
                last.then_inc(acc_done, 1)

            middle(0)
            for n in range(NT // 2):
                if n + 1 < NT // 2:
                    middle(n + 1)
                gather(n)
            pe.wait_ge(summed_ready, 1)
            for k in range(KD):
                last = pe.transpose(tail[:, k, :], summed[:, k * P:(k + 1) * P], ident[0:NE, 0:NE])
            last.then_inc(tail_done, 1)
            pe.wait_ge(tail_read, 1)
            pe.wait_ge(w2_loaded, 16)
            for k in range(KD):
                last = pe.matmul(rows[:], summed_t[:, k, :], w2[:, k, :], start=(k == 0), stop=(k == KD - 1))
            last.then_inc(rows_done, 1)

        @block.scalar
        def _(act):
            act.wait_ge(w_in_loaded, 16)
            act.activation(w_in_hi[:], w_in_raw[:], ACT.Copy).then_inc(w_hi_ready, 1)
            act.wait_ge(gap_ready, 1)
            act.activation(ratio[:], gap[:], ACT.Exp).then_inc(ratio_ready, 1)
            for n in range(KD * NB):
                b, m = n // KD, n % KD
                act.wait_ge(up_done, n + 1)
                act.activation(hidden_t[:, m, b * SEQ:(b + 1) * SEQ], up[n % 2][:], ACT.Silu).then_inc(up_read, 1)
            for n in range(NT // 2):
                act.wait_ge(mid_done, n + 1)
                if n >= 2:
                    act.wait_ge(acc_done, n - 1)
                act.activation(hidden[:, n % 2, :, :], mid[n % 2][:], ACT.Silu).then_inc(mid_read, 1)

        @block.vector
        def _(dve):
            dve.wait_ge(w_hi_ready, 1)
            dve.tensor_tensor(w_in_lo[:], w_in_raw[:], f32(w_in_hi[:]), ALU.subtract).then_inc(w_lo_ready, 1)
            dve.wait_ge(logits_done, 1)
            dve.wait_ge(rank_set, NE)
            dve.tensor_copy(logits[:], logits_ps[:]).then_inc(route, 1)
            step = 1
            wide = [P, NT, NE]
            for pick in range(2):
                src = logits if pick == 0 else masked
                dve.wait_ge(route, step)
                dve.tensor_reduce(top[:, pick, :], src[:], AX.X, ALU.max).then_inc(route, 1)
                dve.wait_ge(route, step + 1)
                dve.tensor_tensor(same[:], src[:], top[:, pick, :].unsqueeze(2).to_broadcast(wide),
                                  ALU.is_equal).then_inc(route, 1)
                dve.wait_ge(route, step + 2)
                dve.tensor_tensor(ranked[:], same[:], rank[:].unsqueeze(1).to_broadcast(wide),
                                  ALU.mult).then_inc(route, 1)
                dve.wait_ge(route, step + 3)
                dve.tensor_reduce(first[:, pick, :], ranked[:], AX.X, ALU.max).then_inc(route, 1)
                dve.wait_ge(route, step + 4)
                dve.tensor_tensor(chosen[:, pick, :, :], ranked[:], first[:, pick, :].unsqueeze(2).to_broadcast(wide),
                                  ALU.is_equal).then_inc(route, 1)
                step += 5
                if pick == 0:
                    dve.wait_ge(route, step)
                    dve.scalar_tensor_tensor(masked[:], chosen[:, 0, :, :], -3.0e38, logits[:],
                                             ALU.mult, ALU.add).then_inc(route, 1)
                    step += 1
            dve.wait_ge(route, step)
            dve.tensor_tensor(gap[:], top[:, 1, :], top[:, 0, :], ALU.subtract).then_inc(gap_ready, 1)
            dve.wait_ge(ratio_ready, 1)
            dve.tensor_scalar(total[:], ratio[:], 1.0, None, ALU.add).then_inc(route, 1)
            dve.wait_ge(route, step + 1)
            dve.reciprocal(weight[:, 0, :], total[:]).then_inc(route, 1)
            dve.wait_ge(route, step + 2)
            dve.tensor_tensor(weight[:, 1, :], ratio[:], weight[:, 0, :], ALU.mult).then_inc(route, 1)
            dve.wait_ge(route, step + 3)
            for pick in range(2):
                dve.tensor_tensor(gates[:, pick, :, :], chosen[:, pick, :, :],
                                  weight[:, pick, :].unsqueeze(2).to_broadcast(wide), ALU.mult).then_inc(route, 1)
            dve.wait_ge(route, step + 5)
            dve.tensor_tensor(gates[:, 2, :, :], gates[:, 0, :, :], gates[:, 1, :, :], ALU.add).then_inc(gates_ready, 1)
            dve.wait_ge(acc_done, NT // 2)
            dve.tensor_copy(summed[:], acc[:]).then_inc(summed_ready, 1)
            dve.wait_ge(tail_done, 1)
            dve.tensor_copy(summed_t[:], tail[:]).then_inc(tail_read, 1)
            dve.wait_ge(rows_done, 1)
            dve.tensor_tensor(x_tok[0:NE, 0, :], rows[:], x_tok[0:NE, 0, :], ALU.add).then_inc(rows_added, 1)


def decay_gates(nc, semaphore, w_beta, b_beta, xn_hi, xn_lo, ident, beta_tok, keep_rows):
    with ExitStack() as ctx:
        def sb(name, shape, dt=F32):
            return ctx.enter_context(nc.sbuf_tensor(f"d_{name}", shape, dt))

        def sem(name):
            return semaphore(f"d_{name}")

        w_raw = sb("w_raw", [P, KD, LH])
        w_hi = sb("w_hi", [P, KD, LH], F32R)
        w_lo = sb("w_lo", [P, KD, LH], F32R)
        bias = sb("bias", [1, LH])
        ones = sb("ones", [1, P])
        keep = sb("keep", [P, NT, LH])
        keep_t = sb("keep_t", [P, 2, P])
        z = ctx.enter_context(nc.psum_tensor("d_z", [P, NT, LH], F32))
        turned = ctx.enter_context(nc.psum_tensor("d_turned", [P, 2, P], F32))
        loaded, w_hi_ready, w_lo_ready, ones_set, z_done, beta_done, keep_done, turned_done, copied, written = (
            sem(n) for n in ("loaded", "w_hi_ready", "w_lo_ready", "ones_set", "z_done", "beta_done", "keep_done",
                             "turned_done", "copied", "written"))
        block = ctx.enter_context(nc.Block())

        @block.sync
        def _(sp):
            sp.dma_start(w_raw[:], w_beta).then_inc(loaded, 16)
            sp.dma_start(bias[:], b_beta).then_inc(loaded, 16)
            sp.wait_ge(copied, 1)
            rows = keep_rows.rearrange("h (j t p) -> j t h p", j=2, p=P)
            for j in range(2):
                sp.dma_start(rows[j], keep_t[:, j, :]).then_inc(written, 16)
            sp.wait_ge(written, 32)

        @block.gpsimd
        def _(pool):
            pool.memset(ones[:], 1.0).then_inc(ones_set, 1)

        @block.tensor
        def _(pe):
            pe.wait_ge(w_hi_ready, 1)
            pe.wait_ge(w_lo_ready, 1)
            pe.wait_ge(ones_set, 1)
            for n in range(NT):
                tok, j = slice(n * P, (n + 1) * P), 0
                for k in range(KD):
                    for lhs, rhs in split_passes(xn_hi[:, k, tok], xn_lo[:, k, tok], w_hi[:, k, :], w_lo[:, k, :]):
                        pe.matmul(z[:, n, :], lhs, rhs, start=(j == 0), stop=False)
                        j += 1
                last = pe.matmul(z[:, n, :], ones[:], bias[:], start=False, stop=True)
            last.then_inc(z_done, 1)
            pe.wait_ge(keep_done, 1)
            for j in range(2):
                last = pe.transpose(turned[:, j, :], keep[:, j * (NT // 2):(j + 1) * (NT // 2), :], ident[:])
            last.then_inc(turned_done, 1)

        @block.scalar
        def _(act):
            act.wait_ge(loaded, 32)
            act.activation(w_hi[:], w_raw[:], ACT.Copy).then_inc(w_hi_ready, 1)
            act.wait_ge(z_done, 1)
            act.activation(beta_tok[:], z[:], ACT.Sigmoid).then_inc(beta_done, 1)

        @block.vector
        def _(dve):
            dve.wait_ge(w_hi_ready, 1)
            dve.tensor_tensor(w_lo[:], w_raw[:], f32(w_hi[:]), ALU.subtract).then_inc(w_lo_ready, 1)
            dve.wait_ge(beta_done, 1)
            dve.tensor_scalar(keep[:], beta_tok[:], -1.0, 1.0, ALU.mult, ALU.add).then_inc(keep_done, 1)
            dve.wait_ge(turned_done, 1)
            dve.tensor_copy(keep_t[:], turned[:]).then_inc(copied, 1)


def linear_attention(nc, semaphore, w_heads, w_o, params, norms, xn_hi, xn_lo, ident, beta_tok, keep_rows, x_tok):
    PAIRS, BODY = LH // 2, 2 * NB
    UNITS = PAIRS * BODY
    PAIR = 2 * DK
    NPAR = 2 * (TAPS + 1)
    WIDTH = [SEQ - i * P for i in range(TPB)]
    START = [0, 512, 1024, 896]
    CAUSAL = sum(WIDTH)
    with ExitStack() as ctx:
        def sb(name, shape, dt=F32):
            return ctx.enter_context(nc.sbuf_tensor(f"l_{name}", shape, dt))

        def psum(name, shape=(P, SEQ)):
            return ctx.enter_context(nc.psum_tensor(f"l_{name}", list(shape), F32))

        def sem(name):
            return semaphore(f"l_{name}")

        Q, K, G, V = range(4)
        w_raw = sb("w_raw", [P, KD, 4, PAIR])
        w_hi = sb("w_hi", [P, KD, 4, PAIR], F32R)
        w_lo = sb("w_lo", [P, KD, 4, PAIR], F32R)
        wo = sb("wo", [P, LH, D])
        par = sb("par", [P, LH, NPAR])
        norm = sb("norm", [P, 4])
        minus_half = sb("minus_half", [P, 2 * TPB])
        quarter = sb("quarter", [P, 2 * TPB])
        diag = sb("diag", [P, SEQ])
        keep = sb("keep", [P, 4, SEQ])
        conv = sb("conv", [P, 2, 2, SEQ])
        stats = sb("stats", [P, 2, 2 * TPB, 6])
        small = sb("small", [P, 8, 2 * TPB])
        scale = sb("scale", [P, 2, 2 * TPB])
        shift = sb("shift", [P, 2, 2 * TPB])
        normed = sb("normed", [P, 2, TPB, DK])
        qk = sb("qk", [P, 2, 2, SEQ])
        decay = sb("decay", [P, CAUSAL])
        masked = sb("masked", [P, 2, CAUSAL])
        gate = sb("gate", [P, 4, SEQ])
        values = sb("values", [P, 4, TPB, PAIR])
        gated = sb("gated", [P, 4, SEQ])

        proj_q, proj_k, proj_gv, turn_q, turn_k, score_a, score_b, outp = (psum(n) for n in (
            "proj_q", "proj_k", "proj_gv", "turn_q", "turn_k", "score_a", "score_b", "outp"))
        proj = (proj_q, proj_k)
        turn = (turn_q, turn_k)

        w_loaded, consts_loaded, consts_set, w_hi_done, w_ready = (sem(n) for n in (
            "w_loaded", "consts_loaded", "consts_set", "w_hi_done", "w_ready"))
        keep_loaded = [sem(f"keep_loaded{i}") for i in range(4)]
        q_proj, k_proj, g_proj, v_proj = (sem(n) for n in ("q_proj", "k_proj", "g_proj", "v_proj"))
        q_tap, k_tap, conv_step, q_conv, k_conv = (sem(n) for n in ("q_tap", "k_tap", "conv_step", "q_conv", "k_conv"))
        q_act, k_act, gate_act = (sem(n) for n in ("q_act", "k_act", "gate_act"))
        turned, stats_done, stat_step, scales_ready = (sem(n) for n in ("turned", "stats_done", "stat_step", "scales_ready"))
        norm_done, returned, qk_ready = (sem(n) for n in ("norm_done", "returned", "qk_ready"))
        score_a_done, score_b_done, score_c_done = (sem(n) for n in ("score_a_done", "score_b_done", "score_c_done"))
        decay_done, masked_a, masked_b, masked_c = (sem(n) for n in ("decay_done", "masked_a", "masked_b", "masked_c"))
        values_done, read_out, gated_done, out_done, added = (sem(n) for n in (
            "values_done", "read_out", "gated_done", "out_done", "added"))
        proj_sem, tap_sem, conv_sem, act_sem = (q_proj, k_proj), (q_tap, k_tap), (q_conv, k_conv), (q_act, k_act)
        block = ctx.enter_context(nc.Block())

        def wait(eng, semaphore, count):
            if not isinstance(count, int) or count > 0:
                eng.wait_ge(semaphore, count)

        def wait_apart(eng, semaphore, count):
            wait(eng, semaphore, count)
            eng.nop(nofuse=True)

        def has(u, lag):
            return not isinstance(u, int) or 0 <= u - lag < UNITS

        def steps(eng, step, lags):
            for k in range(BODY):
                step(0, k, k)
            with eng.Fori(1, PAIRS) as pair:
                for k in range(BODY):
                    step(pair, k, pair * BODY + k)
            for k in range(lags):
                step(PAIRS, k, UNITS + k)

        @block.sync
        def _(sp):
            sp.dma_start(w_raw[:], w_heads[0]).then_inc(w_loaded, 16)
            sp.dma_start(par[:], params).then_inc(consts_loaded, 16)
            sp.dma_start(norm[:], norms).then_inc(consts_loaded, 16)
            sp.dma_start(wo[:], w_o).then_inc(consts_loaded, 16)

            def step(pair, k, u):
                wait(sp, decay_done, u - 3)
                b, e = k // 2, k % 2
                row = keep_rows[bass.ds(2 * pair + e, 1), b * SEQ:(b + 1) * SEQ]
                sp.dma_start(keep[:, k % 4, :], row.to_broadcast([P, SEQ])).then_inc(keep_loaded[k % 4], 16)
                if k == BODY - 1:
                    wait(sp, w_ready, 4 * (pair + 1))
                    nxt = pair + 1
                    if not (isinstance(nxt, int) and nxt >= PAIRS):
                        sp.dma_start(w_raw[:], w_heads[bass.ds(nxt, 1)]).then_inc(w_loaded, 16)

            for k in range(BODY):
                step(0, k, k)
            with sp.Fori(1, PAIRS - 1) as pair:
                for k in range(BODY):
                    step(pair, k, pair * BODY + k)
            for k in range(BODY):
                step(PAIRS - 1, k, (PAIRS - 1) * BODY + k)

        @block.gpsimd
        def _(pool):
            pool.memset(minus_half[:], -0.5).then_inc(consts_set, 1)
            pool.memset(quarter[:], 0.25).then_inc(consts_set, 1)
            pool.memset(diag[:, P:], 0.0).then_inc(consts_set, 1)
            pool.tensor_copy(diag[:, 0:P], ident[:]).then_inc(consts_set, 1)

            def split_weights(pair, part):
                n = 4 * pair + part
                if part == Q:
                    wait(pool, w_loaded, 16 * (pair + 1))
                wait_apart(pool, (q_proj, k_proj, g_proj, v_proj)[part], BODY * pair)
                pool.tensor_copy(w_hi[:, :, part, :], w_raw[:, :, part, :]).then_inc(w_hi_done, 1)
                wait(pool, w_hi_done, n + 1)
                pool.tensor_tensor(w_lo[:, :, part, :], w_raw[:, :, part, :], f32(w_hi[:, :, part, :]),
                                   ALU.subtract).then_inc(w_ready, 1)

            def scales(v, k):
                i = k % 2
                st = stats[:, i]
                wait(pool, stats_done, v + 1)
                wait(pool, norm_done, 2 * (v - 1))
                pool.tensor_tensor(small[:, 0, :], st[:, :, 1], st[:, :, 4], ALU.add)
                pool.tensor_tensor(small[:, 1, :], st[:, :, 1], st[:, :, 4], ALU.subtract)
                pool.tensor_tensor(small[:, 2, :], st[:, :, 2], st[:, :, 5], ALU.add).then_inc(stat_step, 1)
                wait(pool, stat_step, 4 * v + 1)
                pool.tensor_tensor(small[:, 3, :], small[:, 1, :], small[:, 1, :], ALU.mult)
                pool.tensor_scalar(small[:, 4, :], small[:, 2, :], 1.0 / DK, EPS, ALU.mult, ALU.add)
                pool.tensor_scalar(small[:, 5, :], small[:, 0, :], -0.5, 0.0, ALU.mult, ALU.add).then_inc(stat_step, 1)
                wait(pool, stat_step, 4 * v + 2)
                pool.tensor_tensor(small[:, 6, :], small[:, 3, :], quarter[:], ALU.mult).then_inc(stat_step, 1)
                wait(pool, stat_step, 4 * v + 3)
                pool.tensor_tensor(small[:, 7, :], small[:, 6, :], small[:, 4, :], ALU.add).then_inc(stat_step, 1)
                wait(pool, stat_step, 4 * v + 4)
                pool.tensor_tensor(scale[:, i, :], small[:, 7, :], minus_half[:], ALU.pow).then_inc(scales_ready, 1)
                wait(pool, scales_ready, 2 * v + 1)
                pool.tensor_tensor(shift[:, i, :], small[:, 5, :], scale[:, i, :], ALU.mult).then_inc(scales_ready, 1)

            pool.wait_ge(consts_set, 4)
            for part in (Q, K, G):
                split_weights(0, part)

            def step(pair, k, u):
                if k == 0 and has(u, 0):
                    split_weights(pair, V)
                if has(u, 1):
                    scales(u - 1, (k - 1) % BODY)
                if k == BODY - 1 and has(u, 0):
                    nxt = pair + 1
                    for part in (Q, K, G):
                        split_weights(nxt, part)

            for k in range(BODY):
                step(0, k, k)
            with pool.Fori(1, PAIRS - 1) as pair:
                for k in range(BODY):
                    step(pair, k, pair * BODY + k)
            for k in range(BODY):
                u = (PAIRS - 1) * BODY + k
                if k == 0:
                    split_weights(PAIRS - 1, V)
                scales(u - 1, (k - 1) % BODY)
            scales(UNITS - 1, BODY - 1)

        @block.tensor
        def _(pe):
            def project(out, part, k, lhs_is_weight=True):
                b, e = k // 2, k % 2
                tok, ch, j = slice(b * SEQ, (b + 1) * SEQ), slice(e * DK, (e + 1) * DK), 0
                for kd in range(KD):
                    for lhs, rhs in split_passes(w_hi[:, kd, part, ch], w_lo[:, kd, part, ch],
                                                 xn_hi[:, kd, tok], xn_lo[:, kd, tok]):
                        last = pe.matmul(out[:], lhs, rhs, start=(j == 0), stop=(j == 3 * KD - 1))
                        j += 1
                return last

            def project_values(k):
                b, half = k // 2, k % 2
                for t in range(2):
                    n = b * TPB + half * 2 + t
                    tok, j = slice(n * P, (n + 1) * P), 0
                    for kd in range(KD):
                        for lhs, rhs in split_passes(xn_hi[:, kd, tok], xn_lo[:, kd, tok],
                                                     w_hi[:, kd, V, :], w_lo[:, kd, V, :]):
                            last = pe.matmul(proj_gv[:, t * PAIR:(t + 1) * PAIR], lhs, rhs,
                                             start=(j == 0), stop=(j == 3 * KD - 1))
                            j += 1
                return last

            def score(out, at, i, par_):
                return pe.matmul(out[:, at:at + WIDTH[i]], qk[:, 1, par_, i * P:(i + 1) * P],
                                 qk[:, 0, par_, i * P:SEQ], start=True, stop=True)

            def step(pair, k, u):
                if has(u, 0):
                    for w in range(2):
                        if k == 0:
                            wait(pe, w_ready, 4 * pair + w + 1)
                        wait(pe, conv_sem[w], u)
                        project(proj[w], w, k).then_inc(proj_sem[w], 1)
                if has(u, 1):
                    v, kk = u - 1, (k - 1) % BODY
                    wait(pe, qk_ready, v)
                    for w in range(2):
                        wait(pe, act_sem[w], v + 1)
                        for t in range(TPB):
                            last = pe.transpose(turn[w][:, t * P:(t + 1) * P],
                                                conv[:, w, kk % 2, t * P:(t + 1) * P], ident[:])
                    last.then_inc(turned, 1)
                if has(u, 3):
                    v, kk = u - 3, (k - 3) % BODY
                    m, e, c = kk % 2, kk % 2, kk // 2
                    wait(pe, masked_c, v + 1)
                    wait(pe, values_done, v + 2 - kk % 2)
                    wait(pe, added, v - 1)
                    for i in reversed(range(TPB)):
                        last = pe.matmul(outp[:, i * P:SEQ], values[:, c, i, e * DK:(e + 1) * DK],
                                         masked[:, m, START[i]:START[i] + WIDTH[i]],
                                         start=(i == TPB - 1), stop=(i == 0), skip_group_check=True)
                    last.then_inc(read_out, 1)
                if has(u, 0):
                    if k == 0:
                        wait(pe, w_ready, 4 * pair + G + 1)
                    wait(pe, values_done, u)
                    project(proj_gv, G, k).then_inc(g_proj, 1)
                if has(u, 2):
                    v, m = u - 2, k % 2
                    wait(pe, qk_ready, v + 1)
                    wait(pe, masked_c, v)
                    score(score_a, 0, 0, m).then_inc(score_a_done, 1)
                    score(score_b, 0, 1, m)
                    score(score_b, WIDTH[1], 3, m).then_inc(score_b_done, 1)
                if has(u, 0):
                    if k == 0:
                        wait(pe, w_ready, 4 * pair + V + 1)
                    wait(pe, gate_act, u + 1)
                    project_values(k).then_inc(v_proj, 1)
                if has(u, 4):
                    v, kk = u - 4, (k - 4) % BODY
                    w, half, p_out = kk // 2, kk % 2, None
                    wait(pe, gated_done, min(v + 2, UNITS) if isinstance(v, int) else v + 2)
                    wait(pe, added, v)
                    head = 2 * ((pair if k >= 4 else pair - 1))
                    for t in range(2):
                        for e in range(2):
                            tok = slice((half * 2 + t) * P, (half * 2 + t + 1) * P)
                            last = pe.matmul(outp[:, t * D:(t + 1) * D], gated[:, (2 * w + e) % 4, tok],
                                             wo[:, head_of(head, e), :], start=(e == 0), stop=(e == 1))
                    last.then_inc(out_done, 1)
                if has(u, 2):
                    v, m = u - 2, k % 2
                    wait(pe, masked_a, v + 1)
                    score(score_a, 0, 2, m).then_inc(score_c_done, 1)
                if has(u, 1):
                    v = u - 1
                    wait(pe, norm_done, 2 * v + 2)
                    for w in range(2):
                        for t in range(TPB):
                            last = pe.transpose(turn[w][:, t * P:(t + 1) * P], normed[:, w, t, :], ident[:])
                    last.then_inc(returned, 1)

            def head_of(head, e):
                return head + e

            pe.wait_ge(consts_loaded, 48)
            steps(pe, step, 5)

        @block.scalar
        def _(act):
            def step(pair, k, u):
                if has(u, 2):
                    v, m = u - 2, k % 2
                    wait(act, returned, v + 1)
                    wait(act, score_c_done, v - 1)
                    for w in range(2):
                        last = act.activation(qk[:, w, m, :], turn[w][:], ACT.Identity, scale=norm[:, 2 * w:2 * w + 1],
                                              bias=norm[:, 2 * w + 1:2 * w + 2])
                    last.then_inc(qk_ready, 1)
                if has(u, 0):
                    h, m = 2 * pair + k % 2, k % 2
                    for w in range(2):
                        wait(act, proj_sem[w], u + 1)
                        wait_apart(act, turned, u - 1)
                        act.activation(conv[:, w, m, :], proj[w][:], ACT.Copy,
                                       scale=par[:, h, (w + 1) * TAPS - 1:(w + 1) * TAPS]).then_inc(tap_sem[w], 1)
                    for w in range(2):
                        wait_apart(act, conv_sem[w], u + 1)
                        act.activation(conv[:, w, m, :], conv[:, w, m, :], ACT.Silu,
                                       bias=par[:, h, 2 * TAPS + w:2 * TAPS + w + 1]).then_inc(act_sem[w], 1)
                if has(u, 1):
                    v, m = u - 1, (k - 1) % 2
                    wait(act, scales_ready, 2 * v + 2)
                    wait(act, returned, v)
                    for w in range(2):
                        for t in range(TPB):
                            j = w * TPB + t
                            last = act.activation(normed[:, w, t, :], turn[w][:, t * P:(t + 1) * P], ACT.Identity,
                                                  scale=scale[:, m, j:j + 1], bias=shift[:, m, j:j + 1])
                        last.then_inc(norm_done, 1)
                if has(u, 0):
                    wait(act, g_proj, u + 1)
                    wait(act, gated_done, u - 3)
                    act.activation(gate[:, k % 4, :], proj_gv[:], ACT.Silu).then_inc(gate_act, 1)

            act.wait_ge(consts_loaded, 48)
            steps(act, step, 2)

        @block.vector
        def _(dve):
            def step(pair, k, u):
                if has(u, 0):
                    h, m = 2 * pair + k % 2, k % 2
                    for s in range(1, TAPS):
                        for w in range(2):
                            if s == 1:
                                wait(dve, tap_sem[w], u + 1)
                            else:
                                wait(dve, conv_step, 4 * u + 2 * (s - 2) + w + 1)
                            tap = w * TAPS + TAPS - 1 - s
                            ins = dve.scalar_tensor_tensor(conv[:, w, m, s:], proj[w][:, 0:SEQ - s],
                                                           par[:, h, tap:tap + 1], conv[:, w, m, s:],
                                                           ALU.mult, ALU.add)
                            ins.then_inc(conv_sem[w] if s == TAPS - 1 else conv_step, 1)
                if has(u, 1):
                    v, m = u - 1, (k - 1) % 2
                    wait(dve, turned, v + 1)
                    wait(dve, scales_ready, 2 * (v - 1))
                    for w in range(2):
                        for t in range(TPB):
                            last = dve.bn_stats(stats[:, m, w * TPB + t, :], turn[w][:, t * P:(t + 1) * P])
                    last.then_inc(stats_done, 1)
                if has(u, 3):
                    v, r = u - 3, (k - 3) % 4
                    wait(dve, read_out, v + 1)
                    wait(dve, gate_act, v + 1)
                    wait(dve, out_done, v - 2 - (k - 3) % 2)
                    dve.tensor_tensor(gated[:, r, :], outp[:], gate[:, r, :], ALU.mult).then_inc(gated_done, 1)
                if has(u, 2):
                    v, r, m = u - 2, (k - 2) % 4, k % 2
                    kk = (k - 2) % BODY
                    rounds = 2 * (pair if k >= 2 else pair - 1) + kk // 4 + 1
                    wait(dve, keep_loaded[r], 16 * rounds)
                    wait(dve, masked_c, v)
                    for i in range(TPB):
                        last = dve.tensor_tensor_scan(decay[:, START[i]:START[i] + WIDTH[i]], keep[:, r, i * P:SEQ],
                                                      diag[:, 0:WIDTH[i]], 0.0, ALU.mult, ALU.add)
                    last.then_inc(decay_done, 1)
                    wait(dve, decay_done, v + 1)
                    wait(dve, read_out, v - 1)
                    wait(dve, score_a_done, v + 1)
                    dve.tensor_tensor(masked[:, m, 0:512], score_a[:], decay[:, 0:512], ALU.mult).then_inc(masked_a, 1)
                    wait(dve, score_b_done, v + 1)
                    dve.tensor_tensor(masked[:, m, 512:1024], score_b[:], decay[:, 512:1024],
                                      ALU.mult).then_inc(masked_b, 1)
                if has(u, 0):
                    b, half, m = k // 2, k % 2, k // 2
                    n = b * TPB + 2 * half
                    wait(dve, v_proj, u + 1)
                    wait(dve, read_out, u - half - 6)
                    dve.tensor_tensor(
                        values[:, m, 2 * half:2 * half + 2, :].rearrange("p t (e c) -> p t e c", e=2),
                        proj_gv[:].rearrange("p (t e c) -> p t e c", t=2, e=2),
                        beta_tok[:, n:n + 2, bass.ds(2 * pair, 2)].unsqueeze(3).to_broadcast([P, 2, 2, DK]),
                        ALU.mult).then_inc(values_done, 1)
                if has(u, 4):
                    v, kk = u - 4, (k - 4) % BODY
                    n = (kk // 2) * TPB + 2 * (kk % 2)
                    wait(dve, out_done, v + 1)
                    wait(dve, added, v - 3)
                    dve.tensor_tensor(x_tok[:, n:n + 2, :], outp[:].rearrange("p (t d) -> p t d", t=2),
                                      x_tok[:, n:n + 2, :], ALU.add).then_inc(added, 1)
                if has(u, 2):
                    v, m = u - 2, k % 2
                    wait(dve, score_c_done, v + 1)
                    dve.tensor_tensor(masked[:, m, 1024:CAUSAL], score_a[:, 0:CAUSAL - 1024], decay[:, 1024:CAUSAL],
                                      ALU.mult).then_inc(masked_c, 1)

            dve.wait_ge(consts_loaded, 48)
            dve.wait_ge(consts_set, 4)
            steps(dve, step, 5)


def store(nc, semaphore, x_tok, out):
    with ExitStack() as ctx:
        stored = semaphore("stored")
        block = ctx.enter_context(nc.Block())

        @block.sync
        def _(sp):
            sp.dma_start(out.rearrange("b (t p) d -> p (b t) d", p=P), x_tok[:]).then_inc(stored, 16)
            sp.wait_ge(stored, 16)


def build(nc, x, w_qkv, w_proj, b_proj, w_in, w_mid, w_out, w_beta, b_beta, w_heads, w_o, params, norms, out, stage=9):
    keep_rows = nc.dram_tensor("keep_rows", [LH, NB * SEQ], F32, kind="Internal").ap()
    held = []

    def semaphore(name):
        held.append(nc.alloc_semaphore(name))
        return held[-1]

    with ExitStack() as ctx:
        x_tok = ctx.enter_context(nc.sbuf_tensor("x_tok", [P, NT, D], F32))
        ident = ctx.enter_context(nc.sbuf_tensor("ident", [P, P], F32))
        xn_hi = ctx.enter_context(nc.sbuf_tensor("xn_hi", [P, KD, NB * SEQ], F32R))
        xn_lo = ctx.enter_context(nc.sbuf_tensor("xn_lo", [P, KD, NB * SEQ], F32R))
        setup(nc, semaphore, x, ident, x_tok)
        norm_transpose(nc, semaphore, "a", x_tok, ident, xn_hi, xn_lo, NT, TPB)
        with nc.sbuf_tensor("ctx_tok", [P, NB, TPB, D], F32) as ctx_tok:
            softmax_attention(nc, semaphore, w_qkv, xn_hi, xn_lo, ident, ctx_tok)
            project_context(nc, semaphore, w_proj, b_proj, ctx_tok, ident, x_tok)
        if stage >= 2:
            norm_transpose(nc, semaphore, "b", x_tok, ident, xn_hi, xn_lo, NT, TPB)
            routed_ffn(nc, semaphore, "b", w_in, w_mid, w_out, xn_hi, xn_lo, ident, x_tok)
        nc.clear_and_free_semaphores(held)
        nc.all_engine_barrier()
        held.clear()
        if stage >= 3:
            norm_transpose(nc, semaphore, "c", x_tok, ident, xn_hi, xn_lo, 1, 1)
            with nc.sbuf_tensor("beta_tok", [P, NT, LH], F32) as beta_tok:
                decay_gates(nc, semaphore, w_beta, b_beta, xn_hi, xn_lo, ident, beta_tok, keep_rows)
                linear_attention(nc, semaphore, w_heads, w_o, params, norms, xn_hi, xn_lo, ident, beta_tok, keep_rows, x_tok)
        if stage >= 4:
            norm_transpose(nc, semaphore, "d", x_tok, ident, xn_hi, xn_lo, NT, TPB)
            routed_ffn(nc, semaphore, "d", w_in, w_mid, w_out, xn_hi, xn_lo, ident, x_tok)
        store(nc, semaphore, x_tok, out)


def kernel(**inputs):
    import numpy as np
    import concourse.bacc as bacc
    from concourse.bass_utils import run_bass_kernel_spmd

    def by_channel(a):
        return np.ascontiguousarray(a.reshape(-1, P, a.shape[-1]).transpose(1, 0, 2))

    a = {k: np.asarray(v) for k, v in inputs.items()}
    qkv = a["L0_attn_a_Wqkv"].reshape(NH // 4, 4, 3, HN, D)
    q, k = (qkv[:, :, i].transpose(0, 2, 1, 3).reshape(D, D) for i in range(2))
    v = qkv[:, :, 2].reshape(D, D)
    heads = np.stack([a[f"L0_attn_b_W{n}"].reshape(KD, P, LH // 2, 2 * DK) for n in "qkgv"], axis=3)
    taps = [a[f"L0_attn_b_{n}conv_w"].reshape(LH, DK, TAPS) for n in "qk"]
    biases = [a[f"L0_attn_b_{n}conv_b"].reshape(LH, DK, 1) for n in "qk"]
    arrays = {
        "x": a["L0_attn_a_query"],
        "w_qkv": by_channel(np.concatenate([q, k, v]).T),
        "w_proj": by_channel(a["L0_attn_a_Wproj"].T),
        "b_proj": a["L0_attn_a_bproj"][None],
        "w_in": by_channel(np.concatenate([a["L0_ffn_w1"], a["L0_ffn_wr"]]).T),
        "w_mid": by_channel(a["L0_ffn_w3"].T),
        "w_out": by_channel(a["L0_ffn_w2"].T),
        "w_beta": by_channel(a["L0_attn_b_Wb"]),
        "b_beta": a["L0_attn_b_bb"][None],
        "w_heads": heads.transpose(2, 1, 0, 3, 4),
        "w_o": by_channel(a["L0_attn_b_Wo"]),
        "params": np.concatenate(taps + biases, axis=-1).transpose(1, 0, 2),
        "norms": np.stack([a[f"L0_attn_b_{n}"] for n in ("qn_w", "qn_b", "kn_w", "kn_b")], axis=1),
    }
    arrays = {n: np.ascontiguousarray(v) for n, v in arrays.items()}
    nc = bacc.Bacc("TRN2", target_bir_lowering=False, num_devices=1)
    args = {n: nc.dram_tensor(n, v.shape, mybir.dt.from_np(v.dtype), kind="ExternalInput").ap()
            for n, v in arrays.items()}
    out = nc.dram_tensor("out", (NB, SEQ, D), F32, kind="ExternalOutput").ap()
    build(nc, out=out, **args)
    return run_bass_kernel_spmd(nc, [arrays], core_ids=[0]).results[0]["out"]
```

```python
from contextlib import ExitStack

import concourse.bass as bass
from concourse import mybir

F32 = mybir.dt.float32
F32R = mybir.dt.float32r
ALU = mybir.AluOpType
ACT = mybir.ActivationFunctionType
AX = mybir.AxisListType

P = 128
EPS = 1e-5
NB, SEQ, D = 4, 512, 256
KD = D // P
NT = NB * SEQ // P
TPB = SEQ // P

NH, HN = 16, 16
SLOT = 32
HPG = P // HN
STACK = 3 * HN
SOFT_SCALE = float(HN) ** -0.5

NE = 8

LH, DK, TAPS = 16, 128, 4


def f32(ap):
    return ap.bitcast(F32)


def split_passes(hi_a, lo_a, hi_b, lo_b):
    return ((hi_a, hi_b), (hi_a, lo_b), (lo_a, hi_b))


def setup(nc, semaphore, x, ident, x_tok):
    with ExitStack() as ctx:
        x_loaded = semaphore("x_loaded")
        ident_zero = semaphore("ident_zero")
        ident_ready = semaphore("ident_ready")
        block = ctx.enter_context(nc.Block())

        @block.sync
        def _(sp):
            sp.dma_start(x_tok[:], x.rearrange("b (t p) d -> p (b t) d", p=P)).then_inc(x_loaded, 16)
            sp.wait_ge(x_loaded, 16)

        @block.gpsimd
        def _(pool):
            pool.memset(ident[:], 0.0).then_inc(ident_zero, 1)
            pool.wait_ge(ident_zero, 1)
            pool.affine_select(out=ident[:], in_=ident[:], compare_op=ALU.not_equal, fill=1.0, base=0,
                               pattern=[[-1, P]], channel_multiplier=1).then_inc(ident_ready, 1)
            pool.wait_ge(ident_ready, 1)


def norm_transpose(nc, semaphore, tag, x_tok, ident, xn_hi, xn_lo, tiles, group):
    groups = tiles // group
    cols = group * P
    with ExitStack() as ctx:
        def sb(name, shape, dt=F32):
            return ctx.enter_context(nc.sbuf_tensor(f"{name}_{tag}", shape, dt))

        def sem(name):
            return semaphore(f"{name}_{tag}")

        stats = sb("ln_stats", [P, tiles, 6])
        mean_var = sb("ln_mean_var", [P, tiles, 2])
        var_eps = sb("ln_var_eps", [P, tiles])
        rstd = sb("ln_rstd", [P, tiles])
        minus_half = sb("ln_minus_half", [P, group])
        xn = sb("ln_xn", [P, 2, group, D])
        xt = [[ctx.enter_context(nc.psum_tensor(f"ln_xt{i}{k}_{tag}", [P, cols], F32)) for k in range(KD)]
              for i in range(2)]
        stats_done, aggregated, half_set, eps_added, rstd_ready, normed, transposed, hi_done, lo_done = (
            sem(s) for s in ("stats_done", "aggregated", "half_set", "eps_added", "rstd_ready", "normed",
                             "transposed", "hi_done", "lo_done"))
        block = ctx.enter_context(nc.Block())

        @block.vector
        def _(dve):
            def statistics(g):
                for n in range(g * group, (g + 1) * group):
                    dve.bn_stats(stats[:, n, :], x_tok[:, n, :]).then_inc(stats_done, 1)
                for n in range(g * group, (g + 1) * group):
                    dve.wait_ge(stats_done, n + 1)
                    dve.bn_aggr(mean_var[:, n, :], stats[:, n, :]).then_inc(aggregated, 1)

            def normalise(g):
                dve.wait_ge(rstd_ready, g + 1)
                if g >= 2:
                    dve.wait_ge(transposed, g - 1)
                for t in range(group):
                    n = g * group + t
                    dve.tensor_scalar(xn[:, g % 2, t, :], x_tok[:, n, :], mean_var[:, n, 0:1], rstd[:, n:n + 1],
                                      ALU.subtract, ALU.mult).then_inc(normed, 1)

            def low_parts(g):
                for k in range(KD):
                    dve.wait_ge(hi_done, g * KD + k + 1)
                    c = slice(g * cols, (g + 1) * cols)
                    dve.tensor_tensor(xn_lo[:, k, c], xt[g % 2][k][:], f32(xn_hi[:, k, c]),
                                      ALU.subtract).then_inc(lo_done, 1)

            statistics(0)
            for g in range(groups):
                if g + 1 < groups:
                    statistics(g + 1)
                normalise(g)
                if g >= 1:
                    low_parts(g - 1)
            low_parts(groups - 1)

        @block.gpsimd
        def _(pool):
            pool.memset(minus_half[:], -0.5).then_inc(half_set, 1)
            pool.wait_ge(half_set, 1)
            for g in range(groups):
                c = slice(g * group, (g + 1) * group)
                pool.wait_ge(aggregated, (g + 1) * group)
                pool.tensor_scalar(var_eps[:, c], mean_var[:, c, 1], EPS, None, ALU.add).then_inc(eps_added, 1)
                pool.wait_ge(eps_added, g + 1)
                pool.tensor_tensor(rstd[:, c], var_eps[:, c], minus_half[:], ALU.pow).then_inc(rstd_ready, 1)

        @block.tensor
        def _(pe):
            for g in range(groups):
                pe.wait_ge(normed, (g + 1) * group)
                if g >= 2:
                    pe.wait_ge(lo_done, KD * (g - 1))
                for k in range(KD):
                    for t in range(group):
                        last = pe.transpose(xt[g % 2][k][:, t * P:(t + 1) * P],
                                            xn[:, g % 2, t, k * P:(k + 1) * P], ident[:])
                last.then_inc(transposed, 1)

        @block.scalar
        def _(act):
            for g in range(groups):
                act.wait_ge(transposed, g + 1)
                for k in range(KD):
                    act.activation(xn_hi[:, k, g * cols:(g + 1) * cols], xt[g % 2][k][:],
                                   ACT.Copy).then_inc(hi_done, 1)


def softmax_attention(nc, semaphore, w_qkv, xn_hi, xn_lo, ident, ctx_tok):
    groups = NB * KD
    tiles_per_group = HPG * TPB
    quads = HPG // 4
    chunks = quads * TPB
    max_per_chunk = tiles_per_group // chunks
    tiles_per_quad = tiles_per_group // quads
    qkv = 3 * D
    with ExitStack() as ctx:
        def sb(name, shape, dt=F32):
            return ctx.enter_context(nc.sbuf_tensor(name, shape, dt))

        def psum(name, shape):
            return ctx.enter_context(nc.psum_tensor(name, shape, F32))

        def sem(name):
            return semaphore(name)

        w_raw = sb("a_w_raw", [P, KD, qkv])
        w_hi = sb("a_w_hi", [P, KD, qkv], F32R)
        w_lo = sb("a_w_lo", [P, KD, qkv], F32R)
        dense_hi = sb("a_dense_hi", [P, 2, 2, SEQ], F32R)
        dense_lo = sb("a_dense_lo", [P, 2, 2, SEQ], F32R)
        q_stack = [sb(f"a_q_stack{i}", [STACK + 2, HPG, SEQ], F32R) for i in range(2)]
        k_stack = [sb(f"a_k_stack{i}", [STACK + 2, HPG, SEQ], F32R) for i in range(2)]
        v_tok = [sb(f"a_v_tok{i}", [P, TPB, HPG, SLOT]) for i in range(3)]
        neg_max = sb("a_neg_max", [P, 2, tiles_per_group])
        max_hi = sb("a_max_hi", [tiles_per_quad, quads, P], F32R)
        max_lo = sb("a_max_lo", [tiles_per_quad, quads, P], F32R)
        probs = sb("a_probs", [P, 2, 4, SEQ])
        ctx_t = sb("a_ctx_t", [P, 2, SEQ])
        rden = sb("a_rden", [P, 2, 4, TPB])

        scores_t = [psum(f"a_scores_t{i}", [P, 2, SEQ]) for i in range(2)]
        scores = [psum(f"a_scores{i}", [P, SEQ]) for i in range(2)]
        ctx_acc = psum("a_ctx_acc", [P, SEQ])
        misc = psum("a_misc", [P, SEQ])

        w_loaded = sem("a_w_loaded")
        w_hi_ready = sem("a_w_hi_ready")
        w_lo_ready = sem("a_w_lo_ready")
        constants = sem("a_constants")
        proj_done = sem("a_proj_done")
        dense_hi_done = sem("a_dense_hi_done")
        dense_lo_done = sem("a_dense_lo_done")
        stacked = [[sem(f"a_stacked{i}{q}") for q in range(quads)] for i in range(2)]
        v_done = sem("a_v_done")
        v_copied = sem("a_v_copied")
        scores_done = sem("a_scores_done")
        max_done = sem("a_max_done")
        max_t_done = sem("a_max_t_done")
        max_hi_done = sem("a_max_hi_done")
        max_lo_done = sem("a_max_lo_done")
        max_rows = [sem(f"a_max_rows{q}") for q in range(quads)]
        scores_t_done = sem("a_scores_t_done")
        probs_done = sem("a_probs_done")
        pv_done = sem("a_pv_done")
        ctx_copied = sem("a_ctx_copied")
        ctx_t_done = sem("a_ctx_t_done")
        rden_done = sem("a_rden_done")
        ctx_done = sem("a_ctx_done")
        block = ctx.enter_context(nc.Block())

        @block.sync
        def _(sp):
            sp.dma_start(w_raw[:], w_qkv).then_inc(w_loaded, 16)

            def stack(g, quad):
                i, hs = g % 2, slice(quad * 4, quad * 4 + 4)
                rows = slice(quad * 4 * HN, (quad + 1) * 4 * HN)
                if g == 0:
                    sp.wait_ge(constants, 11)
                sp.wait_ge(dense_hi_done, 2 * g + 2)
                sp.wait_ge(dense_lo_done, 2 * g + 2)
                if g >= 2:
                    sp.wait_ge(scores_t_done, 2 * ((g - 2) * chunks + (quad + 1) * TPB))
                for dst, w, parts in ((q_stack[i], 0, (dense_hi, dense_lo, dense_hi)),
                                      (k_stack[i], 1, (dense_hi, dense_hi, dense_lo))):
                    for r, src in enumerate(parts):
                        sp.dma_start(f32(dst[r * HN:(r + 1) * HN, hs, :]),
                                     f32(src[rows, i, w, :])).then_inc(stacked[i][quad], 16)

            def rows(g, quad):
                i, hs = g % 2, slice(quad * 4, quad * 4 + 4)
                for r, src, done in ((STACK, max_hi, max_hi_done), (STACK + 1, max_lo, max_lo_done)):
                    sp.wait_ge(done, quads * g + quad + 1)
                    sp.dma_start(f32(q_stack[i][r:r + 1, hs, :]), f32(src[:, quad, :])).then_inc(max_rows[quad], 16)

            stack(0, 0)
            stack(0, 1)
            for s in range(groups + 1):
                if s >= 1:
                    rows(s - 1, 1)
                if s + 1 < groups:
                    stack(s + 1, 0)
                if s < groups:
                    rows(s, 0)
                if s + 1 < groups:
                    stack(s + 1, 1)

        @block.gpsimd
        def _(pool):
            for i in range(2):
                pool.memset(f32(k_stack[i][:]), 1.0).then_inc(constants, 1)
            for i in range(3):
                pool.memset(v_tok[i][:, :, :, 0:HN], 0.0).then_inc(constants, 1)
                pool.memset(v_tok[i][:, :, :, HN:HN + 1], 1.0).then_inc(constants, 1)
                pool.memset(v_tok[i][:, :, :, HN + 1:SLOT], 0.0).then_inc(constants, 1)

        @block.tensor
        def _(pe):
            def project(g, w):
                b, m = g // KD, g % KD
                tok, ch, n = slice(b * SEQ, (b + 1) * SEQ), slice(w * D + m * P, w * D + (m + 1) * P), 0
                for k in range(KD):
                    for lhs, rhs in split_passes(w_hi[:, k, ch], w_lo[:, k, ch], xn_hi[:, k, tok], xn_lo[:, k, tok]):
                        last = pe.matmul(misc[:], lhs, rhs, start=(n == 0), stop=(n == 3 * KD - 1))
                        n += 1
                last.then_inc(proj_done, 1)

            def project_values(g):
                b, m = g // KD, g % KD
                ch = slice(2 * D + m * P, 2 * D + (m + 1) * P)
                for t in range(TPB):
                    tok = slice(b * SEQ + t * P, b * SEQ + (t + 1) * P)
                    n = 0
                    for k in range(KD):
                        for lhs, rhs in split_passes(xn_hi[:, k, tok], xn_lo[:, k, tok], w_hi[:, k, ch], w_lo[:, k, ch]):
                            last = pe.matmul(misc[:, t * P:(t + 1) * P], lhs, rhs, start=(n == 0), stop=(n == 3 * KD - 1))
                            n += 1
                last.then_inc(v_done, 1)

            def transpose_max(g, quad):
                pe.wait_ge(max_done, g * tiles_per_group + (quad + 1) * tiles_per_quad)
                js = slice(quad * tiles_per_quad, (quad + 1) * tiles_per_quad)
                pe.transpose(misc[0:tiles_per_quad, 0:P], neg_max[:, g % 2, js], ident[:]).then_inc(max_t_done, 1)

            def transpose_context(q):
                pe.wait_ge(ctx_copied, q + 1)
                for t in range(TPB):
                    last = pe.transpose(misc[:, t * P:(t + 1) * P], ctx_t[:, q % 2, t * P:(t + 1) * P], ident[:])
                last.then_inc(ctx_t_done, 1)

            def max_scores(g, j):
                h, t, i = j // TPB, j % TPB, g % 2
                n = g * tiles_per_group + j
                if j % tiles_per_quad == 0:
                    pe.wait_ge(stacked[i][j // tiles_per_quad], 6 * 16 * (g // 2 + 1))
                if n >= 2:
                    pe.wait_ge(max_done, n - 1)
                pe.matmul(scores[n % 2][:], q_stack[i][0:STACK, h, t * P:(t + 1) * P], k_stack[i][0:STACK, h, :],
                          start=True, stop=True).then_inc(scores_done, 1)

            def probs_chunk(g, c, half):
                quad, t, i = c // TPB, c % TPB, g % 2
                n = g * chunks + c
                if t == 0 and half == 0:
                    pe.wait_ge(max_rows[quad], 32 * (g + 1))
                if n >= 1:
                    pe.wait_ge(probs_done, 2 * (n - 1) + half + 1)
                for e in range(2):
                    h = quad * 4 + half * 2 + e
                    last = pe.matmul(scores_t[half][:, e, :], k_stack[i][:, h, t * P:(t + 1) * P],
                                     q_stack[i][:, h, :], start=True, stop=True)
                last.then_inc(scores_t_done, 1)

            def context(n):
                g, c = n // chunks, n % chunks
                quad, t = c // TPB, c % TPB
                pe.wait_ge(probs_done, 2 * n + 2)
                if t == 0:
                    if n >= TPB:
                        pe.wait_ge(ctx_copied, n // TPB)
                    pe.wait_ge(v_copied, g + 1)
                for e in range(4):
                    last = pe.matmul(ctx_acc[e * SLOT:(e + 1) * SLOT, :], v_tok[g % 3][:, t, quad * 4 + e, :],
                                     probs[:, n % 2, e, :], start=(t == 0), stop=(t == TPB - 1))
                last.then_inc(pv_done, 1)

            def errand(s, c):
                if c == 0 and s >= 1:
                    if s < groups:
                        pe.wait_ge(v_copied, s + 1)
                    transpose_max(s - 1, 1)
                elif c == 1 and s >= 2:
                    pe.wait_ge(max_lo_done, quads * s)
                    transpose_context(quads * (s - 1) - 1)
                elif c == 2 and s + 1 < groups:
                    if s >= 2:
                        pe.wait_ge(ctx_done, quads * (s - 1))
                    elif s == 1:
                        pe.wait_ge(max_lo_done, quads * s)
                    else:
                        pe.wait_ge(v_copied, 1)
                    project(s + 1, 0)
                elif c == 3 and s + 1 < groups:
                    pe.wait_ge(dense_lo_done, 2 * (s + 1) + 1)
                    project(s + 1, 1)
                elif c == 4 and s < groups:
                    if s + 1 < groups:
                        pe.wait_ge(dense_lo_done, 2 * (s + 1) + 2)
                    else:
                        pe.wait_ge(ctx_done, quads * (s - 1))
                    transpose_max(s, 0)
                elif c == 5 and s >= 1:
                    if s < groups:
                        pe.wait_ge(max_lo_done, quads * s + 1)
                    else:
                        pe.wait_ge(ctx_done, quads * (s - 1))
                    transpose_context(quads * (s - 1))
                elif c == 6 and s + 1 < groups:
                    if s >= 1:
                        pe.wait_ge(ctx_done, quads * (s - 1) + 1)
                    else:
                        pe.wait_ge(max_lo_done, 1)
                    project_values(s + 1)

            pe.wait_ge(w_lo_ready, 1)
            pe.wait_ge(w_hi_ready, 1)
            project(0, 0)
            pe.wait_ge(dense_lo_done, 1)
            project(0, 1)
            pe.wait_ge(dense_lo_done, 2)
            project_values(0)
            for s in range(groups + 1):
                for c in range(chunks):
                    n = (s - 1) * chunks + c
                    j = c * max_per_chunk
                    for half in range(2):
                        if s >= 1:
                            probs_chunk(s - 1, c, half)
                        if s < groups:
                            max_scores(s, j + half)
                    if n >= 1:
                        context(n - 1)
                    if s < groups:
                        max_scores(s, j + 2)
                    errand(s, c)
                    if s < groups:
                        max_scores(s, j + 3)
            context(groups * chunks - 1)
            pe.wait_ge(ctx_done, quads * groups - 1)
            transpose_context(quads * groups - 1)

        @block.scalar
        def _(act):
            act.wait_ge(w_loaded, 16)
            act.activation(w_hi[:], w_raw[:], ACT.Copy).then_inc(w_hi_ready, 1)

            def split_projection(g, w):
                i = g % 2
                act.wait_ge(proj_done, 2 * g + w + 1)
                if g >= 2 and w == 0:
                    for quad in range(quads):
                        act.wait_ge(stacked[i][quad], 6 * 16 * (g // 2))
                act.activation(dense_hi[:, i, w, :], misc[:], ACT.Copy).then_inc(dense_hi_done, 1)

            def copy_values(g):
                act.wait_ge(v_done, g + 1)
                if g == 0:
                    act.wait_ge(constants, 11)
                if g >= 3:
                    act.wait_ge(pv_done, (g - 2) * chunks)
                act.activation(v_tok[g % 3][:, :, :, 0:HN], misc[:].rearrange("p (t h e) -> p t h e", t=TPB, h=HPG),
                               ACT.Copy).then_inc(v_copied, 1)

            def exponentials(n):
                for half in range(2):
                    act.wait_ge(scores_t_done, 2 * n + half + 1)
                    if n >= 2:
                        act.wait_ge(pv_done, n - 1)
                    act.activation(probs[:, n % 2, 2 * half:2 * half + 2, :], scores_t[half][:], ACT.Exp,
                                   scale=SOFT_SCALE).then_inc(probs_done, 1)

            def copy_context(q):
                act.wait_ge(pv_done, (q + 1) * TPB)
                if q >= 2:
                    act.wait_ge(ctx_t_done, q - 1)
                act.activation(ctx_t[:, q % 2, :], ctx_acc[:], ACT.Copy).then_inc(ctx_copied, 1)

            def split_max(g, quad):
                act.wait_ge(max_t_done, quads * g + quad + 1)
                if g >= 1:
                    act.wait_ge(max_rows[quad], 32 * g)
                act.activation(max_hi[:, quad, :], misc[0:tiles_per_quad, 0:P], ACT.Copy).then_inc(max_hi_done, 1)

            for w in range(2):
                split_projection(0, w)
            copy_values(0)
            for s in range(groups + 1):
                for c in range(chunks):
                    if s >= 1:
                        exponentials((s - 1) * chunks + c)
                    if c == 0 and s >= 2:
                        copy_context(quads * (s - 1) - 1)
                    if c == 0 and s >= 1:
                        split_max(s - 1, 1)
                    if c in (2, 3) and s + 1 < groups:
                        split_projection(s + 1, c - 2)
                    if c == 4 and s >= 1:
                        copy_context(quads * (s - 1))
                    if c == 4 and s < groups:
                        split_max(s, 0)
                    if c == 6 and s + 1 < groups:
                        copy_values(s + 1)
            copy_context(groups * quads - 1)

        @block.vector
        def _(dve):
            dve.wait_ge(w_hi_ready, 1)
            dve.tensor_tensor(w_lo[:], w_raw[:], f32(w_hi[:]), ALU.subtract).then_inc(w_lo_ready, 1)

            def split_projection(g, w):
                i = g % 2
                dve.wait_ge(dense_hi_done, 2 * g + w + 1)
                dve.tensor_tensor(dense_lo[:, i, w, :], misc[:], f32(dense_hi[:, i, w, :]),
                                  ALU.subtract).then_inc(dense_lo_done, 1)

            def negated_max(g, j):
                n = g * tiles_per_group + j
                dve.wait_ge(scores_done, n + 1)
                if j == 0 and g >= 2:
                    dve.wait_ge(max_t_done, quads * (g - 1))
                dve.tensor_reduce(neg_max[:, g % 2, j:j + 1], scores[n % 2][:], AX.X, ALU.max,
                                  negate=True).then_inc(max_done, 1)

            def split_max(g, quad):
                dve.wait_ge(max_hi_done, quads * g + quad + 1)
                dve.tensor_tensor(max_lo[:, quad, :], misc[0:tiles_per_quad, 0:P], f32(max_hi[:, quad, :]),
                                  ALU.subtract).then_inc(max_lo_done, 1)

            def normalise(q):
                dve.wait_ge(ctx_t_done, q + 1)
                view = misc[:].rearrange("p (t h e) -> p h t e", t=TPB, h=4)
                dve.reciprocal(rden[:, q % 2, :, :], view[:, :, :, HN]).then_inc(rden_done, 1)
                dve.wait_ge(rden_done, q + 1)
                dve.tensor_tensor(ctx_tok[:, :, :, q * HN:(q + 1) * HN], view[:, :, :, 0:HN],
                                  rden[:, q % 2, :, :].unsqueeze(3).to_broadcast([P, 4, TPB, HN]),
                                  ALU.mult).then_inc(ctx_done, 1)

            for w in range(2):
                split_projection(0, w)
            for s in range(groups + 1):
                for c in range(chunks):
                    if s < groups:
                        for j in range(c * max_per_chunk, (c + 1) * max_per_chunk):
                            negated_max(s, j)
                    if c == 0 and s >= 1:
                        split_max(s - 1, 1)
                    if c == 1 and s >= 2:
                        normalise(quads * (s - 1) - 1)
                    if c in (2, 3) and s + 1 < groups:
                        split_projection(s + 1, c - 2)
                    if c == 4 and s < groups:
                        split_max(s, 0)
                    if c == 5 and s >= 1:
                        normalise(quads * (s - 1))
            normalise(groups * quads - 1)


def project_context(nc, semaphore, w_proj, b_proj, ctx_tok, ident, x_tok):
    with ExitStack() as ctx:
        def sem(name):
            return semaphore(name)

        w = ctx.enter_context(nc.sbuf_tensor("p_w", [P, KD, D], F32))
        bias = ctx.enter_context(nc.sbuf_tensor("p_bias", [1, D], F32))
        ones = ctx.enter_context(nc.sbuf_tensor("p_ones", [1, P], F32))
        ctx_t = ctx.enter_context(nc.sbuf_tensor("p_ctx_t", [P, 2, KD, SEQ], F32))
        turned = [[ctx.enter_context(nc.psum_tensor(f"p_turned{i}{k}", [P, SEQ], F32)) for k in range(KD)]
                  for i in range(2)]
        acc = [ctx.enter_context(nc.psum_tensor(f"p_acc{i}", [P, 2, D], F32)) for i in range(2)]
        w_loaded, ones_set, turned_done, copied_act, copied_dve, acc_done, added = (
            sem(s) for s in ("p_w_loaded", "p_ones_set", "p_turned_done", "p_copied_act", "p_copied_dve",
                             "p_acc_done", "p_added"))
        block = ctx.enter_context(nc.Block())

        @block.sync
        def _(sp):
            sp.dma_start(w[:], w_proj).then_inc(w_loaded, 16)
            sp.dma_start(bias[:], b_proj).then_inc(w_loaded, 16)

        @block.gpsimd
        def _(pool):
            pool.memset(ones[:], 1.0).then_inc(ones_set, 1)

        @block.tensor
        def _(pe):
            def turn(b):
                if b >= 2:
                    pe.wait_ge(copied_act, b - 1)
                    pe.wait_ge(copied_dve, b - 1)
                for k in range(KD):
                    for t in range(TPB):
                        last = pe.transpose(turned[b % 2][k][:, t * P:(t + 1) * P],
                                            ctx_tok[:, b, t, k * P:(k + 1) * P], ident[:])
                last.then_inc(turned_done, 1)

            turn(0)
            for b in range(NB):
                if b + 1 < NB:
                    turn(b + 1)
                if b == 0:
                    pe.wait_ge(w_loaded, 32)
                    pe.wait_ge(ones_set, 1)
                pe.wait_ge(copied_act, b + 1)
                pe.wait_ge(copied_dve, b + 1)
                for half in range(2):
                    n = 2 * b + half
                    if n >= 2:
                        pe.wait_ge(added, n - 1)
                    for e in range(2):
                        t = half * 2 + e
                        for k in range(KD):
                            pe.matmul(acc[half][:, e, :], ctx_t[:, b % 2, k, t * P:(t + 1) * P], w[:, k, :],
                                      start=(k == 0), stop=False)
                        last = pe.matmul(acc[half][:, e, :], ones[:], bias[:], start=False, stop=True)
                    last.then_inc(acc_done, 1)

        @block.scalar
        def _(act):
            for b in range(NB):
                act.wait_ge(turned_done, b + 1)
                if b >= 2:
                    act.wait_ge(acc_done, 2 * (b - 1))
                act.activation(ctx_t[:, b % 2, 0, :], turned[b % 2][0][:], ACT.Copy).then_inc(copied_act, 1)

        @block.vector
        def _(dve):
            def copy(b):
                dve.wait_ge(turned_done, b + 1)
                if b >= 2:
                    dve.wait_ge(acc_done, 2 * (b - 1))
                dve.tensor_copy(ctx_t[:, b % 2, 1, :], turned[b % 2][1][:]).then_inc(copied_dve, 1)

            copy(0)
            for b in range(NB):
                if b + 1 < NB:
                    copy(b + 1)
                for half in range(2):
                    dve.wait_ge(acc_done, 2 * b + half + 1)
                    t = b * TPB + half * 2
                    dve.tensor_tensor(x_tok[:, t:t + 2, :], acc[half][:], x_tok[:, t:t + 2, :],
                                      ALU.add).then_inc(added, 1)


def routed_ffn(nc, semaphore, tag, w_in, w_mid, w_out, xn_hi, xn_lo, ident, x_tok):
    with ExitStack() as ctx:
        def sb(name, shape, dt=F32):
            return ctx.enter_context(nc.sbuf_tensor(f"f_{name}_{tag}", shape, dt))

        def psum(name, shape):
            return ctx.enter_context(nc.psum_tensor(f"f_{name}_{tag}", shape, F32))

        def sem(name):
            return semaphore(f"f_{name}_{tag}")

        w_in_raw = sb("w_in_raw", [P, KD, D + NE])
        w_in_hi = sb("w_in_hi", [P, KD, D + NE], F32R)
        w_in_lo = sb("w_in_lo", [P, KD, D + NE], F32R)
        w3 = sb("w3", [P, KD, D])
        w2 = sb("w2", [P, KD, D])
        hidden_t = sb("hidden_t", [P, KD, NB * SEQ])
        hidden = sb("hidden", [P, 2, 2, D])
        rank = sb("rank", [P, NE])
        logits = sb("logits", [P, NT, NE])
        masked = sb("masked", [P, NT, NE])
        same = sb("same", [P, NT, NE])
        ranked = sb("ranked", [P, NT, NE])
        top = sb("top", [P, 2, NT])
        first = sb("first", [P, 2, NT])
        chosen = sb("chosen", [P, 2, NT, NE])
        gap = sb("gap", [P, NT])
        ratio = sb("ratio", [P, NT])
        total = sb("total", [P, NT])
        weight = sb("weight", [P, 2, NT])
        gates = sb("gates", [P, 3, NT, NE])
        summed = sb("summed", [NE, D])
        summed_t = sb("summed_t", [P, KD, NE])
        logits_ps = psum("logits_ps", [P, NT, NE])
        up = [psum(f"up{i}", [P, SEQ]) for i in range(2)]
        mid = [psum(f"mid{i}", [P, 2, D]) for i in range(2)]
        acc = psum("acc", [NE, D])
        tail = psum("tail", [P, KD, NE])
        rows = psum("rows", [NE, D])

        names = ("w_in_loaded", "w3_loaded", "w2_loaded", "rank_set", "w_hi_ready", "w_lo_ready", "logits_done", "route", "gap_ready",
                 "ratio_ready", "gates_ready", "up_done", "up_read", "mid_done", "mid_read", "acc_done",
                 "hidden_used", "summed_ready", "tail_done", "tail_read", "rows_done", "rows_added")
        (w_in_loaded, w3_loaded, w2_loaded, rank_set, w_hi_ready, w_lo_ready, logits_done, route, gap_ready,
         ratio_ready, gates_ready, up_done, up_read, mid_done, mid_read, acc_done,
         hidden_used, summed_ready, tail_done, tail_read, rows_done, rows_added) = (sem(n) for n in names)
        block = ctx.enter_context(nc.Block())

        @block.sync
        def _(sp):
            sp.dma_start(w_in_raw[:], w_in).then_inc(w_in_loaded, 16)
            sp.dma_start(w3[:], w_mid).then_inc(w3_loaded, 16)
            sp.dma_start(w2[:], w_out).then_inc(w2_loaded, 16)

        @block.gpsimd
        def _(pool):
            for e in range(NE):
                pool.memset(rank[:, e:e + 1], float(NE - e)).then_inc(rank_set, 1)

        @block.tensor
        def _(pe):
            pe.wait_ge(w_hi_ready, 1)
            pe.wait_ge(w_lo_ready, 1)
            for n in range(NT):
                tok, j = slice(n * P, (n + 1) * P), 0
                for k in range(KD):
                    for lhs, rhs in split_passes(xn_hi[:, k, tok], xn_lo[:, k, tok],
                                                 w_in_hi[:, k, D:], w_in_lo[:, k, D:]):
                        last = pe.matmul(logits_ps[:, n, :], lhs, rhs, start=(j == 0), stop=(j == 3 * KD - 1))
                        j += 1
            last.then_inc(logits_done, 1)

            for n in range(KD * NB):
                b, m, j = n // KD, n % KD, 0
                tok, ch = slice(b * SEQ, (b + 1) * SEQ), slice(m * P, (m + 1) * P)
                if n >= 2:
                    pe.wait_ge(up_read, n - 1)
                for k in range(KD):
                    for lhs, rhs in split_passes(w_in_hi[:, k, ch], w_in_lo[:, k, ch],
                                                 xn_hi[:, k, tok], xn_lo[:, k, tok]):
                        last = pe.matmul(up[n % 2][:], lhs, rhs, start=(j == 0), stop=(j == 3 * KD - 1))
                        j += 1
                last.then_inc(up_done, 1)

            pe.wait_ge(w3_loaded, 16)

            def middle(n):
                pe.wait_ge(up_read, KD * (n * 2 // TPB + 1))
                if n >= 2:
                    pe.wait_ge(mid_read, n - 1)
                for e in range(2):
                    t = 2 * n + e
                    for k in range(KD):
                        last = pe.matmul(mid[n % 2][:, e, :], hidden_t[:, k, t * P:(t + 1) * P], w3[:, k, :],
                                         start=(k == 0), stop=(k == KD - 1))
                last.then_inc(mid_done, 1)

            def gather(n):
                pe.wait_ge(mid_read, n + 1)
                if n == 0:
                    pe.wait_ge(gates_ready, 1)
                for e in range(2):
                    t = 2 * n + e
                    last = pe.matmul(acc[:], gates[:, 2, t, :], hidden[:, n % 2, e, :], start=(t == 0), stop=(t == NT - 1))
                last.then_inc(acc_done, 1)

            middle(0)
            for n in range(NT // 2):
                if n + 1 < NT // 2:
                    middle(n + 1)
                gather(n)
            pe.wait_ge(summed_ready, 1)
            for k in range(KD):
                last = pe.transpose(tail[:, k, :], summed[:, k * P:(k + 1) * P], ident[0:NE, 0:NE])
            last.then_inc(tail_done, 1)
            pe.wait_ge(tail_read, 1)
            pe.wait_ge(w2_loaded, 16)
            for k in range(KD):
                last = pe.matmul(rows[:], summed_t[:, k, :], w2[:, k, :], start=(k == 0), stop=(k == KD - 1))
            last.then_inc(rows_done, 1)

        @block.scalar
        def _(act):
            act.wait_ge(w_in_loaded, 16)
            act.activation(w_in_hi[:], w_in_raw[:], ACT.Copy).then_inc(w_hi_ready, 1)
            act.wait_ge(gap_ready, 1)
            act.activation(ratio[:], gap[:], ACT.Exp).then_inc(ratio_ready, 1)
            for n in range(KD * NB):
                b, m = n // KD, n % KD
                act.wait_ge(up_done, n + 1)
                act.activation(hidden_t[:, m, b * SEQ:(b + 1) * SEQ], up[n % 2][:], ACT.Silu).then_inc(up_read, 1)
            for n in range(NT // 2):
                act.wait_ge(mid_done, n + 1)
                if n >= 2:
                    act.wait_ge(acc_done, n - 1)
                act.activation(hidden[:, n % 2, :, :], mid[n % 2][:], ACT.Silu).then_inc(mid_read, 1)

        @block.vector
        def _(dve):
            dve.wait_ge(w_hi_ready, 1)
            dve.tensor_tensor(w_in_lo[:], w_in_raw[:], f32(w_in_hi[:]), ALU.subtract).then_inc(w_lo_ready, 1)
            dve.wait_ge(logits_done, 1)
            dve.wait_ge(rank_set, NE)
            dve.tensor_copy(logits[:], logits_ps[:]).then_inc(route, 1)
            step = 1
            wide = [P, NT, NE]
            for pick in range(2):
                src = logits if pick == 0 else masked
                dve.wait_ge(route, step)
                dve.tensor_reduce(top[:, pick, :], src[:], AX.X, ALU.max).then_inc(route, 1)
                dve.wait_ge(route, step + 1)
                dve.tensor_tensor(same[:], src[:], top[:, pick, :].unsqueeze(2).to_broadcast(wide),
                                  ALU.is_equal).then_inc(route, 1)
                dve.wait_ge(route, step + 2)
                dve.tensor_tensor(ranked[:], same[:], rank[:].unsqueeze(1).to_broadcast(wide),
                                  ALU.mult).then_inc(route, 1)
                dve.wait_ge(route, step + 3)
                dve.tensor_reduce(first[:, pick, :], ranked[:], AX.X, ALU.max).then_inc(route, 1)
                dve.wait_ge(route, step + 4)
                dve.tensor_tensor(chosen[:, pick, :, :], ranked[:], first[:, pick, :].unsqueeze(2).to_broadcast(wide),
                                  ALU.is_equal).then_inc(route, 1)
                step += 5
                if pick == 0:
                    dve.wait_ge(route, step)
                    dve.scalar_tensor_tensor(masked[:], chosen[:, 0, :, :], -3.0e38, logits[:],
                                             ALU.mult, ALU.add).then_inc(route, 1)
                    step += 1
            dve.wait_ge(route, step)
            dve.tensor_tensor(gap[:], top[:, 1, :], top[:, 0, :], ALU.subtract).then_inc(gap_ready, 1)
            dve.wait_ge(ratio_ready, 1)
            dve.tensor_scalar(total[:], ratio[:], 1.0, None, ALU.add).then_inc(route, 1)
            dve.wait_ge(route, step + 1)
            dve.reciprocal(weight[:, 0, :], total[:]).then_inc(route, 1)
            dve.wait_ge(route, step + 2)
            dve.tensor_tensor(weight[:, 1, :], ratio[:], weight[:, 0, :], ALU.mult).then_inc(route, 1)
            dve.wait_ge(route, step + 3)
            for pick in range(2):
                dve.tensor_tensor(gates[:, pick, :, :], chosen[:, pick, :, :],
                                  weight[:, pick, :].unsqueeze(2).to_broadcast(wide), ALU.mult).then_inc(route, 1)
            dve.wait_ge(route, step + 5)
            dve.tensor_tensor(gates[:, 2, :, :], gates[:, 0, :, :], gates[:, 1, :, :], ALU.add).then_inc(gates_ready, 1)
            dve.wait_ge(acc_done, NT // 2)
            dve.tensor_copy(summed[:], acc[:]).then_inc(summed_ready, 1)
            dve.wait_ge(tail_done, 1)
            dve.tensor_copy(summed_t[:], tail[:]).then_inc(tail_read, 1)
            dve.wait_ge(rows_done, 1)
            dve.tensor_tensor(x_tok[0:NE, 0, :], rows[:], x_tok[0:NE, 0, :], ALU.add).then_inc(rows_added, 1)


def decay_gates(nc, semaphore, w_beta, b_beta, xn_hi, xn_lo, ident, beta_tok, keep_rows):
    with ExitStack() as ctx:
        def sb(name, shape, dt=F32):
            return ctx.enter_context(nc.sbuf_tensor(f"d_{name}", shape, dt))

        def sem(name):
            return semaphore(f"d_{name}")

        w_raw = sb("w_raw", [P, KD, LH])
        w_hi = sb("w_hi", [P, KD, LH], F32R)
        w_lo = sb("w_lo", [P, KD, LH], F32R)
        bias = sb("bias", [1, LH])
        ones = sb("ones", [1, P])
        keep = sb("keep", [P, NT, LH])
        keep_t = sb("keep_t", [P, 2, P])
        z = ctx.enter_context(nc.psum_tensor("d_z", [P, NT, LH], F32))
        turned = ctx.enter_context(nc.psum_tensor("d_turned", [P, 2, P], F32))
        loaded, w_hi_ready, w_lo_ready, ones_set, z_done, beta_done, keep_done, turned_done, copied, written = (
            sem(n) for n in ("loaded", "w_hi_ready", "w_lo_ready", "ones_set", "z_done", "beta_done", "keep_done",
                             "turned_done", "copied", "written"))
        block = ctx.enter_context(nc.Block())

        @block.sync
        def _(sp):
            sp.dma_start(w_raw[:], w_beta).then_inc(loaded, 16)
            sp.dma_start(bias[:], b_beta).then_inc(loaded, 16)
            sp.wait_ge(copied, 1)
            rows = keep_rows.rearrange("h (j t p) -> j t h p", j=2, p=P)
            for j in range(2):
                sp.dma_start(rows[j], keep_t[:, j, :]).then_inc(written, 16)
            sp.wait_ge(written, 32)

        @block.gpsimd
        def _(pool):
            pool.memset(ones[:], 1.0).then_inc(ones_set, 1)

        @block.tensor
        def _(pe):
            pe.wait_ge(w_hi_ready, 1)
            pe.wait_ge(w_lo_ready, 1)
            pe.wait_ge(ones_set, 1)
            for n in range(NT):
                tok, j = slice(n * P, (n + 1) * P), 0
                for k in range(KD):
                    for lhs, rhs in split_passes(xn_hi[:, k, tok], xn_lo[:, k, tok], w_hi[:, k, :], w_lo[:, k, :]):
                        pe.matmul(z[:, n, :], lhs, rhs, start=(j == 0), stop=False)
                        j += 1
                last = pe.matmul(z[:, n, :], ones[:], bias[:], start=False, stop=True)
            last.then_inc(z_done, 1)
            pe.wait_ge(keep_done, 1)
            for j in range(2):
                last = pe.transpose(turned[:, j, :], keep[:, j * (NT // 2):(j + 1) * (NT // 2), :], ident[:])
            last.then_inc(turned_done, 1)

        @block.scalar
        def _(act):
            act.wait_ge(loaded, 32)
            act.activation(w_hi[:], w_raw[:], ACT.Copy).then_inc(w_hi_ready, 1)
            act.wait_ge(z_done, 1)
            act.activation(beta_tok[:], z[:], ACT.Sigmoid).then_inc(beta_done, 1)

        @block.vector
        def _(dve):
            dve.wait_ge(w_hi_ready, 1)
            dve.tensor_tensor(w_lo[:], w_raw[:], f32(w_hi[:]), ALU.subtract).then_inc(w_lo_ready, 1)
            dve.wait_ge(beta_done, 1)
            dve.tensor_scalar(keep[:], beta_tok[:], -1.0, 1.0, ALU.mult, ALU.add).then_inc(keep_done, 1)
            dve.wait_ge(turned_done, 1)
            dve.tensor_copy(keep_t[:], turned[:]).then_inc(copied, 1)


def linear_attention(nc, semaphore, w_heads, w_o, params, norms, xn_hi, xn_lo, ident, beta_tok, keep_rows, x_tok):
    PAIRS, BODY = LH // 2, 2 * NB
    UNITS = PAIRS * BODY
    PAIR = 2 * DK
    NPAR = 2 * (TAPS + 1)
    WIDTH = [SEQ - i * P for i in range(TPB)]
    START = [0, 512, 1024, 896]
    CAUSAL = sum(WIDTH)
    with ExitStack() as ctx:
        def sb(name, shape, dt=F32):
            return ctx.enter_context(nc.sbuf_tensor(f"l_{name}", shape, dt))

        def psum(name, shape=(P, SEQ)):
            return ctx.enter_context(nc.psum_tensor(f"l_{name}", list(shape), F32))

        def sem(name):
            return semaphore(f"l_{name}")

        Q, K, G, V = range(4)
        w_raw = sb("w_raw", [P, KD, 4, PAIR])
        w_hi = sb("w_hi", [P, KD, 4, PAIR], F32R)
        w_lo = sb("w_lo", [P, KD, 4, PAIR], F32R)
        wo = sb("wo", [P, LH, D])
        par = sb("par", [P, LH, NPAR])
        norm = sb("norm", [P, 4])
        minus_half = sb("minus_half", [P, 2 * TPB])
        quarter = sb("quarter", [P, 2 * TPB])
        diag = sb("diag", [P, SEQ])
        keep = sb("keep", [P, 4, SEQ])
        conv = sb("conv", [P, 2, 2, SEQ])
        stats = sb("stats", [P, 2, 2 * TPB, 6])
        small = sb("small", [P, 8, 2 * TPB])
        scale = sb("scale", [P, 2, 2 * TPB])
        shift = sb("shift", [P, 2, 2 * TPB])
        normed = sb("normed", [P, 2, TPB, DK])
        qk = sb("qk", [P, 2, 2, SEQ])
        decay = sb("decay", [P, CAUSAL])
        masked = sb("masked", [P, 2, CAUSAL])
        gate = sb("gate", [P, 4, SEQ])
        values = sb("values", [P, 4, TPB, PAIR])
        gated = sb("gated", [P, 4, SEQ])

        proj_q, proj_k, proj_gv, turn_q, turn_k, score_a, score_b, outp = (psum(n) for n in (
            "proj_q", "proj_k", "proj_gv", "turn_q", "turn_k", "score_a", "score_b", "outp"))
        proj = (proj_q, proj_k)
        turn = (turn_q, turn_k)

        w_loaded, consts_loaded, consts_set, w_hi_done, w_ready = (sem(n) for n in (
            "w_loaded", "consts_loaded", "consts_set", "w_hi_done", "w_ready"))
        keep_loaded = [sem(f"keep_loaded{i}") for i in range(4)]
        q_proj, k_proj, g_proj, v_proj = (sem(n) for n in ("q_proj", "k_proj", "g_proj", "v_proj"))
        q_tap, k_tap, q_step, k_step, q_conv, k_conv = (sem(n) for n in (
            "q_tap", "k_tap", "q_step", "k_step", "q_conv", "k_conv"))
        q_act, k_act, gate_act = (sem(n) for n in ("q_act", "k_act", "gate_act"))
        turned, stats_done, stat_step, scales_ready, norm_done, returned, qk_ready = (
            (sem(f"{n}_q"), sem(f"{n}_k")) for n in (
                "turned", "stats_done", "stat_step", "scales_ready", "norm_done", "returned", "qk_ready"))
        score_a_done, score_b_done, score_c_done = (sem(n) for n in ("score_a_done", "score_b_done", "score_c_done"))
        decay_done, masked_a, masked_b, masked_c = (sem(n) for n in ("decay_done", "masked_a", "masked_b", "masked_c"))
        values_done, read_out, gated_done, out_done, added = (sem(n) for n in (
            "values_done", "read_out", "gated_done", "out_done", "added"))
        proj_sem, tap_sem, step_sem, conv_sem, act_sem = (
            (q_proj, k_proj), (q_tap, k_tap), (q_step, k_step), (q_conv, k_conv), (q_act, k_act))
        block = ctx.enter_context(nc.Block())

        def wait(eng, semaphore, count):
            if not isinstance(count, int) or count > 0:
                eng.wait_ge(semaphore, count)

        def wait_apart(eng, semaphore, count):
            wait(eng, semaphore, count)
            eng.nop(nofuse=True)

        def has(u, lag):
            return not isinstance(u, int) or 0 <= u - lag < UNITS

        def steps(eng, step, lags):
            for k in range(BODY):
                step(0, k, k)
            with eng.Fori(1, PAIRS) as pair:
                for k in range(BODY):
                    step(pair, k, pair * BODY + k)
            for k in range(lags):
                step(PAIRS, k, UNITS + k)

        @block.sync
        def _(sp):
            sp.dma_start(w_raw[:], w_heads[0]).then_inc(w_loaded, 16)
            sp.dma_start(par[:], params).then_inc(consts_loaded, 16)
            sp.dma_start(norm[:], norms).then_inc(consts_loaded, 16)
            sp.dma_start(wo[:], w_o).then_inc(consts_loaded, 16)

            def step(pair, k, u):
                wait(sp, decay_done, u - 3)
                b, e = k // 2, k % 2
                row = keep_rows[bass.ds(2 * pair + e, 1), b * SEQ:(b + 1) * SEQ]
                sp.dma_start(keep[:, k % 4, :], row.to_broadcast([P, SEQ])).then_inc(keep_loaded[k % 4], 16)
                if k == BODY - 1:
                    wait(sp, w_ready, 4 * (pair + 1))
                    nxt = pair + 1
                    if not (isinstance(nxt, int) and nxt >= PAIRS):
                        sp.dma_start(w_raw[:], w_heads[bass.ds(nxt, 1)]).then_inc(w_loaded, 16)

            for k in range(BODY):
                step(0, k, k)
            with sp.Fori(1, PAIRS - 1) as pair:
                for k in range(BODY):
                    step(pair, k, pair * BODY + k)
            for k in range(BODY):
                step(PAIRS - 1, k, (PAIRS - 1) * BODY + k)

        @block.gpsimd
        def _(pool):
            pool.memset(minus_half[:], -0.5).then_inc(consts_set, 1)
            pool.memset(quarter[:], 0.25).then_inc(consts_set, 1)
            pool.memset(diag[:, P:], 0.0).then_inc(consts_set, 1)
            pool.tensor_copy(diag[:, 0:P], ident[:]).then_inc(consts_set, 1)

            def split_weights(pair, part):
                n = 4 * pair + part
                if part == Q:
                    wait(pool, w_loaded, 16 * (pair + 1))
                wait_apart(pool, (q_proj, k_proj, g_proj, v_proj)[part], BODY * pair)
                pool.tensor_scalar(w_hi[:, :, part, :], w_raw[:, :, part, :], 1.0, 0.0, ALU.mult,
                                   ALU.add).then_inc(w_hi_done, 1)
                wait(pool, w_hi_done, n + 1)
                pool.tensor_tensor(w_lo[:, :, part, :], w_raw[:, :, part, :], f32(w_hi[:, :, part, :]),
                                   ALU.subtract).then_inc(w_ready, 1)

            def scales(v, k, w):
                i, tiles = k % 2, slice(w * TPB, (w + 1) * TPB)
                st = stats[:, i, tiles]
                wait(pool, stats_done[w], v + 1)
                wait(pool, norm_done[w], v - 1)
                pool.tensor_tensor(small[:, 1, tiles], st[:, :, 1], st[:, :, 4], ALU.subtract)
                pool.tensor_tensor(small[:, 2, tiles], st[:, :, 2], st[:, :, 5], ALU.add).then_inc(stat_step[w], 1)
                pool.tensor_tensor(small[:, 0, tiles], st[:, :, 1], st[:, :, 4], ALU.add)
                wait(pool, stat_step[w], 4 * v + 1)
                pool.tensor_tensor(small[:, 3, tiles], small[:, 1, tiles], small[:, 1, tiles], ALU.mult)
                pool.tensor_scalar(small[:, 4, tiles], small[:, 2, tiles], 1.0 / DK, EPS, ALU.mult,
                                   ALU.add).then_inc(stat_step[w], 1)
                wait(pool, stat_step[w], 4 * v + 2)
                pool.tensor_tensor(small[:, 6, tiles], small[:, 3, tiles], quarter[:, tiles],
                                   ALU.mult).then_inc(stat_step[w], 1)
                pool.tensor_scalar(small[:, 5, tiles], small[:, 0, tiles], -0.5, 0.0, ALU.mult, ALU.add)
                wait(pool, stat_step[w], 4 * v + 3)
                pool.tensor_tensor(small[:, 7, tiles], small[:, 6, tiles], small[:, 4, tiles],
                                   ALU.add).then_inc(stat_step[w], 1)
                wait(pool, stat_step[w], 4 * v + 4)
                pool.tensor_tensor(scale[:, i, tiles], small[:, 7, tiles], minus_half[:, tiles],
                                   ALU.pow).then_inc(scales_ready[w], 1)
                wait(pool, scales_ready[w], 2 * v + 1)
                pool.tensor_tensor(shift[:, i, tiles], small[:, 5, tiles], scale[:, i, tiles],
                                   ALU.mult).then_inc(scales_ready[w], 1)

            pool.wait_ge(consts_set, 4)
            for part in (Q, K, G):
                split_weights(0, part)

            def step(pair, k, u):
                if has(u, 1):
                    for w in range(2):
                        scales(u - 1, (k - 1) % BODY, w)
                if k == 0 and has(u, 0):
                    split_weights(pair, V)
                if k == BODY - 1 and has(u, 0):
                    nxt = pair + 1
                    for part in (Q, K, G):
                        split_weights(nxt, part)

            for k in range(BODY):
                step(0, k, k)
            with pool.Fori(1, PAIRS - 1) as pair:
                for k in range(BODY):
                    step(pair, k, pair * BODY + k)
            for k in range(BODY):
                u = (PAIRS - 1) * BODY + k
                for w in range(2):
                    scales(u - 1, (k - 1) % BODY, w)
                if k == 0:
                    split_weights(PAIRS - 1, V)
            for w in range(2):
                scales(UNITS - 1, BODY - 1, w)

        @block.tensor
        def _(pe):
            def project(out, part, k):
                b, e = k // 2, k % 2
                tok, ch, j = slice(b * SEQ, (b + 1) * SEQ), slice(e * DK, (e + 1) * DK), 0
                for kd in range(KD):
                    for lhs, rhs in split_passes(w_hi[:, kd, part, ch], w_lo[:, kd, part, ch],
                                                 xn_hi[:, kd, tok], xn_lo[:, kd, tok]):
                        last = pe.matmul(out[:], lhs, rhs, start=(j == 0), stop=(j == 3 * KD - 1))
                        j += 1
                return last

            def project_values(k):
                b, half = k // 2, k % 2
                for t in range(2):
                    n = b * TPB + half * 2 + t
                    tok, j = slice(n * P, (n + 1) * P), 0
                    for kd in range(KD):
                        for lhs, rhs in split_passes(xn_hi[:, kd, tok], xn_lo[:, kd, tok],
                                                     w_hi[:, kd, V, :], w_lo[:, kd, V, :]):
                            last = pe.matmul(proj_gv[:, t * PAIR:(t + 1) * PAIR], lhs, rhs,
                                             start=(j == 0), stop=(j == 3 * KD - 1))
                            j += 1
                return last

            def score(out, at, i, par_):
                return pe.matmul(out[:, at:at + WIDTH[i]], qk[:, 1, par_, i * P:(i + 1) * P],
                                 qk[:, 0, par_, i * P:SEQ], start=True, stop=True)

            def turn_tokens(v, k, w):
                wait(pe, act_sem[w], v + 1)
                wait(pe, qk_ready[w], v)
                for t in range(TPB):
                    last = pe.transpose(turn[w][:, t * P:(t + 1) * P], conv[:, w, k % 2, t * P:(t + 1) * P], ident[:])
                last.then_inc(turned[w], 1)

            def turn_back(v, w):
                wait(pe, norm_done[w], v + 1)
                for t in range(TPB):
                    last = pe.transpose(turn[w][:, t * P:(t + 1) * P], normed[:, w, t, :], ident[:])
                last.then_inc(returned[w], 1)

            def step(pair, k, u):
                if has(u, 1):
                    for w in range(2):
                        turn_tokens(u - 1, (k - 1) % BODY, w)
                if has(u, 2):
                    v, m = u - 2, k % 2
                    for w in range(2):
                        wait(pe, qk_ready[w], v + 1)
                    wait(pe, masked_c, v)
                    score(score_a, 0, 0, m).then_inc(score_a_done, 1)
                    score(score_b, 0, 1, m)
                    score(score_b, WIDTH[1], 3, m).then_inc(score_b_done, 1)
                if has(u, 0):
                    for w in range(2):
                        if k == 0:
                            wait(pe, w_ready, 4 * pair + w + 1)
                        wait(pe, conv_sem[w], u)
                        project(proj[w], w, k).then_inc(proj_sem[w], 1)
                if has(u, 2):
                    v, m = u - 2, k % 2
                    wait(pe, masked_a, v + 1)
                    score(score_a, 0, 2, m).then_inc(score_c_done, 1)
                if has(u, 0):
                    if k == 0:
                        wait(pe, w_ready, 4 * pair + G + 1)
                    wait(pe, values_done, u)
                    project(proj_gv, G, k).then_inc(g_proj, 1)
                if has(u, 1):
                    turn_back(u - 1, 0)
                if has(u, 3):
                    v, kk = u - 3, (k - 3) % BODY
                    m, e, c = kk % 2, kk % 2, kk // 2
                    wait(pe, masked_c, v + 1)
                    wait(pe, values_done, v + 2 - kk % 2)
                    wait(pe, added, v - 1)
                    for i in reversed(range(TPB)):
                        last = pe.matmul(outp[:, i * P:SEQ], values[:, c, i, e * DK:(e + 1) * DK],
                                         masked[:, m, START[i]:START[i] + WIDTH[i]],
                                         start=(i == TPB - 1), stop=(i == 0), skip_group_check=True)
                    last.then_inc(read_out, 1)
                if has(u, 1):
                    turn_back(u - 1, 1)
                if has(u, 0):
                    if k == 0:
                        wait(pe, w_ready, 4 * pair + V + 1)
                    wait(pe, gate_act, u + 1)
                    project_values(k).then_inc(v_proj, 1)
                if has(u, 4):
                    v, kk = u - 4, (k - 4) % BODY
                    w, half = kk // 2, kk % 2
                    wait(pe, gated_done, min(v + 2, UNITS) if isinstance(v, int) else v + 2)
                    wait(pe, added, v)
                    head = 2 * (pair if k >= 4 else pair - 1)
                    for t in range(2):
                        for e in range(2):
                            tok = slice((half * 2 + t) * P, (half * 2 + t + 1) * P)
                            last = pe.matmul(outp[:, t * D:(t + 1) * D], gated[:, (2 * w + e) % 4, tok],
                                             wo[:, head_of(head, e), :], start=(e == 0), stop=(e == 1))
                    last.then_inc(out_done, 1)

            def head_of(head, e):
                return head + e

            pe.wait_ge(consts_loaded, 48)
            steps(pe, step, 5)

        @block.scalar
        def _(act):
            def tap(pair, k, u, w):
                h, m = 2 * pair + k % 2, k % 2
                wait(act, proj_sem[w], u + 1)
                wait_apart(act, turned[w], u - 1)
                act.activation(conv[:, w, m, :], proj[w][:], ACT.Copy,
                               scale=par[:, h, (w + 1) * TAPS - 1:(w + 1) * TAPS]).then_inc(tap_sem[w], 1)

            def silu(pair, k, u, w):
                h, m = 2 * pair + k % 2, k % 2
                wait_apart(act, conv_sem[w], u + 1)
                act.activation(conv[:, w, m, :], conv[:, w, m, :], ACT.Silu,
                               bias=par[:, h, 2 * TAPS + w:2 * TAPS + w + 1]).then_inc(act_sem[w], 1)

            def normalise(v, k, w):
                m = k % 2
                wait(act, scales_ready[w], 2 * v + 2)
                wait(act, returned[w], v)
                for t in range(TPB):
                    j = w * TPB + t
                    last = act.activation(normed[:, w, t, :], turn[w][:, t * P:(t + 1) * P], ACT.Identity,
                                          scale=scale[:, m, j:j + 1], bias=shift[:, m, j:j + 1])
                last.then_inc(norm_done[w], 1)

            def norm_affine(v, k, w):
                m = k % 2
                wait(act, returned[w], v + 1)
                wait(act, score_c_done, v - 1)
                act.activation(qk[:, w, m, :], turn[w][:], ACT.Identity, scale=norm[:, 2 * w:2 * w + 1],
                               bias=norm[:, 2 * w + 1:2 * w + 2]).then_inc(qk_ready[w], 1)

            def step(pair, k, u):
                before = (u - 1, (k - 1) % BODY)
                if has(u, 0):
                    tap(pair, k, u, 0)
                if has(u, 1):
                    normalise(*before, 0)
                if has(u, 0):
                    tap(pair, k, u, 1)
                if has(u, 1):
                    normalise(*before, 1)
                if has(u, 0):
                    wait(act, g_proj, u + 1)
                    wait(act, gated_done, u - 3)
                    act.activation(gate[:, k % 4, :], proj_gv[:], ACT.Silu).then_inc(gate_act, 1)
                    silu(pair, k, u, 0)
                if has(u, 1):
                    norm_affine(*before, 0)
                if has(u, 0):
                    silu(pair, k, u, 1)
                if has(u, 1):
                    norm_affine(*before, 1)

            act.wait_ge(consts_loaded, 48)
            steps(act, step, 1)

        @block.vector
        def _(dve):
            def convolve(pair, k, u, w, s):
                h, m = 2 * pair + k % 2, k % 2
                if s == 1:
                    wait(dve, tap_sem[w], u + 1)
                else:
                    wait(dve, step_sem[w], 2 * u + s - 1)
                tap = w * TAPS + TAPS - 1 - s
                ins = dve.scalar_tensor_tensor(conv[:, w, m, s:], proj[w][:, 0:SEQ - s], par[:, h, tap:tap + 1],
                                               conv[:, w, m, s:], ALU.mult, ALU.add)
                ins.then_inc(conv_sem[w] if s == TAPS - 1 else step_sem[w], 1)

            def mask(score, v, k, at, n):
                return dve.tensor_tensor(masked[:, k % 2, at:at + n], score[:, 0:n], decay[:, at:at + n], ALU.mult)

            def scan(r, tiles):
                for i in tiles:
                    last = dve.tensor_tensor_scan(decay[:, START[i]:START[i] + WIDTH[i]], keep[:, r, i * P:SEQ],
                                                  diag[:, 0:WIDTH[i]], 0.0, ALU.mult, ALU.add)
                return last

            def step(pair, k, u):
                if has(u, 1):
                    v, m = u - 1, (k - 1) % 2
                    for w in range(2):
                        wait(dve, turned[w], v + 1)
                        wait(dve, scales_ready[w], 2 * (v - 1))
                        for t in range(TPB):
                            last = dve.bn_stats(stats[:, m, w * TPB + t, :], turn[w][:, t * P:(t + 1) * P])
                        last.then_inc(stats_done[w], 1)
                if has(u, 2):
                    v = u - 2
                    wait(dve, decay_done, v + 1)
                    wait(dve, read_out, v - 1)
                    wait(dve, score_a_done, v + 1)
                    mask(score_a, v, k, 0, 512).then_inc(masked_a, 1)
                    wait(dve, score_b_done, v + 1)
                    mask(score_b, v, k, 512, 512).then_inc(masked_b, 1)
                if has(u, 0):
                    convolve(pair, k, u, 0, 1)
                if has(u, 2):
                    v = u - 2
                    wait(dve, score_c_done, v + 1)
                    mask(score_a, v, k, 1024, CAUSAL - 1024).then_inc(masked_c, 1)
                if has(u, 0):
                    convolve(pair, k, u, 0, 2)
                    convolve(pair, k, u, 1, 1)
                    convolve(pair, k, u, 0, 3)
                    convolve(pair, k, u, 1, 2)
                if has(u, 1):
                    v, kk = u - 1, (k - 1) % BODY
                    rounds = 2 * (pair if k >= 1 else pair - 1) + kk // 4 + 1
                    wait(dve, keep_loaded[kk % 4], 16 * rounds)
                    wait(dve, masked_c, v)
                    scan(kk % 4, [0])
                if has(u, 0):
                    convolve(pair, k, u, 1, 3)
                if has(u, 3):
                    v, r = u - 3, (k - 3) % 4
                    wait(dve, read_out, v + 1)
                    wait(dve, gate_act, v + 1)
                    wait(dve, out_done, v - 2 - (k - 3) % 2)
                    dve.tensor_tensor(gated[:, r, :], outp[:], gate[:, r, :], ALU.mult).then_inc(gated_done, 1)
                if has(u, 1):
                    scan((k - 1) % 4, [1, 2, 3]).then_inc(decay_done, 1)
                if has(u, 0):
                    b, half = k // 2, k % 2
                    n = b * TPB + 2 * half
                    wait(dve, v_proj, u + 1)
                    wait(dve, read_out, u - half - 6)
                    dve.tensor_tensor(
                        values[:, b, 2 * half:2 * half + 2, :].rearrange("p t (e c) -> p t e c", e=2),
                        proj_gv[:].rearrange("p (t e c) -> p t e c", t=2, e=2),
                        beta_tok[:, n:n + 2, bass.ds(2 * pair, 2)].unsqueeze(3).to_broadcast([P, 2, 2, DK]),
                        ALU.mult).then_inc(values_done, 1)
                if has(u, 4):
                    v, kk = u - 4, (k - 4) % BODY
                    n = (kk // 2) * TPB + 2 * (kk % 2)
                    wait(dve, out_done, v + 1)
                    wait(dve, added, v - 3)
                    dve.tensor_tensor(x_tok[:, n:n + 2, :], outp[:].rearrange("p (t d) -> p t d", t=2),
                                      x_tok[:, n:n + 2, :], ALU.add).then_inc(added, 1)

            dve.wait_ge(consts_loaded, 48)
            dve.wait_ge(consts_set, 4)
            steps(dve, step, 5)


def store(nc, semaphore, x_tok, out):
    with ExitStack() as ctx:
        stored = semaphore("stored")
        block = ctx.enter_context(nc.Block())

        @block.sync
        def _(sp):
            sp.dma_start(out.rearrange("b (t p) d -> p (b t) d", p=P), x_tok[:]).then_inc(stored, 16)
            sp.wait_ge(stored, 16)


def build(nc, x, w_qkv, w_proj, b_proj, w_in, w_mid, w_out, w_beta, b_beta, w_heads, w_o, params, norms, out, stage=9):
    keep_rows = nc.dram_tensor("keep_rows", [LH, NB * SEQ], F32, kind="Internal").ap()
    held = []

    def semaphore(name):
        held.append(nc.alloc_semaphore(name))
        return held[-1]

    with ExitStack() as ctx:
        x_tok = ctx.enter_context(nc.sbuf_tensor("x_tok", [P, NT, D], F32))
        ident = ctx.enter_context(nc.sbuf_tensor("ident", [P, P], F32))
        xn_hi = ctx.enter_context(nc.sbuf_tensor("xn_hi", [P, KD, NB * SEQ], F32R))
        xn_lo = ctx.enter_context(nc.sbuf_tensor("xn_lo", [P, KD, NB * SEQ], F32R))
        setup(nc, semaphore, x, ident, x_tok)
        norm_transpose(nc, semaphore, "a", x_tok, ident, xn_hi, xn_lo, NT, TPB)
        with nc.sbuf_tensor("ctx_tok", [P, NB, TPB, D], F32) as ctx_tok:
            softmax_attention(nc, semaphore, w_qkv, xn_hi, xn_lo, ident, ctx_tok)
            project_context(nc, semaphore, w_proj, b_proj, ctx_tok, ident, x_tok)
        if stage >= 2:
            norm_transpose(nc, semaphore, "b", x_tok, ident, xn_hi, xn_lo, NT, TPB)
            routed_ffn(nc, semaphore, "b", w_in, w_mid, w_out, xn_hi, xn_lo, ident, x_tok)
        nc.clear_and_free_semaphores(held)
        nc.all_engine_barrier()
        held.clear()
        if stage >= 3:
            norm_transpose(nc, semaphore, "c", x_tok, ident, xn_hi, xn_lo, 1, 1)
            with nc.sbuf_tensor("beta_tok", [P, NT, LH], F32) as beta_tok:
                decay_gates(nc, semaphore, w_beta, b_beta, xn_hi, xn_lo, ident, beta_tok, keep_rows)
                linear_attention(nc, semaphore, w_heads, w_o, params, norms, xn_hi, xn_lo, ident, beta_tok, keep_rows, x_tok)
        if stage >= 4:
            norm_transpose(nc, semaphore, "d", x_tok, ident, xn_hi, xn_lo, NT, TPB)
            routed_ffn(nc, semaphore, "d", w_in, w_mid, w_out, xn_hi, xn_lo, ident, x_tok)
        store(nc, semaphore, x_tok, out)


def kernel(**inputs):
    import numpy as np
    import concourse.bacc as bacc
    from concourse.bass_utils import run_bass_kernel_spmd

    def by_channel(a):
        return np.ascontiguousarray(a.reshape(-1, P, a.shape[-1]).transpose(1, 0, 2))

    a = {k: np.asarray(v) for k, v in inputs.items()}
    qkv = a["L0_attn_a_Wqkv"].reshape(NH // 4, 4, 3, HN, D)
    q, k = (qkv[:, :, i].transpose(0, 2, 1, 3).reshape(D, D) for i in range(2))
    v = qkv[:, :, 2].reshape(D, D)
    heads = np.stack([a[f"L0_attn_b_W{n}"].reshape(KD, P, LH // 2, 2 * DK) for n in "qkgv"], axis=3)
    taps = [a[f"L0_attn_b_{n}conv_w"].reshape(LH, DK, TAPS) for n in "qk"]
    biases = [a[f"L0_attn_b_{n}conv_b"].reshape(LH, DK, 1) for n in "qk"]
    arrays = {
        "x": a["L0_attn_a_query"],
        "w_qkv": by_channel(np.concatenate([q, k, v]).T),
        "w_proj": by_channel(a["L0_attn_a_Wproj"].T),
        "b_proj": a["L0_attn_a_bproj"][None],
        "w_in": by_channel(np.concatenate([a["L0_ffn_w1"], a["L0_ffn_wr"]]).T),
        "w_mid": by_channel(a["L0_ffn_w3"].T),
        "w_out": by_channel(a["L0_ffn_w2"].T),
        "w_beta": by_channel(a["L0_attn_b_Wb"]),
        "b_beta": a["L0_attn_b_bb"][None],
        "w_heads": heads.transpose(2, 1, 0, 3, 4),
        "w_o": by_channel(a["L0_attn_b_Wo"]),
        "params": np.concatenate(taps + biases, axis=-1).transpose(1, 0, 2),
        "norms": np.stack([a[f"L0_attn_b_{n}"] for n in ("qn_w", "qn_b", "kn_w", "kn_b")], axis=1),
    }
    arrays = {n: np.ascontiguousarray(v) for n, v in arrays.items()}
    nc = bacc.Bacc("TRN2", target_bir_lowering=False, num_devices=1)
    args = {n: nc.dram_tensor(n, v.shape, mybir.dt.from_np(v.dtype), kind="ExternalInput").ap()
            for n, v in arrays.items()}
    out = nc.dram_tensor("out", (NB, SEQ, D), F32, kind="ExternalOutput").ap()
    build(nc, out=out, **args)
    return run_bass_kernel_spmd(nc, [arrays], core_ids=[0]).results[0]["out"]
```

```python
from contextlib import ExitStack

import concourse.bass as bass
from concourse import mybir

F32 = mybir.dt.float32
F32R = mybir.dt.float32r
ALU = mybir.AluOpType
ACT = mybir.ActivationFunctionType
AX = mybir.AxisListType

P = 128
EPS = 1e-5
NB, SEQ, D = 4, 512, 256
KD = D // P
NT = NB * SEQ // P
TPB = SEQ // P

NH, HN = 16, 16
SLOT = 32
HPG = P // HN
STACK = 3 * HN
SOFT_SCALE = float(HN) ** -0.5

NE = 8

LH, DK, TAPS = 16, 128, 4
HALF = SEQ // 2


def f32(ap):
    return ap.bitcast(F32)


def split_passes(hi_a, lo_a, hi_b, lo_b):
    return ((hi_a, hi_b), (hi_a, lo_b), (lo_a, hi_b))


class Steps:
    pass


def layer_norm(nc, ctx, semaphore, tag, x_tok, ident, xn_hi, xn_lo, xt, tiles, group, xn=None):
    cols, turns = group * P, len(xt)

    def sb(name, shape):
        return ctx.enter_context(nc.sbuf_tensor(f"ln_{name}_{tag}", shape, F32))

    stats = sb("stats", [P, tiles, 6])
    mean_var = sb("mean_var", [P, tiles, 2])
    var_eps = sb("var_eps", [P, tiles])
    rstd = sb("rstd", [P, tiles])
    minus_half = sb("minus_half", [P, group])
    xn = sb("xn", [P, 2, group, D]) if xn is None else xn
    stats_done, aggregated, half_set, eps_added, rstd_ready, normed, transposed, hi_done, lo_done = (
        semaphore(f"ln_{s}_{tag}") for s in ("stats_done", "aggregated", "half_set", "eps_added", "rstd_ready",
                                             "normed", "transposed", "hi_done", "lo_done"))

    def statistics(dve, g):
        for n in range(g * group, (g + 1) * group):
            dve.bn_stats(stats[:, n, :], x_tok[:, n, :]).then_inc(stats_done, 1)
        for n in range(g * group, (g + 1) * group):
            dve.wait_ge(stats_done, n + 1)
            dve.bn_aggr(mean_var[:, n, :], stats[:, n, :]).then_inc(aggregated, 1)

    def constants(pool):
        pool.memset(minus_half[:], -0.5).then_inc(half_set, 1)
        pool.wait_ge(half_set, 1)

    def deviations(pool, g):
        c = slice(g * group, (g + 1) * group)
        pool.wait_ge(aggregated, (g + 1) * group)
        pool.tensor_scalar(var_eps[:, c], mean_var[:, c, 1], EPS, None, ALU.add).then_inc(eps_added, 1)
        pool.wait_ge(eps_added, g + 1)
        pool.tensor_tensor(rstd[:, c], var_eps[:, c], minus_half[:], ALU.pow).then_inc(rstd_ready, 1)

    def normalise(dve, g):
        dve.wait_ge(rstd_ready, g + 1)
        if g >= 2:
            dve.wait_ge(transposed, g - 1)
        for t in range(group):
            n = g * group + t
            dve.tensor_scalar(xn[:, g % 2, t, :], x_tok[:, n, :], mean_var[:, n, 0:1], rstd[:, n:n + 1],
                              ALU.subtract, ALU.mult).then_inc(normed, 1)

    def transpose(pe, g):
        pe.wait_ge(normed, (g + 1) * group)
        if g >= turns:
            pe.wait_ge(lo_done, KD * (g - turns + 1))
        for k in range(KD):
            for t in range(group):
                last = pe.transpose(xt[g % turns][k][:, t * P:(t + 1) * P],
                                    xn[:, g % 2, t, k * P:(k + 1) * P], ident[:])
        last.then_inc(transposed, 1)

    def high_parts(act, g):
        act.wait_ge(transposed, g + 1)
        for k in range(KD):
            act.activation(xn_hi[:, k, g * cols:(g + 1) * cols], xt[g % turns][k][:], ACT.Copy).then_inc(hi_done, 1)

    def low_parts(dve, g):
        for k in range(KD):
            dve.wait_ge(hi_done, g * KD + k + 1)
            c = slice(g * cols, (g + 1) * cols)
            dve.tensor_tensor(xn_lo[:, k, c], xt[g % turns][k][:], f32(xn_hi[:, k, c]),
                              ALU.subtract).then_inc(lo_done, 1)

    steps = Steps()
    steps.statistics, steps.normalise, steps.low_parts, steps.lo_done = statistics, normalise, low_parts, lo_done
    steps.normed = normed
    steps.constants, steps.deviations, steps.transpose, steps.high_parts = constants, deviations, transpose, high_parts
    return steps


def softmax_attention(nc, semaphore, x, w_qkv, loads, bias_rows, x_tok, xn_hi, xn_lo, ident, ctx_tok):
    groups = NB * KD
    tiles_per_group = HPG * TPB
    quads = HPG // 4
    chunks = quads * TPB
    max_per_chunk = tiles_per_group // chunks
    tiles_per_quad = tiles_per_group // quads
    with ExitStack() as ctx:
        def sb(name, shape, dt=F32):
            return ctx.enter_context(nc.sbuf_tensor(name, shape, dt))

        def psum(name, shape):
            return ctx.enter_context(nc.psum_tensor(name, shape, F32))

        def sem(name):
            return semaphore(name)

        w_raw = ctx_tok[:].rearrange("p b t d -> p (b t d)")[:, 0:KD * 3 * D].rearrange("p (k n) -> p k n", k=KD)
        w_hi = sb("a_w_hi", [P, KD, 3 * D], F32R)
        w_lo = sb("a_w_lo", [P, KD, 3 * D], F32R)
        dense_hi = sb("a_dense_hi", [P, 2, 2, SEQ], F32R)
        dense_lo = sb("a_dense_lo", [P, 2, 2, SEQ], F32R)
        q_stack = [sb(f"a_q_stack{i}", [STACK + 2, HPG, SEQ], F32R) for i in range(2)]
        k_stack = [sb(f"a_k_stack{i}", [STACK + 2, HPG, SEQ], F32R) for i in range(2)]
        v_tok = [sb(f"a_v_tok{i}", [P, TPB, HPG, SLOT]) for i in range(4)]
        neg_max = sb("a_neg_max", [P, 2, tiles_per_group])
        max_hi = sb("a_max_hi", [tiles_per_quad, quads, P], F32R)
        max_lo = sb("a_max_lo", [tiles_per_quad, quads, P], F32R)
        probs = sb("a_probs", [P, 2, 4, SEQ])
        ctx_t = sb("a_ctx_t", [P, SEQ])
        rden = sb("a_rden", [P, 2, 4, TPB])

        scores_t = [psum(f"a_scores_t{i}", [P, 2, SEQ]) for i in range(2)]
        scores = [psum(f"a_scores{i}", [P, SEQ]) for i in range(2)]
        ctx_acc = psum("a_ctx_acc", [P, SEQ])
        misc = psum("a_misc", [P, SEQ])

        first_banks = scores
        first_scores = [scores[0][:], scores[1][:]] + [scores_t[i][:, e, :] for i in range(2) for e in range(2)]

        def max_bank(g, j):
            return first_scores[j % len(first_scores)] if g == 0 else scores[j % 2][:]

        def copied(g):
            return 2 * (g // KD) + 2


        xn = probs[:].rearrange("p i h s -> p (i h s)")[:, 0:2 * TPB * D].rearrange("p (i t d) -> p i t d", i=2, t=TPB)
        xt = [[scores_t[i][:, k, :] for k in range(KD)] for i in range(2)]
        ln = layer_norm(nc, ctx, semaphore, "a", x_tok, ident, xn_hi, xn_lo, xt, NT, TPB, xn)
        x_loaded = [sem(f"x_loaded{b}") for b in range(NB)]
        w_qkv_loaded, w_loaded, ident_zero, ident_ready, set_up, w_hi_ready, w_lo_ready = (sem(n) for n in (
            "w_qkv_loaded", "w_loaded", "ident_zero", "ident_ready", "set_up", "w_hi_ready", "w_lo_ready"))
        bias_added = sem("a_bias_added")
        proj_done = sem("a_proj_done")
        dense_hi_done = sem("a_dense_hi_done")
        dense_lo_done = sem("a_dense_lo_done")
        stacked = [[sem(f"a_stacked{i}{q}") for q in range(quads)] for i in range(2)]
        v_done = sem("a_v_done")
        v_copied = sem("a_v_copied")
        scores_done = sem("a_scores_done")
        max_done = sem("a_max_done")
        max_t_done = sem("a_max_t_done")
        max_hi_done = sem("a_max_hi_done")
        max_lo_done = sem("a_max_lo_done")
        max_rows = [sem(f"a_max_rows{q}") for q in range(quads)]
        scores_t_done = sem("a_scores_t_done")
        probs_done = sem("a_probs_done")
        pv_done = sem("a_pv_done")
        ctx_copied = sem("a_ctx_copied")
        ctx_t_done = sem("a_ctx_t_done")
        rden_done = sem("a_rden_done")
        ctx_done = sem("a_ctx_done")
        block = ctx.enter_context(nc.Block())

        @block.sync
        def _(sp):
            for b in range(NB):
                sp.dma_start(x_tok[:, b * TPB:(b + 1) * TPB, :],
                             x[b].rearrange("(t p) d -> p t d", p=P)).then_inc(x_loaded[b], 16)
                if b == 0:
                    sp.dma_start(w_raw, w_qkv).then_inc(w_qkv_loaded, 16)
            for dst, src in loads:
                sp.dma_start(dst, src).then_inc(w_loaded, 16)
            sp.wait_ge(w_loaded, 16 * len(loads))
            sp.wait_ge(set_up, 2)

            def stack(g, quad):
                i, hs = g % 2, slice(quad * 4, quad * 4 + 4)
                rows = slice(quad * 4 * HN, (quad + 1) * 4 * HN)
                sp.wait_ge(dense_hi_done, 2 * g + 2)
                sp.wait_ge(dense_lo_done, 2 * g + 2)
                if g >= 2:
                    sp.wait_ge(scores_t_done, 2 * ((g - 2) * chunks + (quad + 1) * TPB))
                for dst, w, parts in ((q_stack[i], 0, (dense_hi, dense_lo, dense_hi)),
                                      (k_stack[i], 1, (dense_hi, dense_hi, dense_lo))):
                    for r, src in enumerate(parts):
                        sp.dma_start(f32(dst[r * HN:(r + 1) * HN, hs, :]),
                                     f32(src[rows, i, w, :])).then_inc(stacked[i][quad], 16)

            def rows(g, quad):
                i, hs = g % 2, slice(quad * 4, quad * 4 + 4)
                for r, src, done in ((STACK, max_hi, max_hi_done), (STACK + 1, max_lo, max_lo_done)):
                    sp.wait_ge(done, quads * g + quad + 1)
                    sp.dma_start(f32(q_stack[i][r:r + 1, hs, :]), f32(src[:, quad, :])).then_inc(max_rows[quad], 16)

            stack(0, 0)
            stack(0, 1)
            for s in range(groups + 1):
                if s >= 1:
                    rows(s - 1, 1)
                if s + 1 < groups:
                    stack(s + 1, 0)
                if s < groups:
                    rows(s, 0)
                if s + 1 < groups:
                    stack(s + 1, 1)

        @block.gpsimd
        def _(pool):
            pool.memset(ident[:], 0.0).then_inc(ident_zero, 1)
            pool.wait_ge(ident_zero, 1)
            pool.affine_select(out=ident[:], in_=ident[:], compare_op=ALU.not_equal, fill=1.0, base=0,
                               pattern=[[-1, P]], channel_multiplier=1).then_inc(ident_ready, 1)
            ln.constants(pool)
            for i in range(2):
                pool.memset(f32(k_stack[i][:]), 1.0).then_inc(set_up, 1)
            for g in range(NB):
                ln.deviations(pool, g)
                pool.memset(v_tok[g][:, :, :, HN:HN + 1], 1.0).then_inc(set_up, 1)
                pool.memset(v_tok[g][:, :, :, HN + 1:SLOT], 0.0).then_inc(set_up, 1)
            pool.wait_ge(ln.normed, NT)
            pool.wait_ge(w_loaded, 16 * len(loads))
            pool.tensor_tensor(x_tok[:], x_tok[:], bias_rows[:].unsqueeze(1).to_broadcast([P, NT, D]),
                               ALU.add).then_inc(bias_added, 1)

        @block.tensor
        def _(pe):
            def project(g, w):
                bank = first_banks[w] if g == 0 else misc
                b, m = g // KD, g % KD
                tok, ch, n = slice(b * SEQ, (b + 1) * SEQ), slice(w * D + m * P, w * D + (m + 1) * P), 0
                for k in range(KD):
                    for lhs, rhs in split_passes(w_hi[:, k, ch], w_lo[:, k, ch], xn_hi[:, k, tok], xn_lo[:, k, tok]):
                        last = pe.matmul(bank[:], lhs, rhs, start=(n == 0), stop=(n == 3 * KD - 1))
                        n += 1
                last.then_inc(proj_done, 1)

            def project_values(b, pair):
                ch = slice(2 * D, 3 * D)
                for e in range(2):
                    t = 2 * pair + e
                    tok = slice(b * SEQ + t * P, b * SEQ + (t + 1) * P)
                    n = 0
                    for k in range(KD):
                        for lhs, rhs in split_passes(xn_hi[:, k, tok], xn_lo[:, k, tok], w_hi[:, k, ch], w_lo[:, k, ch]):
                            last = pe.matmul(misc[:, e * D:(e + 1) * D], lhs, rhs, start=(n == 0), stop=(n == 3 * KD - 1))
                            n += 1
                last.then_inc(v_done, 1)

            def transpose_max(g, quad):
                pe.wait_ge(max_done, g * tiles_per_group + (quad + 1) * tiles_per_quad)
                js = slice(quad * tiles_per_quad, (quad + 1) * tiles_per_quad)
                pe.transpose(misc[0:tiles_per_quad, 0:P], neg_max[:, g % 2, js], ident[:]).then_inc(max_t_done, 1)

            def transpose_context(q):
                pe.wait_ge(ctx_copied, q + 1)
                for t in range(TPB):
                    last = pe.transpose(misc[:, t * P:(t + 1) * P], ctx_t[:, t * P:(t + 1) * P], ident[:])
                last.then_inc(ctx_t_done, 1)

            def max_scores(g, j):
                h, t, i = j // TPB, j % TPB, g % 2
                n = g * tiles_per_group + j
                if n == 0:
                    pe.wait_ge(dense_lo_done, 2)
                if j % tiles_per_quad == 0:
                    pe.wait_ge(stacked[i][j // tiles_per_quad], 6 * 16 * (g // 2 + 1))
                turns = len(first_scores) if g == 0 else 2
                if n >= turns:
                    pe.wait_ge(max_done, n - turns + 1)
                pe.matmul(max_bank(g, j), q_stack[i][0:STACK, h, t * P:(t + 1) * P], k_stack[i][0:STACK, h, :],
                          start=True, stop=True).then_inc(scores_done, 1)

            def probs_chunk(g, c, half):
                quad, t, i = c // TPB, c % TPB, g % 2
                n = g * chunks + c
                if t == 0 and half == 0:
                    pe.wait_ge(max_rows[quad], 32 * (g + 1))
                if n == 0:
                    pe.wait_ge(max_done, tiles_per_group)
                if n >= 1:
                    pe.wait_ge(probs_done, 2 * (n - 1) + half + 1)
                for e in range(2):
                    h = quad * 4 + half * 2 + e
                    last = pe.matmul(scores_t[half][:, e, :], k_stack[i][:, h, t * P:(t + 1) * P],
                                     q_stack[i][:, h, :], start=True, stop=True)
                last.then_inc(scores_t_done, 1)

            def context(n):
                g, c = n // chunks, n % chunks
                quad, t = c // TPB, c % TPB
                pe.wait_ge(probs_done, 2 * n + 2)
                if t == 0:
                    if n >= TPB:
                        pe.wait_ge(ctx_copied, n // TPB)
                    pe.wait_ge(v_copied, copied(g))
                    if n == 0:
                        pe.wait_ge(set_up, 2 + 2 * len(v_tok))
                for e in range(4):
                    last = pe.matmul(ctx_acc[e * SLOT:(e + 1) * SLOT, :], v_tok[g % 4][:, t, quad * 4 + e, :],
                                     probs[:, n % 2, e, :], start=(t == 0), stop=(t == TPB - 1))
                last.then_inc(pv_done, 1)

            def errand(s, c):
                if c == 0 and s >= 1:
                    if s % KD == 0 and s < groups:
                        pe.wait_ge(v_copied, copied(s))
                    elif s == 1:
                        pe.wait_ge(max_lo_done, 1)
                    else:
                        pe.wait_ge(ctx_done, quads * (s - 2) + 1)
                    transpose_max(s - 1, 1)
                elif c == 1 and s >= 2:
                    pe.wait_ge(max_lo_done, quads * s)
                    transpose_context(quads * (s - 1) - 1)
                elif c == 2 and s + 1 < groups:
                    if s >= 2:
                        pe.wait_ge(ctx_done, quads * (s - 1))
                    elif s == 1:
                        pe.wait_ge(max_lo_done, quads * s)
                    else:
                        pe.wait_ge(v_copied, 2)
                    project(s + 1, 0)
                elif c == 3 and s + 1 < groups:
                    pe.wait_ge(dense_lo_done, 2 * (s + 1) + 1)
                    project(s + 1, 1)
                elif c == 4 and s < groups:
                    if s + 1 < groups:
                        pe.wait_ge(dense_lo_done, 2 * (s + 1) + 2)
                    else:
                        pe.wait_ge(ctx_done, quads * (s - 1))
                    transpose_max(s, 0)
                elif c == 5 and s >= 1:
                    if s < groups:
                        pe.wait_ge(max_lo_done, quads * s + 1)
                    else:
                        pe.wait_ge(ctx_done, quads * (s - 1))
                    transpose_context(quads * (s - 1))
                elif c == 6 and s + 1 < groups and (s + 1) % KD == 0:
                    pe.wait_ge(ctx_done, quads * (s - 1) + 1)
                    project_values((s + 1) // KD, 0)
                elif c == 7 and s + 1 < groups and (s + 1) % KD == 0:
                    pe.wait_ge(v_copied, copied(s + 1) - 1)
                    project_values((s + 1) // KD, 1)

            pe.wait_ge(ident_ready, 1)
            ln.transpose(pe, 0)
            pe.wait_ge(ln.lo_done, KD)
            pe.wait_ge(w_lo_ready, 1)
            project(0, 0)
            project(0, 1)
            ln.transpose(pe, 1)
            project_values(0, 0)
            ln.transpose(pe, 2)
            ln.transpose(pe, 3)
            pe.wait_ge(v_copied, 1)
            project_values(0, 1)
            pe.wait_ge(ln.lo_done, KD * NB)
            for s in range(groups + 1):
                for c in range(chunks):
                    n = (s - 1) * chunks + c
                    j = c * max_per_chunk
                    for half in range(2):
                        if s >= 1:
                            probs_chunk(s - 1, c, half)
                        if s < groups:
                            max_scores(s, j + half)
                    if n >= 1:
                        context(n - 1)
                    if s < groups:
                        max_scores(s, j + 2)
                    errand(s, c)
                    if s < groups:
                        max_scores(s, j + 3)
            context(groups * chunks - 1)
            pe.wait_ge(ctx_done, quads * groups - 1)
            transpose_context(quads * groups - 1)

        @block.scalar
        def _(act):
            def split_projection(g, w):
                i = g % 2
                act.wait_ge(proj_done, 2 * g + w + 1)
                if g >= 2 and w == 0:
                    for quad in range(quads):
                        act.wait_ge(stacked[i][quad], 6 * 16 * (g // 2))
                bank = first_banks[w] if g == 0 else misc
                act.activation(dense_hi[:, i, w, :], bank[:], ACT.Copy).then_inc(dense_hi_done, 1)

            def copy_values(b, pair):
                act.wait_ge(v_done, 2 * b + pair + 1)
                if b >= 2:
                    act.wait_ge(pv_done, (b - 1) * KD * chunks)
                v = misc[:].rearrange("p (t m h e) -> p t m h e", t=2, m=KD, h=HPG)
                for m in range(KD):
                    last = act.activation(v_tok[(KD * b + m) % 4][:, 2 * pair:2 * pair + 2, :, 0:HN], v[:, :, m, :, :],
                                          ACT.Copy)
                last.then_inc(v_copied, 1)

            def exponentials(n):
                for half in range(2):
                    act.wait_ge(scores_t_done, 2 * n + half + 1)
                    if n >= 2:
                        act.wait_ge(pv_done, n - 1)
                    act.activation(probs[:, n % 2, 2 * half:2 * half + 2, :], scores_t[half][:], ACT.Exp,
                                   scale=SOFT_SCALE).then_inc(probs_done, 1)

            def copy_context(q):
                act.wait_ge(pv_done, (q + 1) * TPB)
                if q >= 1:
                    act.wait_ge(ctx_t_done, q)
                act.activation(ctx_t[:], ctx_acc[:], ACT.Copy).then_inc(ctx_copied, 1)

            def split_max(g, quad):
                act.wait_ge(max_t_done, quads * g + quad + 1)
                if g >= 1:
                    act.wait_ge(max_rows[quad], 32 * g)
                act.activation(max_hi[:, quad, :], misc[0:tiles_per_quad, 0:P], ACT.Copy).then_inc(max_hi_done, 1)

            act.wait_ge(w_qkv_loaded, 16)
            act.activation(w_hi[:], w_raw, ACT.Copy).then_inc(w_hi_ready, 1)
            ln.high_parts(act, 0)
            for w in range(2):
                split_projection(0, w)
            ln.high_parts(act, 1)
            copy_values(0, 0)
            ln.high_parts(act, 2)
            ln.high_parts(act, 3)
            copy_values(0, 1)
            for s in range(groups + 1):
                for c in range(chunks):
                    if s >= 1:
                        exponentials((s - 1) * chunks + c)
                    if c == 0 and s >= 2:
                        copy_context(quads * (s - 1) - 1)
                    if c == 0 and s >= 1:
                        split_max(s - 1, 1)
                    if c in (2, 3) and s + 1 < groups:
                        split_projection(s + 1, c - 2)
                    if c == 4 and s >= 1:
                        copy_context(quads * (s - 1))
                    if c == 4 and s < groups:
                        split_max(s, 0)
                    if c >= 6 and s + 1 < groups and (s + 1) % KD == 0:
                        copy_values((s + 1) // KD, c - 6)
            copy_context(groups * quads - 1)

        @block.vector
        def _(dve):
            def split_projection(g, w):
                i = g % 2
                dve.wait_ge(dense_hi_done, 2 * g + w + 1)
                bank = first_banks[w] if g == 0 else misc
                dve.tensor_tensor(dense_lo[:, i, w, :], bank[:], f32(dense_hi[:, i, w, :]),
                                  ALU.subtract).then_inc(dense_lo_done, 1)

            def negated_max(g, j):
                n = g * tiles_per_group + j
                dve.wait_ge(scores_done, n + 1)
                if j == 0 and g >= 2:
                    dve.wait_ge(max_t_done, quads * (g - 1))
                dve.tensor_reduce(neg_max[:, g % 2, j:j + 1], max_bank(g, j), AX.X, ALU.max,
                                  negate=True).then_inc(max_done, 1)

            def split_max(g, quad):
                dve.wait_ge(max_hi_done, quads * g + quad + 1)
                dve.tensor_tensor(max_lo[:, quad, :], misc[0:tiles_per_quad, 0:P], f32(max_hi[:, quad, :]),
                                  ALU.subtract).then_inc(max_lo_done, 1)

            def normalise(q):
                dve.wait_ge(ctx_t_done, q + 1)
                view = misc[:].rearrange("p (t h e) -> p h t e", t=TPB, h=4)
                dve.reciprocal(rden[:, q % 2, :, :], view[:, :, :, HN]).then_inc(rden_done, 1)
                dve.wait_ge(rden_done, q + 1)
                dve.tensor_tensor(ctx_tok[:, :, :, q * HN:(q + 1) * HN], view[:, :, :, 0:HN],
                                  rden[:, q % 2, :, :].unsqueeze(3).to_broadcast([P, 4, TPB, HN]),
                                  ALU.mult).then_inc(ctx_done, 1)

            dve.wait_ge(x_loaded[0], 16)
            ln.statistics(dve, 0)
            dve.wait_ge(w_hi_ready, 1)
            dve.tensor_tensor(w_lo[:], w_raw, f32(w_hi[:]), ALU.subtract).then_inc(w_lo_ready, 1)
            ln.normalise(dve, 0)
            dve.wait_ge(x_loaded[1], 16)
            ln.statistics(dve, 1)
            ln.low_parts(dve, 0)
            ln.normalise(dve, 1)
            for w in range(2):
                dve.wait_ge(x_loaded[2 + w], 16)
                ln.statistics(dve, 2 + w)
                split_projection(0, w)
            ln.low_parts(dve, 1)
            ln.normalise(dve, 2)
            ln.normalise(dve, 3)
            ln.low_parts(dve, 2)
            ln.low_parts(dve, 3)
            for s in range(groups + 1):
                for c in range(chunks):
                    if s < groups:
                        for j in range(c * max_per_chunk, (c + 1) * max_per_chunk):
                            negated_max(s, j)
                    if c == 0 and s >= 1:
                        split_max(s - 1, 1)
                    if c == 1 and s >= 2:
                        normalise(quads * (s - 1) - 1)
                    if c in (2, 3) and s + 1 < groups:
                        split_projection(s + 1, c - 2)
                    if c == 4 and s < groups:
                        split_max(s, 0)
                    if c == 5 and s >= 1:
                        normalise(quads * (s - 1))
            normalise(groups * quads - 1)


def project_context(nc, semaphore, w, ctx_tok, ident, x_tok):
    with ExitStack() as ctx:
        ctx_hi, ctx_lo = (ctx.enter_context(nc.sbuf_tensor(f"p_ctx_{n}", [P, 2, KD, SEQ], F32R)) for n in ("hi", "lo"))
        w_hi, w_lo = (ctx.enter_context(nc.sbuf_tensor(f"p_w_{n}", [P, KD, D], F32R)) for n in ("hi", "lo"))
        turned = [[ctx.enter_context(nc.psum_tensor(f"p_turned{i}{k}", [P, SEQ], F32)) for k in range(KD)]
                  for i in range(2)]
        acc = [ctx.enter_context(nc.psum_tensor(f"p_acc{i}", [P, 2, D], F32)) for i in range(4)]
        w_hi_ready, w_lo_ready, turned_done, hi_done, lo_done, acc_done, added = (
            semaphore(s) for s in ("p_w_hi_ready", "p_w_lo_ready", "p_turned_done", "p_hi_done", "p_lo_done",
                                   "p_acc_done", "p_added"))
        block = ctx.enter_context(nc.Block())

        @block.tensor
        def _(pe):
            def turn(b):
                if b >= 2:
                    pe.wait_ge(lo_done, KD * (b - 1))
                for k in range(KD):
                    for t in range(TPB):
                        last = pe.transpose(turned[b % 2][k][:, t * P:(t + 1) * P],
                                            ctx_tok[:, b, t, k * P:(k + 1) * P], ident[:])
                last.then_inc(turned_done, 1)

            turn(0)
            for b in range(NB):
                if b + 1 < NB:
                    turn(b + 1)
                if b == 0:
                    pe.wait_ge(w_lo_ready, 1)
                pe.wait_ge(lo_done, KD * (b + 1))
                for half in range(2):
                    n = 2 * b + half
                    if n >= 4:
                        pe.wait_ge(added, n - 3)
                    for e in range(2):
                        tok, j = slice((half * 2 + e) * P, (half * 2 + e + 1) * P), 0
                        for k in range(KD):
                            for lhs, rhs in split_passes(ctx_hi[:, b % 2, k, tok], ctx_lo[:, b % 2, k, tok],
                                                         w_hi[:, k, :], w_lo[:, k, :]):
                                last = pe.matmul(acc[n % 4][:, e, :], lhs, rhs, start=(j == 0), stop=(j == 3 * KD - 1))
                                j += 1
                    last.then_inc(acc_done, 1)

        @block.scalar
        def _(act):
            act.activation(w_hi[:], w[:], ACT.Copy).then_inc(w_hi_ready, 1)
            for b in range(NB):
                act.wait_ge(turned_done, b + 1)
                if b >= 2:
                    act.wait_ge(acc_done, 2 * (b - 1))
                for k in range(KD):
                    act.activation(ctx_hi[:, b % 2, k, :], turned[b % 2][k][:], ACT.Copy).then_inc(hi_done, 1)

        @block.vector
        def _(dve):
            def low_parts(b):
                for k in range(KD):
                    dve.wait_ge(hi_done, KD * b + k + 1)
                    dve.tensor_tensor(ctx_lo[:, b % 2, k, :], turned[b % 2][k][:], f32(ctx_hi[:, b % 2, k, :]),
                                      ALU.subtract).then_inc(lo_done, 1)

            dve.wait_ge(w_hi_ready, 1)
            dve.tensor_tensor(w_lo[:], w[:], f32(w_hi[:]), ALU.subtract).then_inc(w_lo_ready, 1)
            low_parts(0)
            for b in range(NB):
                if b + 1 < NB:
                    low_parts(b + 1)
                for half in range(2):
                    n = 2 * b + half
                    dve.wait_ge(acc_done, n + 1)
                    t = b * TPB + half * 2
                    dve.tensor_tensor(x_tok[:, t:t + 2, :], acc[n % 4][:], x_tok[:, t:t + 2, :],
                                      ALU.add).then_inc(added, 1)


def norm_and_ffn(nc, semaphore, tag, weights, xn_hi, xn_lo, ident, x_tok, w_in=None, ahead=None, out=None):
    w_in_hi, w_in_lo, w3, w2 = weights
    with ExitStack() as ctx:
        def sb(name, shape, dt=F32):
            return ctx.enter_context(nc.sbuf_tensor(f"f_{name}_{tag}", shape, dt))

        def psum(name, shape):
            return ctx.enter_context(nc.psum_tensor(f"f_{name}_{tag}", shape, F32))

        def sem(name):
            return semaphore(f"f_{name}_{tag}")

        w_in_raw = sb("w_in_raw", [P, KD, D + NE])
        hidden_t = sb("hidden_t", [P, KD, NB * SEQ])
        hidden = sb("hidden", [P, NT, D])
        logit_rows = sb("logit_rows", [NE, 2, SEQ])
        rank = sb("rank", [P, NE])
        logits = sb("logits", [P, NT, NE])
        masked = sb("masked", [P, NT, NE])
        same = sb("same", [P, NT, NE])
        ranked = sb("ranked", [P, NT, NE])
        top = sb("top", [P, 2, NT])
        first = sb("first", [P, 2, NT])
        chosen = sb("chosen", [P, 2, NT, NE])
        gap = sb("gap", [P, NT])
        ratio = sb("ratio", [P, NT])
        total = sb("total", [P, NT])
        weight = sb("weight", [P, 2, NT])
        gates = sb("gates", [P, 3, NT, NE])
        summed = sb("summed", [NE, D])
        summed_t = sb("summed_t", [P, KD, NE])
        xt = [[psum(f"xt{k}", [P, SEQ]) for k in range(KD)]]
        up = [psum(f"up{i}", [P, SEQ]) for i in range(2)]
        mid = [psum(f"mid{i}", [P, 2, D]) for i in range(2)]
        rows = psum("rows", [NE, SEQ])
        turned = psum("turned", [P, (NT + KD) * NE])
        logits_ps = turned[:, 0:NT * NE].rearrange("p (t e) -> p t e", e=NE)
        tail = turned[:, NT * NE:].rearrange("p (k e) -> p k e", e=NE)
        ln = layer_norm(nc, ctx, semaphore, tag, x_tok, ident, xn_hi, xn_lo, xt, NT, TPB)

        names = ("w_loaded", "rank_set", "w_hi_ready", "w_lo_ready", "router_done", "router_read", "logits_done", "route",
                 "gap_ready", "ratio_ready", "gates_ready", "up_done", "up_read", "mid_done", "mid_read", "acc_done",
                 "summed_ready", "tail_done", "tail_read", "rows_done", "rows_added", "stored")
        (w_loaded, rank_set, w_hi_ready, w_lo_ready, router_done, router_read, logits_done, route,
         gap_ready, ratio_ready, gates_ready, up_done, up_read, mid_done, mid_read, acc_done,
         summed_ready, tail_done, tail_read, rows_done, rows_added, stored) = (sem(n) for n in names)
        block = ctx.enter_context(nc.Block())

        @block.sync
        def _(sp):
            if ahead:
                sp.dma_start(w_in_raw[:], w_in).then_inc(w_loaded, 16)
                ahead.load(sp)
            if out is not None:
                tokens = out.rearrange("b (t p) d -> p (b t) d", p=P)
                sp.dma_start(tokens[:, 1:, :], x_tok[:, 1:, :]).then_inc(stored, 16)
                sp.dma_start(tokens[NE:, 0, :], x_tok[NE:, 0, :]).then_inc(stored, 16)
                sp.wait_ge(rows_added, 1)
                sp.dma_start(tokens[0:NE, 0, :], x_tok[0:NE, 0, :]).then_inc(stored, 16)
                sp.wait_ge(stored, 48)

        @block.gpsimd
        def _(pool):
            ln.constants(pool)
            for g in range(NB):
                ln.deviations(pool, g)
            for e in range(NE):
                pool.memset(rank[:, e:e + 1], float(NE - e)).then_inc(rank_set, 1)
            if ahead:
                ahead.split(pool)

        @block.tensor
        def _(pe):
            def router(g):
                tok, j = slice(g * SEQ, (g + 1) * SEQ), 0
                pe.wait_ge(ln.lo_done, KD * (g + 1))
                if g >= 1:
                    pe.wait_ge(router_read, g)
                for k in range(KD):
                    for lhs, rhs in split_passes(w_in_hi[:, k, D:], w_in_lo[:, k, D:], xn_hi[:, k, tok], xn_lo[:, k, tok]):
                        last = pe.matmul(rows[:], lhs, rhs, start=(j == 0), stop=(j == 3 * KD - 1))
                        j += 1
                last.then_inc(router_done, 1)

            def turn_logits(g):
                pe.wait_ge(router_read, g + 1)
                for t in range(TPB):
                    last = pe.transpose(logits_ps[:, g * TPB + t, :], logit_rows[:, g % 2, t * P:(t + 1) * P],
                                        ident[0:NE, 0:NE])
                last.then_inc(logits_done, 1)

            def upper(g, m):
                n, j = g * KD + m, 0
                tok, ch = slice(g * SEQ, (g + 1) * SEQ), slice(m * P, (m + 1) * P)
                if n >= 2:
                    pe.wait_ge(up_read, n - 1)
                for k in range(KD):
                    for lhs, rhs in split_passes(w_in_hi[:, k, ch], w_in_lo[:, k, ch],
                                                 xn_hi[:, k, tok], xn_lo[:, k, tok]):
                        last = pe.matmul(up[n % 2][:], lhs, rhs, start=(j == 0), stop=(j == 3 * KD - 1))
                        j += 1
                last.then_inc(up_done, 1)

            def middle(n):
                pe.wait_ge(up_read, KD * (n * 2 // TPB + 1))
                if n >= 2:
                    pe.wait_ge(mid_read, n - 1)
                for e in range(2):
                    t = 2 * n + e
                    for k in range(KD):
                        last = pe.matmul(mid[n % 2][:, e, :], hidden_t[:, k, t * P:(t + 1) * P], w3[:, k, :],
                                         start=(k == 0), stop=(k == KD - 1))
                last.then_inc(mid_done, 1)

            ln.transpose(pe, 0)
            if ahead:
                pe.wait_ge(w_lo_ready, 1)
            router(0)
            ln.transpose(pe, 1)
            for g in range(NB + 1):
                if g < NB:
                    if g + 1 == NB:
                        turn_logits(g)
                    for m in range(KD):
                        upper(g, m)
                    if g + 1 < NB:
                        router(g + 1)
                        turn_logits(g)
                    if g + 2 < NB:
                        ln.transpose(pe, g + 2)
                if g >= 1:
                    for half in range(2):
                        middle(2 * (g - 1) + half)
            pe.wait_ge(gates_ready, 1)
            for t in range(NT):
                if t % 2 == 0:
                    pe.wait_ge(mid_read, t // 2 + 1)
                last = pe.matmul(rows[:, 0:D], gates[:, 2, t, :], hidden[:, t, :], start=(t == 0), stop=(t == NT - 1))
            last.then_inc(acc_done, 1)
            pe.wait_ge(summed_ready, 1)
            for k in range(KD):
                last = pe.transpose(tail[:, k, :], summed[:, k * P:(k + 1) * P], ident[0:NE, 0:NE])
            last.then_inc(tail_done, 1)
            pe.wait_ge(tail_read, 1)
            for k in range(KD):
                last = pe.matmul(rows[:, 0:D], summed_t[:, k, :], w2[:, k, :], start=(k == 0), stop=(k == KD - 1))
            last.then_inc(rows_done, 1)

        @block.scalar
        def _(act):
            if ahead:
                act.wait_ge(w_loaded, 16)
                act.activation(w_in_hi[:], w_in_raw[:], ACT.Copy).then_inc(w_hi_ready, 1)
            ln.high_parts(act, 0)
            def copy_logits(g):
                act.wait_ge(router_done, g + 1)
                if g >= 2:
                    act.wait_ge(logits_done, g - 1)
                act.activation(logit_rows[:, g % 2, :], rows[:], ACT.Copy).then_inc(router_read, 1)

            copy_logits(0)
            ln.high_parts(act, 1)
            for g in range(NB + 1):
                if g < NB:
                    for m in range(KD):
                        act.wait_ge(up_done, g * KD + m + 1)
                        act.activation(hidden_t[:, m, g * SEQ:(g + 1) * SEQ], up[(g * KD + m) % 2][:],
                                       ACT.Silu).then_inc(up_read, 1)
                    if g + 1 < NB:
                        copy_logits(g + 1)
                    if g + 2 < NB:
                        ln.high_parts(act, g + 2)
                if g >= 1:
                    for n in range(2 * (g - 1), 2 * g):
                        if n == NT // 2 - 2:
                            act.wait_ge(gap_ready, 1)
                            act.activation(ratio[:], gap[:], ACT.Exp).then_inc(ratio_ready, 1)
                        act.wait_ge(mid_done, n + 1)
                        act.activation(hidden[:, 2 * n:2 * n + 2, :], mid[n % 2][:], ACT.Silu).then_inc(mid_read, 1)

        @block.vector
        def _(dve):
            if ahead:
                ln.statistics(dve, 0)
                dve.wait_ge(w_hi_ready, 1)
                dve.tensor_tensor(w_in_lo[:], w_in_raw[:], f32(w_in_hi[:]), ALU.subtract).then_inc(w_lo_ready, 1)
                ln.statistics(dve, 1)
            else:
                for g in range(2):
                    ln.statistics(dve, g)
            for g in range(NB):
                ln.normalise(dve, g)
                if g >= 1:
                    ln.low_parts(dve, g - 1)
                if g + 2 < NB:
                    ln.statistics(dve, g + 2)
            ln.low_parts(dve, NB - 1)
            dve.wait_ge(logits_done, NB)
            dve.wait_ge(rank_set, NE)
            dve.tensor_copy(logits[:], logits_ps).then_inc(route, 1)
            step = 1
            wide = [P, NT, NE]
            for pick in range(2):
                src = logits if pick == 0 else masked
                dve.wait_ge(route, step)
                dve.tensor_reduce(top[:, pick, :], src[:], AX.X, ALU.max).then_inc(route, 1)
                dve.wait_ge(route, step + 1)
                dve.tensor_tensor(same[:], src[:], top[:, pick, :].unsqueeze(2).to_broadcast(wide),
                                  ALU.is_equal).then_inc(route, 1)
                dve.wait_ge(route, step + 2)
                dve.tensor_tensor(ranked[:], same[:], rank[:].unsqueeze(1).to_broadcast(wide),
                                  ALU.mult).then_inc(route, 1)
                dve.wait_ge(route, step + 3)
                dve.tensor_reduce(first[:, pick, :], ranked[:], AX.X, ALU.max).then_inc(route, 1)
                dve.wait_ge(route, step + 4)
                dve.tensor_tensor(chosen[:, pick, :, :], ranked[:], first[:, pick, :].unsqueeze(2).to_broadcast(wide),
                                  ALU.is_equal).then_inc(route, 1)
                step += 5
                if pick == 0:
                    dve.wait_ge(route, step)
                    dve.scalar_tensor_tensor(masked[:], chosen[:, 0, :, :], -3.0e38, logits[:],
                                             ALU.mult, ALU.add).then_inc(route, 1)
                    step += 1
            dve.wait_ge(route, step)
            dve.tensor_tensor(gap[:], top[:, 1, :], top[:, 0, :], ALU.subtract).then_inc(gap_ready, 1)
            dve.wait_ge(ratio_ready, 1)
            dve.tensor_scalar(total[:], ratio[:], 1.0, None, ALU.add).then_inc(route, 1)
            dve.wait_ge(route, step + 1)
            dve.reciprocal(weight[:, 0, :], total[:]).then_inc(route, 1)
            dve.wait_ge(route, step + 2)
            dve.tensor_tensor(weight[:, 1, :], ratio[:], weight[:, 0, :], ALU.mult).then_inc(route, 1)
            dve.wait_ge(route, step + 3)
            for pick in range(2):
                dve.tensor_tensor(gates[:, pick, :, :], chosen[:, pick, :, :],
                                  weight[:, pick, :].unsqueeze(2).to_broadcast(wide), ALU.mult).then_inc(route, 1)
            dve.wait_ge(route, step + 5)
            dve.tensor_tensor(gates[:, 2, :, :], gates[:, 0, :, :], gates[:, 1, :, :], ALU.add).then_inc(gates_ready, 1)
            dve.wait_ge(acc_done, 1)
            dve.tensor_copy(summed[:], rows[:, 0:D]).then_inc(summed_ready, 1)
            dve.wait_ge(tail_done, 1)
            dve.tensor_copy(summed_t[:], tail).then_inc(tail_read, 1)
            dve.wait_ge(rows_done, 1)
            dve.tensor_tensor(x_tok[0:NE, 0, :], rows[:, 0:D], x_tok[0:NE, 0, :], ALU.add).then_inc(rows_added, 1)


def norm_and_decay(nc, semaphore, w_beta, bias, xn_hi, xn_lo, ident, x_tok, beta_tok, keep_rows):
    with ExitStack() as ctx:
        def sb(name, shape, dt=F32):
            return ctx.enter_context(nc.sbuf_tensor(f"d_{name}", shape, dt))

        def sem(name):
            return semaphore(f"d_{name}")

        w_hi = sb("w_hi", [P, KD, LH], F32R)
        w_lo = sb("w_lo", [P, KD, LH], F32R)
        beta_rows = sb("beta_rows", [LH, NB, SEQ])
        keep = sb("keep", [LH, NB, SEQ + HALF])
        zeros = sb("zeros", [LH, HALF])
        z = [ctx.enter_context(nc.psum_tensor(f"d_z{b}", [LH, SEQ], F32)) for b in range(NB)]
        turned = ctx.enter_context(nc.psum_tensor("d_turned", [P, NT, LH], F32))
        xt = [[ctx.enter_context(nc.psum_tensor(f"d_xt{k}", [P, P], F32)) for k in range(KD)]]
        ln = layer_norm(nc, ctx, semaphore, "c", x_tok, ident, xn_hi, xn_lo, xt, 1, 1)
        zeros_set, w_hi_ready, w_lo_ready, z_done, beta_done, kept, keep_done, turned_done, copied, written = (
            sem(n) for n in ("zeros_set", "w_hi_ready", "w_lo_ready", "z_done", "beta_done", "kept", "keep_done", "turned_done",
                             "copied", "written"))
        block = ctx.enter_context(nc.Block())
        order = list(range(1, NB)) + [0]

        @block.sync
        def _(sp):
            for i, b in enumerate(order):
                sp.wait_ge(keep_done, i + 1)
                sp.dma_start(keep_rows[:, b, :], keep[:, b, :]).then_inc(written, 16)
            sp.wait_ge(written, 16 * NB)

        @block.gpsimd
        def _(pool):
            pool.memset(zeros[:], 0.0).then_inc(zeros_set, 1)
            ln.constants(pool)
            ln.deviations(pool, 0)

        @block.tensor
        def _(pe):
            def turn(i):
                pe.wait_ge(beta_done, i + 1)
                b = order[i]
                for t in range(TPB):
                    last = pe.transpose(turned[:, b * TPB + t, :], beta_rows[:, b, t * P:(t + 1) * P],
                                        ident[0:LH, 0:LH])
                last.then_inc(turned_done, 1)

            pe.wait_ge(w_hi_ready, 1)
            pe.wait_ge(w_lo_ready, 1)
            for i, b in enumerate(order):
                if b == 0:
                    pe.wait_ge(ln.lo_done, KD)
                tok, j = slice(b * SEQ, (b + 1) * SEQ), 0
                for k in range(KD):
                    for lhs, rhs in split_passes(w_hi[:, k, :], w_lo[:, k, :], xn_hi[:, k, tok], xn_lo[:, k, tok]):
                        last = pe.matmul(z[b][:], lhs, rhs, start=(j == 0), stop=(j == 3 * KD - 1))
                        j += 1
                last.then_inc(z_done, 1)
                if i == 0:
                    ln.transpose(pe, 0)
                else:
                    turn(i - 1)
            turn(NB - 1)

        @block.scalar
        def _(act):
            act.activation(w_hi[:], w_beta[:], ACT.Copy).then_inc(w_hi_ready, 1)
            for i, b in enumerate(order):
                act.wait_ge(z_done, i + 1)
                act.activation(beta_rows[:, b, :], z[b][:], ACT.Sigmoid, bias=bias[:]).then_inc(beta_done, 1)
                if i == 0:
                    ln.high_parts(act, 0)

        @block.vector
        def _(dve):
            dve.wait_ge(w_hi_ready, 1)
            dve.tensor_tensor(w_lo[:], w_beta[:], f32(w_hi[:]), ALU.subtract).then_inc(w_lo_ready, 1)
            ln.statistics(dve, 0)
            ln.normalise(dve, 0)
            ln.low_parts(dve, 0)
            for i, b in enumerate(order):
                dve.wait_ge(beta_done, i + 1)
                dve.tensor_scalar(keep[:, b, 0:SEQ], beta_rows[:, b, :], -1.0, 1.0, ALU.mult, ALU.add).then_inc(kept, 1)
                dve.wait_ge(kept, i + 1)
                if i == 0:
                    dve.wait_ge(zeros_set, 1)
                dve.tensor_tensor_scan(keep[:, b, SEQ:], keep[:, b, HALF:SEQ], zeros[:], 1.0, ALU.mult,
                                       ALU.add).then_inc(keep_done, 1)
            dve.wait_ge(turned_done, NB)
            dve.tensor_copy(beta_tok[:], turned[:]).then_inc(copied, 1)


def split_head_weights(pool, w_raw, w_hi, w_lo, part, hi_done, count, ready):
    pool.tensor_scalar(w_hi[:, :, part, :], w_raw[:, :, part, :], 1.0, 0.0, ALU.mult, ALU.add).then_inc(hi_done, 1)
    pool.wait_ge(hi_done, count)
    pool.tensor_tensor(w_lo[:, :, part, :], w_raw[:, :, part, :], f32(w_hi[:, :, part, :]),
                       ALU.subtract).then_inc(ready, 1)


def first_head_weights(semaphore, w_raw, w_hi, w_lo, wo_hi, wo_lo, wo_raw, w_heads, others):
    loaded, constants_loaded, hi_done, ready, wo_hi_done, wo_ready = (semaphore(n) for n in (
        "first_loaded", "first_constants_loaded", "first_hi_done", "first_ready", "wo_hi_done", "wo_ready"))

    def load(sp):
        sp.dma_start(w_raw[:], w_heads[0]).then_inc(loaded, 16)
        for dst, src in others:
            sp.dma_start(dst, src).then_inc(constants_loaded, 16)
        sp.wait_ge(constants_loaded, 16 * len(others))

    def split(pool):
        pool.wait_ge(loaded, 16)
        for part in range(4):
            split_head_weights(pool, w_raw, w_hi, w_lo, part, hi_done, part + 1, ready)
        pool.wait_ge(ready, 4)
        pool.wait_ge(constants_loaded, 16 * len(others))
        pool.tensor_scalar(wo_hi[:], wo_raw[:], 1.0, 0.0, ALU.mult, ALU.add).then_inc(wo_hi_done, 1)
        pool.wait_ge(wo_hi_done, 1)
        pool.tensor_tensor(wo_lo[:], wo_raw[:], f32(wo_hi[:]), ALU.subtract).then_inc(wo_ready, 1)
        pool.wait_ge(wo_ready, 1)

    steps = Steps()
    steps.load, steps.split = load, split
    return steps


def linear_attention(nc, semaphore, head_weights, w_heads, wo, par, norm, k_norm, xn_hi, xn_lo, ident, beta_tok, keep_rows, x_tok):
    PAIRS, BODY = LH // 2, 2 * NB
    UNITS = PAIRS * BODY
    PAIR = 2 * DK
    WIDTH = [HALF - i * P % HALF for i in range(TPB)]
    START = [0, 2 * HALF, HALF, 2 * HALF + P]
    CAUSAL = sum(WIDTH)
    FIRST = HALF // P
    with ExitStack() as ctx:
        def sb(name, shape, dt=F32):
            return ctx.enter_context(nc.sbuf_tensor(f"l_{name}", shape, dt))

        def psum(name, shape=(P, SEQ)):
            return ctx.enter_context(nc.psum_tensor(f"l_{name}", list(shape), F32))

        def sem(name):
            return semaphore(f"l_{name}")

        Q, K, G, V = range(4)
        w_raw, w_hi, w_lo = head_weights
        wo_hi, wo_lo = wo
        minus_half = sb("minus_half", [P, 2 * TPB])
        quarter = sb("quarter", [P, 2 * TPB])
        diag = sb("diag", [P, SEQ])
        keep = sb("keep", [P, 4, SEQ + HALF])
        conv = sb("conv", [P, 2, 2, SEQ])
        stats = sb("stats", [P, 2, 2 * TPB, 6])
        small = sb("small", [P, 8, 2 * TPB])
        scale = sb("scale", [P, 2, 2 * TPB])
        shift = sb("shift", [P, 2, 2 * TPB])
        normed = sb("normed", [P, 2, TPB, DK])
        qk = sb("qk", [P, 2, 2, SEQ])
        k_tok = sb("k_tok", [P, 2, FIRST, DK])
        q_late = sb("q_late", [P, 4, HALF])
        state = sb("state", [P, 2, DK])
        decay = sb("decay", [P, CAUSAL])
        masked = sb("masked", [P, 2, CAUSAL])
        gate = sb("gate", [P, 4, SEQ])
        values = sb("values", [P, 2, TPB, PAIR])
        gated_hi = sb("gated_hi", [P, 4, SEQ], F32R)
        gated_lo = sb("gated_lo", [P, 4, SEQ], F32R)
        gated = sb("gated", [P, 2, SEQ])

        proj_q, proj_k, proj_gv, turn_q, turn_k, score_a, score_b, outp = (psum(n) for n in (
            "proj_q", "proj_k", "proj_gv", "turn_q", "turn_k", "score_a", "score_b", "outp"))
        proj = (proj_q, proj_k)
        turn = (turn_q, turn_k)

        w_loaded, consts_set, w_hi_done, w_ready = (sem(n) for n in (
            "w_loaded", "consts_set", "w_hi_done", "w_ready"))
        keep_loaded = [sem(f"keep_loaded{i}") for i in range(4)]
        q_proj, k_proj, g_proj, v_proj = (sem(n) for n in ("q_proj", "k_proj", "g_proj", "v_proj"))
        q_tap, k_tap, q_step, k_step, q_conv, k_conv = (sem(n) for n in (
            "q_tap", "k_tap", "q_step", "k_step", "q_conv", "k_conv"))
        q_act, k_act, gate_act = (sem(n) for n in ("q_act", "k_act", "gate_act"))
        turned, stats_done, stat_step, scales_ready, norm_done, returned, qk_ready = (
            (sem(f"{n}_q"), sem(f"{n}_k")) for n in (
                "turned", "stats_done", "stat_step", "scales_ready", "norm_done", "returned", "qk_ready"))
        score_a_done, score_b_done = (sem(n) for n in ("score_a_done", "score_b_done"))
        decay_done, masked_a, masked_b = (sem(n) for n in ("decay_done", "masked_a", "masked_b"))
        k_scaled, k_shifted, k_decayed, q_decayed, state_done = (sem(n) for n in (
            "k_scaled", "k_shifted", "k_decayed", "q_decayed", "state_done"))
        values_done, read_out, gated_done, gated_hi_done, gated_lo_done, out_done, added = (sem(n) for n in (
            "values_done", "read_out", "gated_done", "gated_hi_done", "gated_lo_done", "out_done", "added"))
        proj_sem, tap_sem, step_sem, conv_sem, act_sem = (
            (q_proj, k_proj), (q_tap, k_tap), (q_step, k_step), (q_conv, k_conv), (q_act, k_act))
        block = ctx.enter_context(nc.Block())

        def wait(eng, semaphore, count):
            if not isinstance(count, int) or count > 0:
                eng.wait_ge(semaphore, count)

        def wait_apart(eng, semaphore, count):
            wait(eng, semaphore, count)
            eng.nop(nofuse=True)

        def keep_count(pair, k):
            return 16 * (2 * (pair if k >= 1 else pair - 1) + (k - 1) % BODY // 4 + 1)

        def has(u, lag):
            return not isinstance(u, int) or 0 <= u - lag < UNITS

        def steps(eng, step, lags, last_apart=False):
            for k in range(BODY):
                step(0, k, k)
            with eng.Fori(1, PAIRS - 1 if last_apart else PAIRS) as pair:
                for k in range(BODY):
                    step(pair, k, pair * BODY + k)
            if last_apart:
                for k in range(BODY):
                    step(PAIRS - 1, k, (PAIRS - 1) * BODY + k)
            for k in range(lags):
                step(PAIRS, k, UNITS + k)

        @block.sync
        def _(sp):
            def step(pair, k, u):
                wait(sp, decay_done, u - 3)
                wait(sp, q_decayed, u - 3)
                b, e = k // 2, k % 2
                row = keep_rows[bass.ds(2 * pair + e, 1), b, :]
                sp.dma_start(keep[:, k % 4, :], row.to_broadcast([P, SEQ + HALF])).then_inc(keep_loaded[k % 4], 16)
                if k == 1 and not (isinstance(pair, int) and pair + 1 >= PAIRS):
                    wait(sp, w_ready, 4 * pair)
                    sp.dma_start(w_raw[:], w_heads[bass.ds(pair + 1, 1)]).then_inc(w_loaded, 16)

            steps(sp, step, 0, last_apart=True)

        @block.gpsimd
        def _(pool):
            pool.memset(minus_half[:], -0.5).then_inc(consts_set, 1)
            pool.memset(quarter[:], 0.25).then_inc(consts_set, 1)
            pool.memset(diag[:, P:], 0.0).then_inc(consts_set, 1)
            pool.tensor_copy(diag[:, 0:P], ident[:]).then_inc(consts_set, 1)

            def scales(v, k, w):
                i, tiles = k % 2, slice(w * TPB, (w + 1) * TPB)
                st = stats[:, i, tiles]
                wait(pool, stats_done[w], v + 1)
                wait(pool, norm_done[w], v - 1)
                pool.tensor_tensor(small[:, 1, tiles], st[:, :, 1], st[:, :, 4], ALU.subtract)
                pool.tensor_tensor(small[:, 2, tiles], st[:, :, 2], st[:, :, 5], ALU.add).then_inc(stat_step[w], 1)
                pool.tensor_tensor(small[:, 0, tiles], st[:, :, 1], st[:, :, 4], ALU.add)
                wait(pool, stat_step[w], 4 * v + 1)
                pool.tensor_tensor(small[:, 3, tiles], small[:, 1, tiles], small[:, 1, tiles], ALU.mult)
                pool.tensor_scalar(small[:, 4, tiles], small[:, 2, tiles], 1.0 / DK, EPS, ALU.mult,
                                   ALU.add).then_inc(stat_step[w], 1)
                wait(pool, stat_step[w], 4 * v + 2)
                pool.tensor_tensor(small[:, 6, tiles], small[:, 3, tiles], quarter[:, tiles],
                                   ALU.mult).then_inc(stat_step[w], 1)
                pool.tensor_scalar(small[:, 5, tiles], small[:, 0, tiles], -0.5, 0.0, ALU.mult, ALU.add)
                wait(pool, stat_step[w], 4 * v + 3)
                pool.tensor_tensor(small[:, 7, tiles], small[:, 6, tiles], small[:, 4, tiles],
                                   ALU.add).then_inc(stat_step[w], 1)
                wait(pool, stat_step[w], 4 * v + 4)
                pool.tensor_tensor(scale[:, i, tiles], small[:, 7, tiles], minus_half[:, tiles],
                                   ALU.pow).then_inc(scales_ready[w], 1)
                wait(pool, scales_ready[w], 2 * v + 1)
                pool.tensor_tensor(shift[:, i, tiles], small[:, 5, tiles], scale[:, i, tiles],
                                   ALU.mult).then_inc(scales_ready[w], 1)

            def decayed(v, k, rows_in):
                m, r = k % 2, k % 4
                wide = [P, FIRST, DK]
                wait(pool, norm_done[1], v + 1)
                wait(pool, score_b_done, v - 1)
                pool.tensor_tensor(k_tok[:, m], normed[:, 1, 0:FIRST, :],
                                   k_norm[:, 0, :].unsqueeze(1).to_broadcast(wide), ALU.mult).then_inc(k_scaled, 1)
                wait(pool, keep_loaded[r], rows_in)
                wait(pool, qk_ready[0], v + 1)
                wait(pool, read_out, v - 3)
                pool.tensor_tensor(q_late[:, r, :], qk[:, 0, m, HALF:], keep[:, r, SEQ:],
                                   ALU.mult).then_inc(q_decayed, 1)
                wait(pool, k_scaled, v + 1)
                pool.tensor_tensor(k_tok[:, m], k_tok[:, m],
                                   k_norm[:, 1, :].unsqueeze(1).to_broadcast(wide), ALU.add).then_inc(k_shifted, 1)
                wait(pool, k_shifted, v + 1)
                wait_apart(pool, decay_done, v + 1)
                ends = decay[:, HALF - 1:START[1] + P:START[1] + P - HALF]
                pool.tensor_tensor(k_tok[:, m], k_tok[:, m], ends.unsqueeze(2).to_broadcast(wide),
                                   ALU.mult).then_inc(k_decayed, 1)

            def gated_low(v, k):
                wait(pool, gated_hi_done, v + 1)
                pool.tensor_tensor(gated_lo[:, k % 4, :], gated[:, k % 2, :], f32(gated_hi[:, k % 4, :]),
                                   ALU.subtract).then_inc(gated_lo_done, 1)

            pool.wait_ge(consts_set, 4)

            def step(pair, k, u):
                if has(u, 1):
                    for w in range(2):
                        scales(u - 1, (k - 1) % BODY, w)
                    decayed(u - 1, (k - 1) % BODY, keep_count(pair, k))
                if has(u, 3):
                    gated_low(u - 3, (k - 3) % BODY)

            steps(pool, step, 3)

        @block.tensor
        def _(pe):
            def project(out, part, k):
                b, e = k // 2, k % 2
                tok, ch, j = slice(b * SEQ, (b + 1) * SEQ), slice(e * DK, (e + 1) * DK), 0
                for kd in range(KD):
                    for lhs, rhs in split_passes(w_hi[:, kd, part, ch], w_lo[:, kd, part, ch],
                                                 xn_hi[:, kd, tok], xn_lo[:, kd, tok]):
                        last = pe.matmul(out[:], lhs, rhs, start=(j == 0), stop=(j == 3 * KD - 1))
                        j += 1
                return last

            def project_values(k):
                b, half = k // 2, k % 2
                for t in range(2):
                    n = b * TPB + half * 2 + t
                    tok, j = slice(n * P, (n + 1) * P), 0
                    for kd in range(KD):
                        for lhs, rhs in split_passes(xn_hi[:, kd, tok], xn_lo[:, kd, tok],
                                                     w_hi[:, kd, V, :], w_lo[:, kd, V, :]):
                            last = pe.matmul(proj_gv[:, t * PAIR:(t + 1) * PAIR], lhs, rhs,
                                             start=(j == 0), stop=(j == 3 * KD - 1))
                            j += 1
                return last

            def score(out, at, i, par_):
                return pe.matmul(out[:, at:at + WIDTH[i]], qk[:, 1, par_, i * P:(i + 1) * P],
                                 qk[:, 0, par_, i * P:i * P + WIDTH[i]], start=True, stop=True)

            def turn_tokens(v, k, w):
                wait(pe, act_sem[w], v + 1)
                wait(pe, qk_ready[w], v)
                for t in range(TPB):
                    last = pe.transpose(turn[w][:, t * P:(t + 1) * P], conv[:, w, k % 2, t * P:(t + 1) * P], ident[:])
                last.then_inc(turned[w], 1)

            def turn_back(v, w):
                wait(pe, norm_done[w], v + 1)
                for t in range(TPB):
                    last = pe.transpose(turn[w][:, t * P:(t + 1) * P], normed[:, w, t, :], ident[:])
                last.then_inc(returned[w], 1)

            def step(pair, k, u):
                if has(u, 1):
                    for w in range(2):
                        turn_tokens(u - 1, (k - 1) % BODY, w)
                if has(u, 2):
                    v, m = u - 2, k % 2
                    for w in range(2):
                        wait(pe, qk_ready[w], v + 1)
                    wait(pe, masked_a, v)
                    score(score_a, 0, 0, m)
                    score(score_a, HALF, 2, m).then_inc(score_a_done, 1)
                    wait(pe, masked_b, v)
                    wait(pe, state_done, v)
                    score(score_b, 0, 1, m)
                    score(score_b, P, 3, m)
                    wait(pe, k_decayed, v + 1)
                    kk = (k - 2) % BODY
                    wait(pe, values_done, v + 1 - kk % 2)
                    for i in range(FIRST):
                        last = pe.matmul(score_b[:, 2 * P:2 * P + DK], k_tok[:, m, i, :],
                                         values[:, kk // 2 % 2, i, kk % 2 * DK:(kk % 2 + 1) * DK],
                                         start=(i == 0), stop=(i == FIRST - 1))
                    last.then_inc(score_b_done, 1)
                if has(u, 0):
                    for w in range(2):
                        if k == 0:
                            wait(pe, w_ready, 4 * (pair - 1) + w + 1)
                        wait(pe, conv_sem[w], u)
                        project(proj[w], w, k).then_inc(proj_sem[w], 1)
                if has(u, 0):
                    if k == 0:
                        wait(pe, w_ready, 4 * (pair - 1) + G + 1)
                    wait(pe, values_done, u)
                    project(proj_gv, G, k).then_inc(g_proj, 1)
                if has(u, 1):
                    turn_back(u - 1, 0)
                if has(u, 3):
                    v, kk = u - 3, (k - 3) % BODY
                    m, e, c = kk % 2, kk % 2, kk // 2
                    wait(pe, masked_b, v + 1)
                    wait(pe, state_done, v + 1)
                    wait(pe, q_decayed, v + 1)
                    wait(pe, values_done, v + 2 - kk % 2)
                    wait(pe, added, v - 2)
                    for i in (3, 2, None, 1, 0):
                        if i is None:
                            pe.matmul(outp[:, HALF:SEQ], state[:, m, :], q_late[:, kk % 4, :], start=False, stop=False,
                                      skip_group_check=True)
                        else:
                            last = pe.matmul(outp[:, i * P:i * P + WIDTH[i]], values[:, c % 2, i, e * DK:(e + 1) * DK],
                                             masked[:, m, START[i]:START[i] + WIDTH[i]],
                                             start=(i == TPB - 1), stop=(i == 0), skip_group_check=True)
                    last.then_inc(read_out, 1)
                if has(u, 0):
                    if k == 0:
                        wait(pe, w_ready, 4 * (pair - 1) + V + 1)
                    wait(pe, gate_act, u + 1)
                    project_values(k).then_inc(v_proj, 1)
                if has(u, 1):
                    turn_back(u - 1, 1)
                if has(u, 5):
                    v, kk = u - 5, (k - 5) % BODY
                    w, half = kk // 2, kk % 2
                    wait(pe, gated_done, min(v + 3, UNITS) if isinstance(v, int) else v + 3)
                    wait(pe, gated_lo_done, v + 2 - kk % 2)
                    wait(pe, added, v)
                    head = 2 * (pair if k >= 5 else pair - 1)
                    for t in range(2):
                        tok, j = slice((half * 2 + t) * P, (half * 2 + t + 1) * P), 0
                        for e in range(2):
                            r = (2 * w + e) % 4
                            for lhs, rhs in split_passes(gated_hi[:, r, tok], gated_lo[:, r, tok],
                                                         wo_hi[:, head_of(head, e), :], wo_lo[:, head_of(head, e), :]):
                                last = pe.matmul(outp[:, t * D:(t + 1) * D], lhs, rhs, start=(j == 0), stop=(j == 5))
                                j += 1
                    last.then_inc(out_done, 1)

            def head_of(head, e):
                return head + e

            steps(pe, step, 6)

        @block.scalar
        def _(act):
            def tap(pair, k, u, w):
                h, m = 2 * pair + k % 2, k % 2
                wait(act, proj_sem[w], u + 1)
                wait_apart(act, turned[w], u - 1)
                act.activation(conv[:, w, m, :], proj[w][:], ACT.Copy,
                               scale=par[:, h, (w + 1) * TAPS - 1:(w + 1) * TAPS]).then_inc(tap_sem[w], 1)

            def silu(pair, k, u, w):
                h, m = 2 * pair + k % 2, k % 2
                wait_apart(act, conv_sem[w], u + 1)
                act.activation(conv[:, w, m, :], conv[:, w, m, :], ACT.Silu,
                               bias=par[:, h, 2 * TAPS + w:2 * TAPS + w + 1]).then_inc(act_sem[w], 1)

            def normalise(v, k, w):
                m = k % 2
                wait(act, scales_ready[w], 2 * v + 2)
                wait(act, returned[w], v)
                if w == 1:
                    wait(act, k_scaled, v)
                for t in range(TPB):
                    j = w * TPB + t
                    last = act.activation(normed[:, w, t, :], turn[w][:, t * P:(t + 1) * P], ACT.Identity,
                                          scale=scale[:, m, j:j + 1], bias=shift[:, m, j:j + 1])
                last.then_inc(norm_done[w], 1)

            def high_weights(u, part):
                wait(act, (q_proj, k_proj, g_proj, v_proj)[part], u + 1)
                act.activation(w_hi[:, :, part, :], w_raw[:, :, part, :], ACT.Copy).then_inc(w_hi_done, 1)

            def norm_affine(v, k, w):
                m = k % 2
                wait(act, returned[w], v + 1)
                wait(act, score_b_done, v - 1)
                if w == 0:
                    wait(act, q_decayed, v - 1)
                act.activation(qk[:, w, m, :], turn[w][:], ACT.Identity, scale=norm[:, 2 * w:2 * w + 1],
                               bias=norm[:, 2 * w + 1:2 * w + 2]).then_inc(qk_ready[w], 1)

            def step(pair, k, u):
                before = (u - 1, (k - 1) % BODY)
                new_weights = k == BODY - 1 and not (isinstance(pair, int) and pair + 1 >= PAIRS)
                if has(u, 0):
                    tap(pair, k, u, 0)
                if has(u, 1):
                    normalise(*before, 0)
                if has(u, 0):
                    tap(pair, k, u, 1)
                if has(u, 2):
                    v = u - 2
                    wait(act, masked_b, v + 1)
                    wait(act, read_out, v - 1)
                    act.activation(state[:, k % 2, :], score_b[:, 2 * P:2 * P + DK], ACT.Copy).then_inc(state_done, 1)
                if has(u, 0):
                    wait(act, g_proj, u + 1)
                    wait(act, gated_done, u - 3)
                    act.activation(gate[:, k % 4, :], proj_gv[:], ACT.Silu).then_inc(gate_act, 1)
                if has(u, 1):
                    normalise(*before, 1)
                if has(u, 0):
                    silu(pair, k, u, 0)
                if has(u, 1):
                    norm_affine(*before, 0)
                if new_weights:
                    wait(act, w_loaded, 16 * (pair + 1))
                    high_weights(u, Q)
                if has(u, 0):
                    silu(pair, k, u, 1)
                if has(u, 1):
                    norm_affine(*before, 1)
                if new_weights:
                    for part in (K, G, V):
                        high_weights(u, part)

            steps(act, step, 2, last_apart=True)

        @block.vector
        def _(dve):
            def convolve(pair, k, u, w, s):
                h, m = 2 * pair + k % 2, k % 2
                if s == 1:
                    wait(dve, tap_sem[w], u + 1)
                else:
                    wait(dve, step_sem[w], 2 * u + s - 1)
                tap = w * TAPS + TAPS - 1 - s
                ins = dve.scalar_tensor_tensor(conv[:, w, m, s:], proj[w][:, 0:SEQ - s], par[:, h, tap:tap + 1],
                                               conv[:, w, m, s:], ALU.mult, ALU.add)
                ins.then_inc(conv_sem[w] if s == TAPS - 1 else step_sem[w], 1)

            def mask(score, v, k, at, n):
                return dve.tensor_tensor(masked[:, k % 2, at:at + n], score[:, 0:n], decay[:, at:at + n], ALU.mult)

            def scan(r, tiles):
                for i in tiles:
                    last = dve.tensor_tensor_scan(decay[:, START[i]:START[i] + WIDTH[i]], keep[:, r, i * P:i * P + WIDTH[i]],
                                                  diag[:, 0:WIDTH[i]], 0.0, ALU.mult, ALU.add)
                return last

            def low_weights(pair, part):
                wait(dve, w_hi_done, 4 * (pair - 1) + part + 1)
                dve.tensor_tensor(w_lo[:, :, part, :], w_raw[:, :, part, :], f32(w_hi[:, :, part, :]),
                                  ALU.subtract).then_inc(w_ready, 1)

            def step(pair, k, u):
                new_weights = k == 0 and has(u, 0) and not (isinstance(pair, int) and pair == 0)
                if has(u, 1):
                    v, m = u - 1, (k - 1) % 2
                    for w in range(2):
                        wait(dve, turned[w], v + 1)
                        wait(dve, scales_ready[w], 2 * (v - 1))
                        for t in range(TPB):
                            last = dve.bn_stats(stats[:, m, w * TPB + t, :], turn[w][:, t * P:(t + 1) * P])
                        last.then_inc(stats_done[w], 1)
                if new_weights:
                    low_weights(pair, K)
                if has(u, 2):
                    v = u - 2
                    wait(dve, decay_done, v + 1)
                    wait(dve, read_out, v - 1)
                    wait(dve, score_a_done, v + 1)
                    mask(score_a, v, k, 0, 512).then_inc(masked_a, 1)
                    wait(dve, score_b_done, v + 1)
                    mask(score_b, v, k, SEQ, CAUSAL - SEQ).then_inc(masked_b, 1)
                if new_weights:
                    low_weights(pair, G)
                    low_weights(pair, V)
                if has(u, 0):
                    convolve(pair, k, u, 0, 1)
                    convolve(pair, k, u, 0, 2)
                    convolve(pair, k, u, 1, 1)
                    convolve(pair, k, u, 0, 3)
                    convolve(pair, k, u, 1, 2)
                if has(u, 1):
                    v, kk = u - 1, (k - 1) % BODY
                    wait(dve, keep_loaded[kk % 4], keep_count(pair, k))
                    wait(dve, masked_b, v)
                    wait(dve, k_decayed, v)
                    scan(kk % 4, [0])
                if has(u, 3):
                    v, r = u - 3, (k - 3) % 4
                    wait(dve, read_out, v + 1)
                    wait(dve, gate_act, v + 1)
                    wait(dve, gated_lo_done, v - 1)
                    dve.tensor_tensor(gated[:, r % 2, :], outp[:], gate[:, r, :], ALU.mult).then_inc(gated_done, 1)
                if has(u, 0):
                    convolve(pair, k, u, 1, 3)
                if has(u, 3):
                    v, r = u - 3, (k - 3) % 4
                    wait(dve, gated_done, v + 1)
                    wait(dve, out_done, v - 2 - (k - 3) % 2)
                    dve.tensor_scalar(gated_hi[:, r, :], gated[:, r % 2, :], 1.0, 0.0, ALU.mult,
                                      ALU.add).then_inc(gated_hi_done, 1)
                if k == BODY - 1 and not (isinstance(pair, int) and pair + 1 >= PAIRS):
                    low_weights(pair + 1, Q)
                if has(u, 1):
                    scan((k - 1) % 4, [1, 2, 3]).then_inc(decay_done, 1)
                if has(u, 0):
                    b, half = k // 2, k % 2
                    n = b * TPB + 2 * half
                    wait(dve, v_proj, u + 1)
                    wait(dve, read_out, u - half - 2)
                    dve.tensor_tensor(
                        values[:, b % 2, 2 * half:2 * half + 2, :].rearrange("p t (e c) -> p t e c", e=2),
                        proj_gv[:].rearrange("p (t e c) -> p t e c", t=2, e=2),
                        beta_tok[:, n:n + 2, bass.ds(2 * pair, 2)].unsqueeze(3).to_broadcast([P, 2, 2, DK]),
                        ALU.mult).then_inc(values_done, 1)
                if has(u, 5):
                    v, kk = u - 5, (k - 5) % BODY
                    n = (kk // 2) * TPB + 2 * (kk % 2)
                    wait(dve, out_done, v + 1)
                    wait(dve, added, v - 2)
                    dve.tensor_tensor(x_tok[:, n:n + 2, :], outp[:].rearrange("p (t d) -> p t d", t=2),
                                      x_tok[:, n:n + 2, :], ALU.add).then_inc(added, 1)

            dve.wait_ge(consts_set, 4)
            steps(dve, step, 6, last_apart=True)


def build(nc, x, w_qkv, w_proj, b_proj, w_in, w_mid, w_out, w_beta, b_beta, w_heads, w_o, params, norms, k_norms, out):
    keep_rows = nc.dram_tensor("keep_rows", [LH, NB, SEQ + HALF], F32, kind="Internal").ap()
    held = []

    def semaphore(name):
        held.append(nc.alloc_semaphore(name))
        return held[-1]

    with ExitStack() as ctx:
        def sb(name, shape, dt=F32, scope=ctx):
            return scope.enter_context(nc.sbuf_tensor(name, shape, dt))

        x_tok = sb("x_tok", [P, NT, D])
        ident = sb("ident", [P, P])
        xn_hi = sb("xn_hi", [P, KD, NB * SEQ], F32R)
        xn_lo = sb("xn_lo", [P, KD, NB * SEQ], F32R)
        ffn = (sb("w_in_hi", [P, KD, D + NE], F32R), sb("w_in_lo", [P, KD, D + NE], F32R), sb("w3", [P, KD, D]),
               sb("w2", [P, KD, D]))
        beta_w = sb("beta_w", [P, KD, LH])
        beta_bias = sb("beta_bias", [LH, 1])

        with ExitStack() as first:
            proj_w = sb("proj_w", [P, KD, D], scope=first)
            bias_rows = sb("bias_rows", [P, D], scope=first)
            ctx_tok = sb("ctx_tok", [P, NB, TPB, D], scope=first)
            loads = ((proj_w[:], w_proj), (bias_rows[:], b_proj.to_broadcast([P, D])), (ffn[3][:], w_out),
                     (ffn[2][:], w_mid), (beta_w[:], w_beta), (beta_bias[:], b_beta))
            softmax_attention(nc, semaphore, x, w_qkv, loads, bias_rows, x_tok, xn_hi, xn_lo, ident, ctx_tok)
            project_context(nc, semaphore, proj_w, ctx_tok, ident, x_tok)

        with ExitStack() as second:
            head_weights = (sb("head_raw", [P, KD, 4, 2 * DK], scope=second),
                            sb("head_hi", [P, KD, 4, 2 * DK], F32R, second),
                            sb("head_lo", [P, KD, 4, 2 * DK], F32R, second))
            wo = sb("wo_hi", [P, LH, D], F32R, second), sb("wo_lo", [P, LH, D], F32R, second)
            k_norm = sb("k_norm", [P, 2, DK], scope=second)
            par = sb("par", [P, LH, 2 * (TAPS + 1)], scope=second)
            norm = sb("norm", [P, 4], scope=second)
            beta_tok = sb("beta_tok", [P, NT, LH], scope=second)
            with nc.sbuf_tensor("wo_raw", [P, LH, D], F32) as wo_raw:
                ahead = first_head_weights(semaphore, *head_weights, *wo, wo_raw, w_heads,
                                           ((par[:], params), (norm[:], norms),
                                            (k_norm[:], k_norms.to_broadcast([P, 2, DK])), (wo_raw[:], w_o)))
                norm_and_ffn(nc, semaphore, "b", ffn, xn_hi, xn_lo, ident, x_tok, w_in, ahead)
            nc.clear_and_free_semaphores(held)
            nc.all_engine_barrier()
            held.clear()
            norm_and_decay(nc, semaphore, beta_w, beta_bias, xn_hi, xn_lo, ident, x_tok, beta_tok, keep_rows)
            linear_attention(nc, semaphore, head_weights, w_heads, wo, par, norm, k_norm, xn_hi, xn_lo, ident, beta_tok,
                             keep_rows, x_tok)
        norm_and_ffn(nc, semaphore, "d", ffn, xn_hi, xn_lo, ident, x_tok, out=out)


def kernel(**inputs):
    import numpy as np
    import concourse.bacc as bacc
    from concourse.bass_utils import run_bass_kernel_spmd

    def by_channel(a):
        return np.ascontiguousarray(a.reshape(-1, P, a.shape[-1]).transpose(1, 0, 2))

    a = {k: np.asarray(v) for k, v in inputs.items()}
    qkv = a["L0_attn_a_Wqkv"].reshape(NH // 4, 4, 3, HN, D)
    q, k = (qkv[:, :, i].transpose(0, 2, 1, 3).reshape(D, D) for i in range(2))
    v = qkv[:, :, 2].reshape(D, D)
    heads = np.stack([a[f"L0_attn_b_W{n}"].reshape(KD, P, LH // 2, 2 * DK) for n in "qkgv"], axis=3)
    taps = [a[f"L0_attn_b_{n}conv_w"].reshape(LH, DK, TAPS) for n in "qk"]
    biases = [a[f"L0_attn_b_{n}conv_b"].reshape(LH, DK, 1) for n in "qk"]
    arrays = {
        "x": a["L0_attn_a_query"],
        "w_qkv": by_channel(np.concatenate([q, k, v]).T),
        "w_proj": by_channel(a["L0_attn_a_Wproj"].T),
        "b_proj": a["L0_attn_a_bproj"][None],
        "w_in": by_channel(np.concatenate([a["L0_ffn_w1"], a["L0_ffn_wr"]]).T),
        "w_mid": by_channel(a["L0_ffn_w3"].T),
        "w_out": by_channel(a["L0_ffn_w2"].T),
        "w_beta": by_channel(a["L0_attn_b_Wb"]),
        "b_beta": a["L0_attn_b_bb"][:, None],
        "w_heads": heads.transpose(2, 1, 0, 3, 4),
        "w_o": by_channel(a["L0_attn_b_Wo"]),
        "params": np.concatenate(taps + biases, axis=-1).transpose(1, 0, 2),
        "norms": np.stack([a[f"L0_attn_b_{n}"] for n in ("qn_w", "qn_b", "kn_w", "kn_b")], axis=1),
    }
    arrays["k_norms"] = np.stack([a["L0_attn_b_kn_w"], a["L0_attn_b_kn_b"]])[None]
    arrays = {n: np.ascontiguousarray(v) for n, v in arrays.items()}
    nc = bacc.Bacc("TRN2", target_bir_lowering=False, num_devices=1)
    args = {n: nc.dram_tensor(n, v.shape, mybir.dt.from_np(v.dtype), kind="ExternalInput").ap()
            for n, v in arrays.items()}
    out = nc.dram_tensor("out", (NB, SEQ, D), F32, kind="ExternalOutput").ap()
    build(nc, out=out, **args)
    return run_bass_kernel_spmd(nc, [arrays], core_ids=[0]).results[0]["out"]
```
